# Optimizing a Trainium2 kernel written in Bass

```python
import numpy as np
import jax
import jax.numpy as jnp

def _softmax(x, axis=-1):
    return jax.nn.softmax(x, axis=axis)

def _gelu(x):
    return jax.nn.gelu(x, approximate=True)

def _silu(x):
    return jax.nn.silu(x)

def _sigmoid(x):
    return jax.nn.sigmoid(x)

def _layernorm(x, axis=-1, eps=1e-05):
    m = jnp.mean(x, axis=axis, keepdims=True)
    v = jnp.var(x, axis=axis, keepdims=True)
    return (x - m) / jnp.sqrt(v + eps)

def _scatter_add(tgt, idx, src, axis=0):
    return tgt.at[idx].add(src)

def _segment_sum(src, seg, n):
    return jax.ops.segment_sum(src, seg, n)
kernel_name = 'mk_gnn_preln_d4_gnn_r64_c83930'

def setup_inputs(seed: int=0):
    np.random.seed(seed)
    _w = jnp.asarray

    def _rec_inputs():
        import jax
        import jax.numpy as jnp
        _gk = jax.random.key(seed)
        x = -0.0003713 + 1 * jax.random.normal(jax.random.fold_in(_gk, 1), (100000, 128), jnp.float32)
        src = jax.random.randint(jax.random.fold_in(_gk, 2), (25000,), 0, 100000, jnp.int32)
        dst = jax.random.randint(jax.random.fold_in(_gk, 3), (25000,), 0, 100000, jnp.int32)
        _o = jnp.argsort(dst, stable=True)
        src = src[_o]
        dst = dst[_o]
        edge_weight = 0.00107675 + 0.999702 * jax.random.normal(jax.random.fold_in(_gk, 13), (25000,), jnp.float32)
        return (x, src, dst, edge_weight)
    x, src, dst, edge_weight = _rec_inputs()

    def _L0_gnn_setup():
        import jax, jax.numpy as jnp
        import numpy as np
        N_NODES = 100000
        BN_EPS = 1e-05
        key = jax.random.key(seed)
        k1, k2, k3, k4, k5 = jax.random.split(key, 5)
        N, E, D = (N_NODES, 25000, 128)
        feature = jax.random.normal(k1, (N, D), dtype=jnp.float32)
        src = jax.random.randint(k2, (E,), 0, N, dtype=jnp.int32)
        dst = jax.random.randint(k3, (E,), 0, N, dtype=jnp.int32)
        W = jax.random.normal(k4, (D, D), dtype=jnp.float32) * (1.0 / np.sqrt(D))
        b = jax.random.normal(k5, (D,), dtype=jnp.float32) * 0.01
        gamma = jnp.ones((D,), dtype=jnp.float32)
        beta = jnp.zeros((D,), dtype=jnp.float32)
        return {'feature': feature, 'src': src, 'dst': dst, 'W': W, 'b': b, 'gamma': gamma, 'beta': beta}
    _L0_gnn_all = _L0_gnn_setup()
    _L0_gnn_in = {k: v for k, v in _L0_gnn_all.items() if k in ('W', 'b', 'gamma', 'beta')}
    del _L0_gnn_all

    def _L1_gnn_setup():
        import jax, jax.numpy as jnp
        import numpy as np
        import math
        N_NODES, N_EDGES, DIM, N_HEADS = (50000, 12500, 128, 8)
        D_K = DIM // N_HEADS
        key = jax.random.key(seed)
        ks = jax.random.split(key, 12)
        f32 = jnp.float32
        s = 1.0 / math.sqrt(DIM)
        return {'x': jax.random.normal(ks[0], (N_NODES, DIM), f32), 'src': jax.random.randint(ks[1], (N_EDGES,), 0, N_NODES), 'dst': jax.random.randint(ks[2], (N_EDGES,), 0, N_NODES), 'edge_weight': jax.random.normal(ks[3], (N_EDGES,), f32), 'Wk': jax.random.normal(ks[4], (DIM, DIM), f32) * s, 'bk': jax.random.normal(ks[5], (DIM,), f32) * 0.01, 'Wq': jax.random.normal(ks[6], (DIM, DIM), f32) * s, 'bq': jax.random.normal(ks[7], (DIM,), f32) * 0.01, 'Wv': jax.random.normal(ks[8], (DIM, DIM), f32) * s, 'bv': jax.random.normal(ks[9], (DIM,), f32) * 0.01, 'rel_att': jax.random.normal(ks[10], (N_HEADS, D_K), f32) * 0.1, 'rel_msg': jax.random.normal(ks[11], (N_HEADS, D_K, D_K), f32) / math.sqrt(D_K)}
    _L1_gnn_all = _L1_gnn_setup()
    _L1_gnn_in = {k: v for k, v in _L1_gnn_all.items() if k in ('Wk', 'bk', 'Wq', 'bq', 'Wv', 'bv', 'rel_att', 'rel_msg')}
    del _L1_gnn_all

    def _L2_gnn_setup():
        import jax, jax.numpy as jnp
        import numpy as np
        N = 100000
        E = 25000
        F = 128
        UNITS = 128
        key = jax.random.key(seed)
        k1, k2, k3, k4 = jax.random.split(key, 4)
        node_states = jax.random.normal(k1, (N, F), dtype=jnp.float32)
        src = jax.random.randint(k2, (E,), 0, N)
        dst = jax.random.randint(k3, (E,), 0, N)
        kernel = jax.random.normal(k4, (F, UNITS), dtype=jnp.float32) / np.float32(np.sqrt(F))
        bias = jnp.zeros((UNITS,), dtype=jnp.float32)
        return {'node_states': node_states, 'src': src, 'dst': dst, 'kernel': kernel, 'bias': bias}
    _L2_gnn_all = _L2_gnn_setup()
    _L2_gnn_in = {k: v for k, v in _L2_gnn_all.items() if k in ('kernel', 'bias')}
    del _L2_gnn_all

    def _L3_gnn_setup():
        import jax, jax.numpy as jnp
        import numpy as np
        GRID_SIZE = 5
        SPLINE_ORDER = 3
        ALPHA = 0.2

        def _make_grid(in_features, dtype=jnp.float32):
            h = 2.0 / GRID_SIZE
            pts = jnp.arange(-SPLINE_ORDER, GRID_SIZE + SPLINE_ORDER + 1, dtype=dtype) * h - 1.0
            return jnp.broadcast_to(pts, (in_features, pts.shape[0]))

        def _b_splines(x, grid):
            x = x[..., None]
            bases = ((x >= grid[:, :-1]) & (x < grid[:, 1:])).astype(x.dtype)
            for k in range(1, SPLINE_ORDER + 1):
                left = (x - grid[:, :-(k + 1)]) / (grid[:, k:-1] - grid[:, :-(k + 1)])
                right = (grid[:, k + 1:] - x) / (grid[:, k + 1:] - grid[:, 1:-k])
                bases = left * bases[..., :-1] + right * bases[..., 1:]
            return bases

        def _kan(x, base_weight, spline_weight):
            N, Fin = x.shape
            Fout = base_weight.shape[0]
            grid = _make_grid(Fin, x.dtype)
            bases = _b_splines(x, grid)
            base_out = jax.nn.silu(x) @ base_weight.T
            spline_out = bases.reshape(N, -1) @ spline_weight.reshape(Fout, -1).T
            return base_out + spline_out
        key = jax.random.key(seed)
        k1, k2, k3, k4, k5, k6 = jax.random.split(key, 6)
        N, E, Fin, Fout = (50000, 12500, 128, 128)
        C = GRID_SIZE + SPLINE_ORDER
        h = jax.random.normal(k1, (N, Fin), dtype=jnp.float32)
        edge_index = jax.random.randint(k2, (2, E), 0, N, dtype=jnp.int64)
        W = jax.random.normal(k3, (Fin, Fout), dtype=jnp.float32) * (1.414 / np.sqrt(Fin))
        a = jax.random.normal(k4, (2 * Fout, 1), dtype=jnp.float32) * 0.1
        base_weight = jax.random.normal(k5, (Fout, Fin), dtype=jnp.float32) / np.sqrt(Fin)
        spline_weight = jax.random.normal(k6, (Fout, Fin, C), dtype=jnp.float32) * 0.1
        return {'h': h, 'edge_index': edge_index, 'W': W, 'a': a, 'base_weight': base_weight, 'spline_weight': spline_weight}
    _L3_gnn_all = _L3_gnn_setup()
    _L3_gnn_in = {k: v for k, v in _L3_gnn_all.items() if k in ('W', 'a', 'base_weight', 'spline_weight')}
    del _L3_gnn_all
    return {'x': x, 'src': src, 'dst': dst, 'edge_weight': edge_weight, 'L0_gnn_W': _L0_gnn_in['W'], 'L0_gnn_b': _L0_gnn_in['b'], 'L0_gnn_gamma': _L0_gnn_in['gamma'], 'L0_gnn_beta': _L0_gnn_in['beta'], 'L1_gnn_Wk': _L1_gnn_in['Wk'], 'L1_gnn_bk': _L1_gnn_in['bk'], 'L1_gnn_Wq': _L1_gnn_in['Wq'], 'L1_gnn_bq': _L1_gnn_in['bq'], 'L1_gnn_Wv': _L1_gnn_in['Wv'], 'L1_gnn_bv': _L1_gnn_in['bv'], 'L1_gnn_rel_att': _L1_gnn_in['rel_att'], 'L1_gnn_rel_msg': _L1_gnn_in['rel_msg'], 'L2_gnn_kernel': _L2_gnn_in['kernel'], 'L2_gnn_bias': _L2_gnn_in['bias'], 'L3_gnn_W': _L3_gnn_in['W'], 'L3_gnn_a': _L3_gnn_in['a'], 'L3_gnn_base_weight': _L3_gnn_in['base_weight'], 'L3_gnn_spline_weight': _L3_gnn_in['spline_weight']}

def reference(x, src, dst, edge_weight, L0_gnn_W, L0_gnn_b, L0_gnn_gamma, L0_gnn_beta, L1_gnn_Wk, L1_gnn_bk, L1_gnn_Wq, L1_gnn_bq, L1_gnn_Wv, L1_gnn_bv, L1_gnn_rel_att, L1_gnn_rel_msg, L2_gnn_kernel, L2_gnn_bias, L3_gnn_W, L3_gnn_a, L3_gnn_base_weight, L3_gnn_spline_weight):
    import jax
    import jax.numpy as jnp

    def _L0_gnn_ref(feature, src, dst, W, b, gamma, beta):
        import jax, jax.numpy as jnp
        import numpy as np
        N_NODES = 100000
        BN_EPS = 1e-05
        h = jax.ops.segment_sum(feature[src], dst, num_segments=N_NODES)
        h = jax.nn.relu(h @ W.T + b)
        mean = jnp.mean(h, axis=0)
        var = jnp.mean(jnp.square(h - mean), axis=0)
        h = (h - mean) * jax.lax.rsqrt(var + BN_EPS) * gamma + beta
        return h

    def _L1_gnn_ref(x, src, dst, edge_weight, Wk, bk, Wq, bq, Wv, bv, rel_att, rel_msg):
        import jax, jax.numpy as jnp
        import numpy as np
        import math
        N_NODES, N_EDGES, DIM, N_HEADS = (50000, 12500, 128, 8)
        D_K = DIM // N_HEADS
        N, D = x.shape
        H, dk = rel_att.shape
        inv_sqrt_dk = jnp.asarray(1.0 / math.sqrt(dk), x.dtype)
        k = (x @ Wk.T + bk).reshape(N, H, dk)
        q = (x @ Wq.T + bq).reshape(N, H, dk)
        v = (x @ Wv.T + bv).reshape(N, H, dk)
        qp = edge_weight[:, None, None] * rel_att[None]
        att = ((q[dst] + qp) * k[src]).sum(-1) * inv_sqrt_dk
        val = jnp.einsum('ehd,hdk->ehk', v[src], rel_msg)
        m = jax.ops.segment_max(att, dst, num_segments=N)
        e = jnp.exp(att - m[dst])
        s = jax.ops.segment_sum(e, dst, num_segments=N)
        w = e / s[dst]
        h = jax.ops.segment_sum(w[..., None] * val, dst, num_segments=N)
        return jax.nn.relu(h.reshape(N, D))

    def _L2_gnn_ref(node_states, src, dst, kernel, bias):
        import jax, jax.numpy as jnp
        import numpy as np
        N = 100000
        E = 25000
        F = 128
        UNITS = 128
        n = node_states.shape[0]
        ones = jnp.ones(src.shape, dtype=node_states.dtype)
        deg = jax.ops.segment_sum(ones, src, num_segments=n)
        dinv = jnp.where(deg > 0, 1.0 / jnp.sqrt(jnp.maximum(deg, 1.0)), 0.0)
        xw = node_states @ kernel
        coef = (dinv[src] * dinv[dst])[:, None]
        msg = xw[dst] * coef
        out = jax.ops.segment_sum(msg, src, num_segments=n)
        out = out + bias
        return jax.nn.relu(out)

    def _L3_gnn_ref(h, edge_index, W, a, base_weight, spline_weight):
        import jax, jax.numpy as jnp
        import numpy as np
        GRID_SIZE = 5
        SPLINE_ORDER = 3
        ALPHA = 0.2

        def _make_grid(in_features, dtype=jnp.float32):
            h = 2.0 / GRID_SIZE
            pts = jnp.arange(-SPLINE_ORDER, GRID_SIZE + SPLINE_ORDER + 1, dtype=dtype) * h - 1.0
            return jnp.broadcast_to(pts, (in_features, pts.shape[0]))

        def _b_splines(x, grid):
            x = x[..., None]
            bases = ((x >= grid[:, :-1]) & (x < grid[:, 1:])).astype(x.dtype)
            for k in range(1, SPLINE_ORDER + 1):
                left = (x - grid[:, :-(k + 1)]) / (grid[:, k:-1] - grid[:, :-(k + 1)])
                right = (grid[:, k + 1:] - x) / (grid[:, k + 1:] - grid[:, 1:-k])
                bases = left * bases[..., :-1] + right * bases[..., 1:]
            return bases

        def _kan(x, base_weight, spline_weight):
            N, Fin = x.shape
            Fout = base_weight.shape[0]
            grid = _make_grid(Fin, x.dtype)
            bases = _b_splines(x, grid)
            base_out = jax.nn.silu(x) @ base_weight.T
            spline_out = bases.reshape(N, -1) @ spline_weight.reshape(Fout, -1).T
            return base_out + spline_out
        N = h.shape[0]
        Fout = W.shape[1]
        HW = h @ W
        HW_KAN = _kan(h, base_weight, spline_weight)
        row, col = (edge_index[0], edge_index[1])
        s_src = HW @ a[:Fout, 0]
        s_dst = HW @ a[Fout:, 0]
        e = jax.nn.leaky_relu(s_src[row] + s_dst[col], ALPHA)
        m = jax.ops.segment_max(e, row, num_segments=N)
        e_exp = jnp.exp(e - m[row])
        denom = jax.ops.segment_sum(e_exp, row, num_segments=N)
        att = e_exp / denom[row]
        out = jax.ops.segment_sum(att[:, None] * HW_KAN[col], row, num_segments=N)
        return out
    edge_index = jnp.stack([src, dst])
    h = jnp.maximum(_layernorm(x, axis=-1), 0.0)
    x = x + _L0_gnn_ref(h, src, dst, L0_gnn_W, L0_gnn_b, L0_gnn_gamma, L0_gnn_beta)
    h = jnp.maximum(_layernorm(x, axis=-1), 0.0)
    x = x + _L1_gnn_ref(h, src, dst, edge_weight, L1_gnn_Wk, L1_gnn_bk, L1_gnn_Wq, L1_gnn_bq, L1_gnn_Wv, L1_gnn_bv, L1_gnn_rel_att, L1_gnn_rel_msg)
    h = jnp.maximum(_layernorm(x, axis=-1), 0.0)
    x = x + _L2_gnn_ref(h, src, dst, L2_gnn_kernel, L2_gnn_bias)
    h = jnp.maximum(_layernorm(x, axis=-1), 0.0)
    x = x + _L3_gnn_ref(h, edge_index, L3_gnn_W, L3_gnn_a, L3_gnn_base_weight, L3_gnn_spline_weight)
    return x

_drawn_inputs = setup_inputs


def setup_inputs(seed=0):
    import zlib

    import numpy as np

    out = dict(_drawn_inputs(seed))
    spreads = {'L0_gnn_gamma': (1.0, 0.2), 'L0_gnn_beta': (0.0, 0.1), 'L2_gnn_bias': (0.0, 0.1)}
    factors = {'edge_weight': 8.0,
     'L0_gnn_b': 3.625,
     'L1_gnn_Wk': 4.456,
     'L1_gnn_bk': 8.0,
     'L1_gnn_Wq': 4.473,
     'L1_gnn_bq': 8.0,
     'L1_gnn_bv': 8.0,
     'L1_gnn_rel_att': 8.0,
     'L3_gnn_W': 5.228,
     'L3_gnn_a': 4.317}
    for name, (base, spread) in spreads.items():
        noise = np.random.default_rng([zlib.crc32(name.encode()), seed]).standard_normal(out[name].shape)
        drawn = base * np.exp(spread * noise) if base else spread * noise
        out[name] = jnp.asarray(drawn.astype(out[name].dtype))
    for name, factor in factors.items():
        out[name] = (out[name] * factor).astype(out[name].dtype)
    return out
```

```python
import concourse.bass as bass
from concourse import mybir
from contextlib import ExitStack

F32 = mybir.dt.float32
I32 = mybir.dt.int32
ALU = mybir.AluOpType
ACT = mybir.ActivationFunctionType
AX = mybir.AxisListType

N = 100000
E = 25000
D = 128
H = 8
DK = D // H
P = 128
T = -(-E // P)
G = 7
NG = T // G
PAIRS = NG // 2
SORT = 32768
SF = SORT // P
ID_BITS = 15
HALF = N // 2
CODE = 15000
PAD_NODE = N + 1
PAD_CODE = PAD_NODE - HALF + CODE
OUT_OF_RANGE = 200000
BIG = 1.0e38
EPS = 1e-5
BY_DST, BY_SRC = 0, 1
SRC, DST, WEIGHT = 0, 1, 2
BULK_ROWS = 11
BULK_MAIN = P * (N // P)
BULK_STEPS = N // P // BULK_ROWS
KNOTS = 6
SPLINES = 8


class Steps:

    def __init__(self, eng, sem):
        self.eng, self.sem, self.base, self.k = eng, sem, 0, 0

    def inc(self, ins):
        ins.then_inc(self.sem, 1)
        self.k += 1

    def wait(self):
        self.eng.wait_ge(self.sem, self.base + self.k)

    def hold(self, passed):
        hold(self.eng, passed, self.sem, self.base + self.k)

    def link(self, ins):
        self.inc(ins)
        self.wait()


def hold(eng, passed, sem, value):
    eng.wait_ge(sem, value)
    if not isinstance(value, int):
        eng.sem_inc(passed, 1)


def turns(eng, body, steps=None, per=0):
    body(0, True)
    before = steps.base + steps.k if steps else 0
    with eng.Fori(1, PAIRS) as i:
        if steps:
            steps.base, steps.k = i * per + (before - per), 0
        body(i, False)
        assert not steps or steps.k == per, (steps.k, per)
    if steps:
        steps.base, steps.k = before + per * (PAIRS - 1), 0


def group(i, slot):
    return bass.ds((i * 2 + slot) * G, G)


def chunk(rows, i, slot):
    return rows[:, group(i, slot), :]


class Memory:

    def __init__(self, nc, ctx):
        def sb(name, shape, dt=F32):
            return ctx.enter_context(nc.sbuf_tensor(name, shape, dt))

        self.nc, self.ctx, self.sb = nc, ctx, sb
        self.words_dram = nc.dram_tensor("sorted_words", (2, SORT + P), I32).ap()
        self.h0_table = nc.dram_tensor("h0_table", (N, D), F32).ap()
        self.h2_table = nc.dram_tensor("h2_table", (N, D), F32).ap()
        self.dinv_table = nc.dram_tensor("dinv_table", (N, 1), F32).ap()
        def edge_rows(name):
            return nc.dram_tensor(name, (P, T, D), F32).ap()

        self.x_src, self.x_dst, self.x1_dst = edge_rows("x_src"), edge_rows("x_dst"), edge_rows("x1_dst")
        self.y_src, self.y_dst, self.x3_src = edge_rows("y_src"), edge_rows("y_dst"), edge_rows("x3_src")
        self.rows = sb("rows", [P, T, D])
        self.ident = sb("ident", [P, P])
        self.ones = sb("ones", [P, P])
        self.epsilon = sb("epsilon", [P, 1])
        self.edge_no = [sb(f"edge_no{o}", [P, T], I32) for o in (0, 1)]
        self.code = [sb(f"code{o}", [P, T + 2]) for o in (0, 1)]
        self.same = [sb(f"same{o}", [P, T + 1]) for o in (0, 1)]
        self.tail = [sb(f"tail{o}", [P, T, 1]) for o in (0, 1)]
        self.first = [sb(f"first{o}", [P, T, 1]) for o in (0, 1)]
        self.last = [sb(f"last{o}", [P, T, 1]) for o in (0, 1)]
        self.before = [sb(f"before{o}", [P, P]) for o in (0, 1)]
        self.after = [sb(f"after{o}", [P, P]) for o in (0, 1)]
        self.src_idx = [sb(f"src_idx{o}", [P, T], I32) for o in (0, 1)]
        self.dst_idx = [sb(f"dst_idx{o}", [P, T], I32) for o in (0, 1)]
        self.tail_idx = [sb(f"tail_idx{o}", [P, T], I32) for o in (0, 1)]
        self.weight = sb("weight", [P, T, 1])
        self.carry = sb("carry", [P, 1, D])
        def spread(name, cols=D):
            return sb(name, [P, 1, cols])

        self.b0, self.rb0, self.scale0, self.shift0 = spread("b0"), spread("rb0"), spread("scale0"), spread("shift0")
        self.b2, self.rb2, self.rel = spread("b2"), spread("rb2"), spread("rel")
        self.to_src, self.to_dst = spread("to_src"), spread("to_dst")
        self.gamma_beta = sb("gamma_beta", [1, 2 * D])
        self.totals = sb("totals", [1, 2 * D])
        self.w0, self.wq, self.w2 = sb("w0", [D, D]), sb("wq", [D, D]), sb("w2", [D, D])
        self.wkv = sb("wkv", [D, 2 * D])
        self.bias_kvq = sb("bias_kvq", [1, 3 * D])
        self.w_kan = sb("w_kan", [D, KNOTS + 1, D])
        self.score3 = sb("score3", [P, T, 1])
        self.total3 = sb("total3", [P, T, 1])
        self.to_self = sb("to_self", [P, T, 1])
        self.dinv_src = sb("dinv_src", [P, T, 1])
        self.dinv_dst = sb("dinv_dst", [P, T, 1])
        self.phase_sems = []
        self.passed = self.lasting_sem("passed")

    def sem(self, name):
        sem = self.nc.alloc_semaphore(name=name)
        self.phase_sems.append(sem)
        return sem

    def lasting_sem(self, name):
        return self.nc.alloc_semaphore(name=name)

    def end_phase(self):
        for sem in self.phase_sems:
            self.nc.sync.sem_clear(sem)
            self.nc.release_semaphore(sem)
        self.phase_sems = []
        self.nc.all_engine_barrier()


def sort_edges(nc, m, src, dst):
    with ExitStack() as ctx:
        def sb(name, shape, dt=F32):
            return ctx.enter_context(nc.sbuf_tensor(name, shape, dt))

        key = sb("sort_key", [P, 2, SF], I32)
        key_f = sb("sort_key_f", [P, 2, SF])
        low = sb("sort_low", [P, 2, SF])
        code = sb("sort_code", [P, 2, SF], I32)
        slot = sb("sort_slot", [P, 2, SF], I32)
        gray = sb("sort_gray", [P, 2, SF], I32)
        flips = sb("sort_flips", [P, 2, SF], I32)
        zero_row = sb("sort_zero", [1, 2], I32)
        words = [sb(f"sort_words{i}", [P, 2 * SF]) for i in (0, 1)]
        turned = [ctx.enter_context(nc.psum_tensor(f"sort_turned{i}", [P, 2 * SF], F32)) for i in (0, 1)]
        s_key_pad, s_keys, s_ident, s_slot = (m.sem(n) for n in ("key_pad", "keys_in", "ident_made", "slot_made"))
        s_step, s_ready, s_turned = m.sem("sort_step"), m.sem("sort_ready"), m.sem("sort_turned_done")
        s_out, s_zero_row = m.sem("words_out"), m.sem("zero_row_made")
        full = E // SF
        rest = E - full * SF
        s_sorted = m.sem("sorted")

        block = ctx.enter_context(nc.Block())

        @block.sync
        def _(sp):
            sp.wait_ge(s_key_pad, 1)
            for o, keys in ((BY_DST, dst), (BY_SRC, src)):
                sp.dma_start(key[0:full, o, :], keys[0:full * SF].rearrange("(p f) -> p f", f=SF)).then_inc(s_keys, 16)
                sp.dma_start(key[full:full + 1, o, 0:rest],
                             keys[full * SF:E].rearrange("(p f) -> p f", p=1)).then_inc(s_keys, 16)

        @block.scalar
        def _(act):
            act.wait_ge(s_zero_row, 1)
            for o in (BY_DST, BY_SRC):
                act.dma_start(m.words_dram[o:o + 1, 0:1], zero_row[0:1, o:o + 1]).then_inc(s_out, 16)
            act.wait_ge(s_sorted, 1)
            for o in (BY_DST, BY_SRC):
                act.dma_start(m.words_dram[o, 1:1 + SORT].rearrange("(p f) -> p f", f=SF),
                              words[0][:, o * SF:(o + 1) * SF].bitcast(I32)).then_inc(s_out, 16)
            act.wait_ge(s_out, 64)

        @block.gpsimd
        def _(pool):
            nc.gpsimd.memset(key[:, :, :], PAD_NODE).then_inc(s_key_pad, 1)
            nc.gpsimd.memset(m.ident[:, :], 0.0).then_inc(s_ident, 1)
            nc.gpsimd.iota(slot[:, :, :], pattern=[[0, 2], [1, SF]], base=0, channel_multiplier=SF).then_inc(s_slot, 1)
            nc.gpsimd.memset(zero_row[:, :], 0).then_inc(s_zero_row, 1)
            pool.wait_ge(s_ident, 1)
            nc.gpsimd.affine_select(out=m.ident[:, :], in_=m.ident[:, :], compare_op=ALU.not_equal, fill=1.0,
                                    base=0, pattern=[[-1, P]], channel_multiplier=1).then_inc(s_ident, 1)

        @block.vector
        def _(dve):
            steps = Steps(dve, s_step)
            dve.wait_ge(s_slot, 1)
            dve.wait_ge(s_keys, 64)
            v = nc.vector
            steps.inc(v.tensor_scalar(gray[:, :, :], slot[:, :, :], 1, None, ALU.logical_shift_right))
            steps.link(v.tensor_copy(key_f[:, :, :], key[:, :, :]))
            steps.inc(v.tensor_tensor(flips[:, :, :], gray[:, :, :], slot[:, :, :], ALU.bitwise_xor))
            steps.link(v.tensor_scalar(low[:, :, :], key_f[:, :, :], float(HALF), float(2 ** 16 + HALF), ALU.is_lt, ALU.mult))
            steps.inc(v.tensor_copy(gray[:, :, :], flips[:, :, :]))
            steps.link(v.scalar_tensor_tensor(code[:, :, :], key_f[:, :, :], float(CODE - HALF), low[:, :, :], ALU.add, ALU.add))
            steps.inc(v.tensor_scalar(key[:, :, :], code[:, :, :], ID_BITS, None, ALU.logical_shift_left))
            steps.link(v.tensor_scalar(flips[:, :, :], slot[:, :, :], 30, -2 ** 31, ALU.logical_shift_left, ALU.bitwise_and))
            flat = [w[:, :].bitcast(I32) for w in words]
            slot2, key2 = (a[:, :, :].rearrange("p o f -> p (o f)") for a in (slot, key))
            flips2, gray2 = (a[:, :, :].rearrange("p o f -> p (o f)") for a in (flips, gray))
            steps.link(v.tensor_tensor(flat[0], key2, slot2, ALU.bitwise_or))
            turns = 0
            at = 0

            def exchange(a, b, distance):
                x, y = (w[:, :].rearrange("p (a two b) -> p a two b", two=2, b=distance) for w in (words[a], words[b]))
                steps.inc(v.tensor_tensor(y[:, :, 0, :], x[:, :, 0, :], x[:, :, 1, :], ALU.min))
                steps.link(v.tensor_tensor(y[:, :, 1, :], x[:, :, 0, :], x[:, :, 1, :], ALU.max))

            def turn(a, b):
                nonlocal turns
                v.nop().then_inc(s_ready, 1)
                turns += 1
                dve.wait_ge(s_turned, turns)
                steps.link(v.tensor_copy(words[b][:, :], turned[0][:, :]))

            for k in range(1, ID_BITS + 1):
                if k > 1:
                    steps.link(v.tensor_scalar(flips2, gray2, 32 - k, -2 ** 31, ALU.logical_shift_left, ALU.bitwise_and))
                steps.link(v.tensor_tensor(flat[1 - at], flat[at], flips2, ALU.bitwise_xor))
                at = 1 - at
                if k > 8:
                    turn(at, 1 - at)
                    at = 1 - at
                    for j in range(k - 1, 7, -1):
                        exchange(at, 1 - at, 2 ** (j - 8))
                        at = 1 - at
                    exchange(at, 1 - at, P)
                    at = 1 - at
                    turn(at, 1 - at)
                    at = 1 - at
                for j in range(min(k - 1, 6 if k > 8 else 7), -1, -1):
                    exchange(at, 1 - at, 2 ** j)
                    at = 1 - at
            if at:
                steps.link(v.tensor_copy(words[0][:, :], words[1][:, :]))
            v.nop().then_inc(s_sorted, 1)

        @block.tensor
        def _(pe):
            pe.wait_ge(s_ident, 2)
            at, turns = 0, 0
            for k in range(1, ID_BITS + 1):
                at = 1 - at
                if k > 8:
                    for exchanges in (k - 7, 0):
                        turns += 1
                        pe.wait_ge(s_ready, turns)
                        for b in range(4):
                            last = nc.tensor.transpose(turned[0][:, b * P:(b + 1) * P], words[at][:, b * P:(b + 1) * P], m.ident[:, :])
                        last.then_inc(s_turned, 1)
                        at = (at + 1 + exchanges) % 2
                at = (at + (7 if k > 8 else k)) % 2


def index_edges(nc, m, records):
    with ExitStack() as ctx:
        def sb(name, shape, dt=F32):
            return ctx.enter_context(nc.sbuf_tensor(name, shape, dt))

        words = [sb(f"words{o}", [P, T + 2], I32) for o in (0, 1)]
        code_i = sb("code_i", [P, T + 2], I32)
        edge_f = sb("edge_f", [P, T])
        not_pad = sb("not_pad", [P, T])
        end_rows = sb("end_rows", [P, P])
        upper = sb("upper", [P, P])
        row_end = ctx.enter_context(nc.psum_tensor("row_end", [P, P], F32))
        before_t = ctx.enter_context(nc.psum_tensor("before_t", [P, P], F32))
        id_stage = sb("id_stage", [P, 2 * G], I32)
        got = [sb(f"record_slot{i}", [P, G, 4], I32) for i in (0, 1)]
        zeros = sb("table_zeros", [P, BULK_ROWS * D])
        s_zero, s_tables = m.sem("zeros_made"), m.sem("tables_zeroed")
        record = [sb(f"record{o}", [P, T, 4], I32) for o in (0, 1)]
        row_f = sb("row_f", [P, T])
        s_words, s_step, s_ids, s_upper = m.sem("words_in"), m.sem("index_step"), m.sem("edge_ids"), m.sem("upper_made")
        s_row, s_rowt, s_bef, s_beft = m.sem("end_rows_ready"), m.sem("end_rows_turned"), m.sem("before_ready"), m.sem("before_turned")
        s_stage = m.sem("id_staged")
        s_got = [m.lasting_sem(f"records_in{i}") for i in (0, 1)]
        s_free = [m.sem(f"record_slot_free{i}") for i in (0, 1)]

        block = ctx.enter_context(nc.Block())

        @block.sync
        def _(sp):
            for o in (BY_DST, BY_SRC):
                w = m.words_dram[o, :]
                src = bass.AP(tensor=w.tensor, offset=w.offset, ap=[[T, P], [1, T + 2]])
                sp.dma_start(words[o][:, :], src).then_inc(s_words, 16)
            sp.wait_ge(s_zero, 1)
            for table in (m.h0_table, m.h2_table):
                whole = table[0:BULK_MAIN, :].rearrange("(p r) d -> p (r d)", p=P)
                with sp.Fori(0, BULK_STEPS) as i:
                    sp.dma_start(whole[:, bass.ds(i * (BULK_ROWS * D), BULK_ROWS * D)], zeros[:, :]).then_inc(s_tables, 16)
                sp.dma_start(table[BULK_MAIN:N, :], zeros[0:N - BULK_MAIN, 0:D]).then_inc(s_tables, 16)
            sp.dma_start(m.dinv_table[0:BULK_MAIN, :].rearrange("(p r) d -> p (r d)", p=P),
                         zeros[:, 0:N // P]).then_inc(s_tables, 16)
            sp.dma_start(m.dinv_table[BULK_MAIN:N, :], zeros[0:N - BULK_MAIN, 0:1]).then_inc(s_tables, 16)
            sp.wait_ge(s_tables, 16 * (2 * BULK_STEPS + 4))

        @block.gpsimd
        def _(pool):
            nc.gpsimd.memset(zeros[:, :], 0.0).then_inc(s_zero, 1)
            nc.gpsimd.memset(upper[:, :], 1.0).then_inc(s_upper, 1)
            pool.wait_ge(s_upper, 1)
            nc.gpsimd.affine_select(out=upper[:, :], in_=upper[:, :], compare_op=ALU.is_gt, fill=0.0,
                                    base=0, pattern=[[1, P]], channel_multiplier=-1).then_inc(s_upper, 1)
            for o in (BY_DST, BY_SRC):
                pool.wait_ge(s_ids, o + 1)
                with pool.Fori(0, PAIRS) as i:
                    for slot in (0, 1):
                        hold(pool, m.passed, s_free[slot], i + (o * PAIRS + 1))
                        g = i * 2 + slot
                        nc.gpsimd.tensor_copy(id_stage[:, slot * G:(slot + 1) * G],
                                              m.edge_no[o][:, bass.ds(g * G, G)]).then_inc(s_stage, 1)
                        hold(pool, m.passed, s_stage, g + (o * NG + 1))
                        for k in range(G):
                            pool.indirect_dma_start(got[slot][:, k, :], None, records,
                                                    bass.IndirectOffsetOnAxis(ap=id_stage[:, slot * G + k:slot * G + k + 1], axis=0)
                                                    ).then_inc(s_got[slot], 16)

        @block.vector
        def _(dve):
            v = nc.vector
            steps = Steps(dve, s_step)
            dve.wait_ge(s_words, 32)
            for o in (BY_DST, BY_SRC):
                code = m.code[o]
                steps.inc(v.tensor_scalar(m.edge_no[o][:, :], words[o][:, 1:T + 1], 2 ** ID_BITS - 1, None, ALU.bitwise_and))
                steps.link(v.tensor_scalar(code_i[:, :], words[o][:, :], ID_BITS, None, ALU.logical_shift_right))
                steps.inc(v.tensor_scalar(edge_f[:, :], m.edge_no[o][:, :], float(E - 1), None, ALU.min))
                steps.link(v.tensor_copy(code[:, :], code_i[:, :]))
                v.tensor_copy(m.edge_no[o][:, :], edge_f[:, :]).then_inc(s_ids, 1)
                dve.wait_ge(s_ids, o + 1)
                steps.inc(v.tensor_tensor(m.same[o][:, :], code[:, 0:T + 1], code[:, 1:T + 2], ALU.is_equal))
                steps.inc(v.tensor_tensor(m.tail[o][:, :, 0], code[:, 1:T + 1], code[:, 2:T + 2], ALU.not_equal))
                steps.inc(v.tensor_scalar(not_pad[:, :], code[:, 1:T + 1], float(PAD_CODE), None, ALU.not_equal))
                steps.inc(v.tensor_scalar(m.first[o][:, :, 0], code[:, 1:T + 1], code[:, 1:2], None, ALU.is_equal))
                steps.inc(v.tensor_scalar(m.last[o][:, :, 0], code[:, 1:T + 1], code[:, T:T + 1], None, ALU.is_equal))
                steps.inc(v.tensor_scalar(end_rows[:, :], m.ident[:, :], 0.0, code[:, 1:2], ALU.mult, ALU.add))
                steps.wait()
                v.tensor_tensor(m.tail[o][:, :, 0], m.tail[o][:, :, 0], not_pad[:, :], ALU.mult).then_inc(s_row, 1)
                dve.wait_ge(s_rowt, o + 1)
                if o == 0:
                    dve.wait_ge(s_upper, 2)
                steps.link(v.tensor_scalar(m.before[o][:, :], row_end[:, :], code[:, T:T + 1], None, ALU.is_equal))
                v.tensor_tensor(m.before[o][:, :], m.before[o][:, :], upper[:, :], ALU.mult).then_inc(s_bef, 1)
                dve.wait_ge(s_beft, o + 1)
                steps.link(v.tensor_copy(m.after[o][:, :], before_t[:, :]))
            for slot in (0, 1):
                steps.link(v.tensor_copy(got[slot][:, 0, 0:1], m.edge_no[0][:, 0:1]))
                v.nop().then_inc(s_free[slot], 1)
            at = steps.k
            for o in (BY_DST, BY_SRC):
                with dve.Fori(0, PAIRS) as i:
                    for slot in (0, 1):
                        dve.wait_ge(s_got[slot], i * (16 * G) + 16 * G * (o * PAIRS + 1))
                        v.tensor_copy(record[o][:, bass.ds((i * 2 + slot) * G, G), :], got[slot][:, :, :]).then_inc(s_free[slot], 1)
            dve.wait_ge(s_free[0], 1 + 2 * PAIRS)
            dve.wait_ge(s_free[1], 1 + 2 * PAIRS)
            for o in (BY_DST, BY_SRC):
                steps.inc(v.tensor_copy(m.src_idx[o][:, :], record[o][:, :, SRC]))
                if o == BY_DST:
                    steps.inc(v.tensor_copy(m.weight[:, :, 0], record[o][:, :, WEIGHT].bitcast(F32)))
                steps.inc(v.tensor_copy(m.dst_idx[o][:, :], record[o][:, :, DST]))
                steps.inc(v.tensor_scalar(row_f[:, :], m.tail[o][:, :, 0], float(-OUT_OF_RANGE), float(OUT_OF_RANGE), ALU.mult, ALU.add))
                steps.wait()
                steps.link(v.tensor_tensor(m.tail_idx[o][:, :], row_f[:, :], record[o][:, :, DST if o == BY_DST else SRC], ALU.add))

        @block.tensor
        def _(pe):
            for o in (BY_DST, BY_SRC):
                pe.wait_ge(s_row, o + 1)
                nc.tensor.transpose(row_end[:, :], end_rows[:, :], m.ident[:, :]).then_inc(s_rowt, 1)
                pe.wait_ge(s_bef, o + 1)
                nc.tensor.transpose(before_t[:, :], m.before[o][:, :], m.ident[:, :]).then_inc(s_beft, 1)


def load_weights(nc, m, w):
    with ExitStack() as ctx:
        def sb(name, shape, dt=F32):
            return ctx.enter_context(nc.sbuf_tensor(name, shape, dt))

        wv, mix, bv = sb("wv", [D, D]), sb("mix", [D, D]), sb("bv", [D, 1])
        w3t, a_src, a_dst = sb("w3t", [D, D]), sb("a_src", [D, 1]), sb("a_dst", [D, 1])
        a_wide = sb("a_wide", [D, 2, P])
        spline = sb("spline", [D, SPLINES, D])
        scaled = [sb(f"scaled{i}", [D, D]) for i in (0, 1)]
        prod = ctx.enter_context(nc.psum_tensor("weight_products", [P, 4 * D], F32))
        s_zero, s_in, s_step, s_ones, s_wide, s_prod, s_mix = (
            m.sem(n) for n in ("mix_zero", "weights_in", "weight_step", "ones_made", "a_wide_made", "products", "mix_in"))
        block = ctx.enter_context(nc.Block())
        rows = [(m.b0, w["b0"]), (m.b2, w["b2"]), (m.rel, w["rel"])]
        whole = [(m.w0, w["w0"]), (m.wq, w["wq"]), (m.w2, w["w2"]), (wv, w["wv"]), (w3t, w["w3t"])]
        n_in = len(rows) + len(whole) + 10

        @block.sync
        def _(sp):
            for out, row in rows:
                sp.dma_start(out[:, 0, :], row.partition_broadcast(P)).then_inc(s_in, 16)
            for out, mat in whole:
                sp.dma_start(out[:, :], mat).then_inc(s_in, 16)
            sp.dma_start(m.wkv[:, 0:D], w["wk"]).then_inc(s_in, 16)
            sp.dma_start(m.bias_kvq[0:1, 0:D], w["bk"].rearrange("(a d) -> a d", a=1)).then_inc(s_in, 16)
            sp.dma_start(m.bias_kvq[0:1, 2 * D:3 * D], w["bq"].rearrange("(a d) -> a d", a=1)).then_inc(s_in, 16)
            sp.dma_start(bv[:, :], w["bv"].rearrange("(d a) -> d a", a=1)).then_inc(s_in, 16)
            sp.dma_start(a_src[:, :], w["a"][0:D, :]).then_inc(s_in, 16)
            sp.dma_start(a_dst[:, :], w["a"][D:2 * D, :]).then_inc(s_in, 16)
            sp.dma_start(m.w_kan[:, 0, :], w["base"]).then_inc(s_in, 16)
            sp.dma_start(spline[:, :, :], w["spline"].rearrange("c i o -> i c o")).then_inc(s_in, 16)
            sp.dma_start(m.gamma_beta[0:1, 0:D], w["gamma"].rearrange("(a d) -> a d", a=1)).then_inc(s_in, 16)
            sp.dma_start(m.gamma_beta[0:1, D:2 * D], w["beta"].rearrange("(a d) -> a d", a=1)).then_inc(s_in, 16)
            sp.wait_ge(s_zero, 1)
            for h in range(H):
                sp.dma_start(mix[h * DK:(h + 1) * DK, h * DK:(h + 1) * DK], w["rel_msg"][h, :, :]).then_inc(s_mix, 16)
            sp.wait_ge(s_mix, 16 * H)

        @block.gpsimd
        def _(pool):
            nc.gpsimd.memset(mix[:, :], 0.0).then_inc(s_zero, 1)
            nc.gpsimd.memset(m.ones[:, :], 1.0).then_inc(s_ones, 1)
            nc.gpsimd.memset(m.epsilon[:, :], EPS).then_inc(s_ones, 1)

        @block.tensor
        def _(pe):
            pe.wait_ge(s_in, 16 * n_in)
            pe.wait_ge(s_mix, 16 * H)
            pe.wait_ge(s_wide, 2)
            nc.tensor.matmul(prod[:, 0:D], wv[:, :], mix[:, :], start=True, stop=True)
            nc.tensor.matmul(prod[0:1, D:2 * D], bv[:, 0:1], mix[:, :], start=True, stop=True)
            nc.tensor.matmul(prod[:, 2 * D:3 * D], a_wide[:, 0, :], w3t[:, :], start=True, stop=True)
            nc.tensor.matmul(prod[:, 3 * D:4 * D], a_wide[:, 1, :], w3t[:, :], start=True, stop=True).then_inc(s_prod, 1)

        @block.vector
        def _(dve):
            v = nc.vector
            steps = Steps(dve, s_step)
            dve.wait_ge(s_in, 16 * n_in)
            dve.wait_ge(s_ones, 2)
            v.tensor_scalar(a_wide[:, 0, :], m.ones[:, :], a_src[:, 0:1], None, ALU.mult).then_inc(s_wide, 1)
            v.tensor_scalar(a_wide[:, 1, :], m.ones[:, :], a_dst[:, 0:1], None, ALU.mult).then_inc(s_wide, 1)
            steps.inc(v.tensor_scalar(m.rb0[:, :, :], m.b0[:, :, :], 0.0, None, ALU.max))
            steps.inc(v.tensor_scalar(m.rb2[:, :, :], m.b2[:, :, :], 0.0, None, ALU.max))
            choose = (1, -4, 6, -4, 1)
            for n in range(KNOTS):
                knot = n + 6
                terms = [(j, choose[knot - j] / 6.0) for j in range(max(0, knot - 4), min(SPLINES, knot + 1))]
                for at, (j, c) in enumerate(terms):
                    if at == 0:
                        steps.link(v.tensor_scalar(m.w_kan[:, 1 + n, :], spline[:, j, :], c, None, ALU.mult))
                    else:
                        steps.link(v.scalar_tensor_tensor(m.w_kan[:, 1 + n, :], spline[:, j, :], c, m.w_kan[:, 1 + n, :],
                                                          ALU.mult, ALU.add))
            dve.wait_ge(s_prod, 1)
            steps.inc(v.tensor_copy(m.wkv[:, D:2 * D], prod[:, 0:D]))
            steps.inc(v.tensor_copy(m.bias_kvq[0:1, D:2 * D], prod[0:1, D:2 * D]))
            steps.inc(v.tensor_copy(m.to_src[:, 0, :], prod[:, 2 * D:3 * D]))
            steps.inc(v.tensor_copy(m.to_dst[:, 0, :], prod[:, 3 * D:4 * D]))
            steps.wait()


def stage_columns(pool, nc, m, stage, idx, i, slot, s_stage, count):
    nc.gpsimd.tensor_copy(stage[slot][:, :], idx[:, group(i, slot)]).then_inc(s_stage, 1)
    hold(pool, m.passed, s_stage, count)


def gather(pool, out, table, stage, sem):
    for k in range(G):
        pool.indirect_dma_start(out[:, k, :], None, table,
                                bass.IndirectOffsetOnAxis(ap=stage[:, k:k + 1], axis=0)).then_inc(sem, 16)


def scatter(pool, table, rows, stage, sem):
    for k in range(G):
        pool.indirect_dma_start(table, bass.IndirectOffsetOnAxis(ap=stage[:, k:k + 1], axis=0), rows[:, k, :], None,
                                bounds_check=N - 1, oob_is_err=False).then_inc(sem, 16)


def row_stats(v, m, steps, rows, n, stats, mean_var):
    for k in range(n):
        steps.inc(v.bn_stats(stats[:, k, :], rows[:, k, :]))
    steps.hold(m.passed)
    for k in range(n - 1):
        steps.inc(v.bn_aggr(mean_var[:, k, :], stats[:, k, :]))
    return v.bn_aggr(mean_var[:, n - 1, :], stats[:, n - 1, :])


def sum_source_rows(nc, m, x):
    with ExitStack() as ctx:
        def sb(name, shape, dt=F32):
            return ctx.enter_context(nc.sbuf_tensor(name, shape, dt))

        o = BY_DST
        stage = [sb(f"l0_stage{i}", [P, G], I32) for i in (0, 1)]
        got = [sb(f"l0_got{i}", [P, G, D]) for i in (0, 1)]
        h = [sb(f"l0_h{i}", [P, G, D]) for i in (0, 1)]
        same_g = [sb(f"l0_same{i}", [P, G]) for i in (0, 1)]
        stats, mv, rstd, shift = sb("l0_stats", [P, G, 6]), [sb(f"l0_mv{i}", [P, G, 2]) for i in (0, 1)], \
            [sb(f"l0_rstd{i}", [P, G, 1]) for i in (0, 1)], [sb(f"l0_shift{i}", [P, G, 1]) for i in (0, 1)]
        std = [sb(f"l0_std{i}", [P, G, 1]) for i in (0, 1)]
        s_stage, s_step, s_var, s_std, s_norm, s_h, s_sum, s_kept = (
            m.sem("l0_" + n) for n in ("staged", "step", "variance", "std", "norm", "h", "summed", "kept"))
        s_got = [m.lasting_sem(f"l0_rows_in{i}") for i in (0, 1)]
        s_stored = [m.sem(f"l0_rows_stored{i}") for i in (0, 1)]
        block = ctx.enter_context(nc.Block())

        @block.gpsimd
        def _(pool):
            def body(i, first):
                for slot in (0, 1):
                    g = i * 2 + slot
                    if not first:
                        hold(pool, m.passed, s_h, g - 1)
                        hold(pool, m.passed, s_stored[slot], i * 16)
                    stage_columns(pool, nc, m, stage, m.src_idx[o], i, slot, s_stage, g + 1)
                    gather(pool, got[slot], x, stage[slot], s_got[slot])
            turns(pool, body)

        @block.sync
        def _(sp):
            with sp.Fori(0, PAIRS) as i:
                for slot in (0, 1):
                    sp.wait_ge(s_got[slot], i * (16 * G) + 16 * G)
                    sp.dma_start(chunk(m.x_src, i, slot), got[slot][:, :, :]).then_inc(s_stored[slot], 16)
            for slot in (0, 1):
                sp.wait_ge(s_stored[slot], 16 * PAIRS)

        @block.scalar
        def _(act):
            def body(i, first):
                for slot in (0, 1):
                    g = i * 2 + slot
                    act.wait_ge(s_var, g + 1)
                    nc.scalar.activation(std[slot][:, :, :], mv[slot][:, :, 1:2], ACT.Sqrt, bias=m.epsilon[:, 0:1]).then_inc(s_std, 1)
                    act.wait_ge(s_norm, g + 1)
                    if not first:
                        act.wait_ge(s_kept, g - 1)
                    for k in range(G):
                        ins = nc.scalar.activation(h[slot][:, k, :], got[slot][:, k, :], ACT.Relu,
                                                   bias=shift[slot][:, k, :], scale=rstd[slot][:, k, :])
                    ins.then_inc(s_h, 1)
                    act.wait_ge(s_sum, g + 1)
                    nc.scalar.copy(m.rows[:, group(i, slot), :], h[slot][:, :, :]).then_inc(s_kept, 1)
            turns(act, body)

        @block.vector
        def _(dve):
            v = nc.vector
            steps = Steps(dve, s_step)

            def body(i, first):
                for slot in (0, 1):
                    g = i * 2 + slot
                    dve.wait_ge(s_got[slot], i * (16 * G) + 16 * G)
                    row_stats(v, m, steps, got[slot], G, stats, mv[slot]).then_inc(s_var, 1)
                    steps.inc(v.tensor_copy(same_g[slot][:, :], m.same[o][:, group(i, slot)]))
                    dve.wait_ge(s_std, g + 1)
                    steps.link(v.reciprocal(rstd[slot][:, :, :], std[slot][:, :, :]))
                    v.scalar_tensor_tensor(shift[slot][:, :, :], mv[slot][:, :, 0:1], -1.0, rstd[slot][:, :, :],
                                           ALU.mult, ALU.mult).then_inc(s_norm, 1)
                    dve.wait_ge(s_h, g + 1)
                    for k in range(G):
                        if first and slot == 0 and k == 0:
                            continue
                        before = h[slot][:, k - 1, :] if k else h[1 - slot][:, G - 1, :]
                        ins = v.scalar_tensor_tensor(h[slot][:, k, :], before, same_g[slot][:, k:k + 1], h[slot][:, k, :],
                                                     ALU.mult, ALU.add)
                        if k < G - 1:
                            steps.link(ins)
                        else:
                            ins.then_inc(s_sum, 1)
                            dve.wait_ge(s_sum, g + 1)
            turns(dve, body, steps, 2 * 3 * G)


def transform_sums0(nc, m, x):
    with ExitStack() as ctx:
        def sb(nm, shape, dt=F32):
            return ctx.enter_context(nc.sbuf_tensor("t0_" + nm, shape, dt))

        def two(nm, shape, dt=F32):
            return [sb(f"{nm}{i}", shape, dt) for i in (0, 1)]

        def psum(nm, cols):
            return ctx.enter_context(nc.psum_tensor("t0_" + nm, [P, cols], F32))

        def sem(nm):
            return m.sem("t0_" + nm)

        o = BY_DST
        numbers, dst_numbers = two("numbers", [P, G], I32), two("dst_numbers", [P, G], I32)
        u, d, sq, xd, uts = two("u", [P, G, D]), two("d", [P, G, D]), two("sq", [P, G, D]), two("xd", [P, G, D]), two("uts", [P, G * D])
        tmp, zero_row, totals = sb("tmp", [P, G, D]), sb("zero_row", [1, 2 * D]), m.totals
        ut, z, carry_ps, sums_ps = [psum(f"ut{i}", 8 * D) for i in (0, 1)], psum("z", 8 * D), psum("carry", 512), psum("sums", 512)
        s_numbers, s_dst_numbers, s_step, s_carry, s_u, s_turned, s_uts, s_z, s_d, s_kept, s_square, s_sums, s_zero_row = (
            sem(n) for n in ("numbers_staged", "dst_numbers_staged", "step", "carry_made", "u_made", "u_turned", "uts_made",
                             "z_made", "d_made", "d_kept", "squared", "summed", "zero_row_made"))
        s_scat = [m.lasting_sem(f"t0_scattered{i}") for i in (0, 1)]
        s_xd, s_stored = [m.lasting_sem(f"t0_xd_in{i}") for i in (0, 1)], [sem(f"xd_stored{i}") for i in (0, 1)]
        block = ctx.enter_context(nc.Block())

        @block.gpsimd
        def _(pool):
            def body(i, first):
                for slot in (0, 1):
                    g = i * 2 + slot
                    if not first:
                        hold(pool, m.passed, s_stored[slot], i * 16)
                    stage_columns(pool, nc, m, dst_numbers, m.dst_idx[o], i, slot, s_dst_numbers, g + 1)
                    gather(pool, xd[slot], x, dst_numbers[slot], s_xd[slot])
                    if not first:
                        hold(pool, m.passed, s_scat[slot], i * (16 * G))
                    stage_columns(pool, nc, m, numbers, m.tail_idx[o], i, slot, s_numbers, g + 1)
                    hold(pool, m.passed, s_d, g + 1)
                    scatter(pool, m.h0_table, d[slot], numbers[slot], s_scat[slot])
            turns(pool, body)
            for slot in (0, 1):
                pool.wait_ge(s_scat[slot], 16 * G * PAIRS)

        @block.sync
        def _(sp):
            with sp.Fori(0, PAIRS) as i:
                for slot in (0, 1):
                    sp.wait_ge(s_xd[slot], i * (16 * G) + 16 * G)
                    sp.dma_start(chunk(m.x_dst, i, slot), xd[slot][:, :, :]).then_inc(s_stored[slot], 16)
            for slot in (0, 1):
                sp.wait_ge(s_stored[slot], 16 * PAIRS)

        @block.tensor
        def _(pe):
            nc.tensor.matmul(carry_ps[:, 0:D], m.before[o][:, :], m.rows[:, T - 1, :], start=True, stop=True).then_inc(s_carry, 1)
            pe.wait_ge(s_zero_row, 1)
            nc.tensor.matmul(sums_ps[0:1, 0:2 * D], m.ones[0:1, 0:1], zero_row[0:1, :], start=True, stop=False)

            def body(i, first):
                for slot in (0, 1):
                    g = i * 2 + slot
                    pe.wait_ge(s_u, g + 1)
                    for k in range(G):
                        ins = nc.tensor.transpose(ut[slot][:, k * D:(k + 1) * D], u[slot][:, k, :], m.ident[:, :])
                    ins.then_inc(s_turned, 1)
                    pe.wait_ge(s_uts, g + 1)
                    if not (first and slot == 0):
                        pe.wait_ge(s_d, g)
                    for k in range(G):
                        ins = nc.tensor.matmul(z[:, k * D:(k + 1) * D], uts[slot][:, k * D:(k + 1) * D], m.w0[:, :],
                                               start=True, stop=True)
                    ins.then_inc(s_z, 1)
                    pe.wait_ge(s_square, g + 1)
                    for k in range(G):
                        nc.tensor.matmul(sums_ps[0:1, 0:D], m.ones[:, 0:1], d[slot][:, k, :], start=False, stop=False)
                        ins = nc.tensor.matmul(sums_ps[0:1, D:2 * D], m.ones[:, 0:1], sq[slot][:, k, :], start=False, stop=False)
                    ins.then_inc(s_sums, 1)
            turns(pe, body)
            nc.tensor.matmul(sums_ps[0:1, 0:2 * D], m.ones[0:1, 0:1], zero_row[0:1, :], start=False, stop=True).then_inc(s_sums, 1)

        @block.scalar
        def _(act):
            def body(i, first):
                for slot in (0, 1):
                    g = i * 2 + slot
                    act.wait_ge(s_turned, g + 1)
                    nc.scalar.activation(uts[slot][:, :], ut[slot][:, 0:G * D], ACT.Copy).then_inc(s_uts, 1)
                    act.wait_ge(s_d, g + 1)
                    if not first:
                        act.wait_ge(s_sums, g - 1)
                    nc.scalar.activation(sq[slot][:, :, :], d[slot][:, :, :], ACT.Square).then_inc(s_square, 1)
                    nc.scalar.activation(m.rows[:, group(i, slot), :], d[slot][:, :, :], ACT.Copy).then_inc(s_kept, 1)
            turns(act, body)

        @block.vector
        def _(dve):
            v = nc.vector
            steps = Steps(dve, s_step)
            v.memset(zero_row[:, :], 0.0).then_inc(s_zero_row, 1)
            dve.wait_ge(s_carry, 1)
            steps.link(v.tensor_copy(m.carry[:, 0, :], carry_ps[:, 0:D]))

            def body(i, first):
                for slot in (0, 1):
                    g = i * 2 + slot
                    steps.link(v.tensor_tensor(tmp[:, :, :], m.carry[:, :, :].to_broadcast([P, G, D]),
                                               m.first[o][:, group(i, slot), :].to_broadcast([P, G, D]), ALU.mult))
                    v.tensor_tensor(u[slot][:, :, :], tmp[:, :, :], m.rows[:, group(i, slot), :], ALU.add).then_inc(s_u, 1)
                    dve.wait_ge(s_u, g + 1)
                    dve.wait_ge(s_z, g + 1)
                    z3 = z[:, 0:G * D].rearrange("p (g d) -> p g d", d=D)
                    steps.link(v.tensor_tensor(tmp[:, :, :], z3, m.b0[:, :, :].to_broadcast([P, G, D]), ALU.add))
                    steps.link(v.scalar_tensor_tensor(tmp[:, :, :], tmp[:, :, :], 0.0, m.rb0[:, :, :].to_broadcast([P, G, D]),
                                                      ALU.max, ALU.subtract))
                    if not first:
                        dve.wait_ge(s_scat[slot], i * (16 * G))
                        dve.wait_ge(s_sums, g - 1)
                        dve.wait_ge(s_kept, g - 1)
                    v.tensor_tensor(d[slot][:, :, :], tmp[:, :, :], m.tail[o][:, group(i, slot), :].to_broadcast([P, G, D]),
                                    ALU.mult).then_inc(s_d, 1)
                    dve.wait_ge(s_d, g + 1)
            turns(dve, body, steps, 2 * 3)
            dve.wait_ge(s_sums, NG + 1)
            steps.link(v.tensor_scalar(m.totals[0:1, 0:2 * D], sums_ps[0:1, 0:2 * D], 1.0 / N, None, ALU.mult))


def batch_norm_rows(nc, m):
    with ExitStack() as ctx:
        work = [ctx.enter_context(nc.sbuf_tensor(f"bn_work{i}", [1, D], F32)) for i in range(4)]
        both = ctx.enter_context(nc.sbuf_tensor("bn_both", [1, 2 * D], F32))
        wide = ctx.enter_context(nc.psum_tensor("bn_wide", [P, 2 * D], F32))
        s_step, s_var, s_std, s_both, s_wide = (m.sem("bn_" + n) for n in ("step", "var", "std", "both", "wide"))
        mean, square = m.totals[0:1, 0:D], m.totals[0:1, D:2 * D]
        block = ctx.enter_context(nc.Block())

        @block.vector
        def _(dve):
            v = nc.vector
            steps = Steps(dve, s_step)
            steps.link(v.tensor_tensor(work[0][:, :], mean, mean, ALU.mult))
            steps.link(v.tensor_tensor(work[1][:, :], square, work[0][:, :], ALU.subtract))
            v.tensor_scalar(work[1][:, :], work[1][:, :], 0.0, None, ALU.max).then_inc(s_var, 1)
            dve.wait_ge(s_std, 1)
            steps.link(v.reciprocal(work[3][:, :], work[2][:, :]))
            steps.link(v.tensor_tensor(both[:, 0:D], work[3][:, :], m.gamma_beta[0:1, 0:D], ALU.mult))
            steps.link(v.tensor_tensor(work[0][:, :], both[:, 0:D], mean, ALU.mult))
            v.tensor_tensor(both[:, D:2 * D], m.gamma_beta[0:1, D:2 * D], work[0][:, :], ALU.subtract).then_inc(s_both, 1)
            dve.wait_ge(s_wide, 1)
            steps.inc(v.tensor_copy(m.scale0[:, 0, :], wide[:, 0:D]))
            steps.inc(v.tensor_copy(m.shift0[:, 0, :], wide[:, D:2 * D]))
            steps.wait()

        @block.scalar
        def _(act):
            act.wait_ge(s_var, 1)
            nc.scalar.activation(work[2][:, :], work[1][:, :], ACT.Sqrt, bias=m.epsilon[0:1, 0:1]).then_inc(s_std, 1)

        @block.tensor
        def _(pe):
            pe.wait_ge(s_both, 1)
            nc.tensor.matmul(wide[:, :], m.ones[0:1, 0:P], both[0:1, :], start=True, stop=True).then_inc(s_wide, 1)


def dense_pass(nc, m, x, out):
    with ExitStack() as ctx:
        def sb(nm, shape, dt=F32):
            return ctx.enter_context(nc.sbuf_tensor("dense_" + nm, shape, dt))

        def sem(nm):
            return m.sem("dense_" + nm)

        C = BULK_ROWS * D
        xin, xout = [sb(f"in{i}", [P, BULK_ROWS, D]) for i in (0, 1)], [sb(f"out{i}", [P, BULK_ROWS, D]) for i in (0, 1)]
        rest_in, rest_out = sb("rest_in", [N - BULK_MAIN, D]), sb("rest_out", [N - BULK_MAIN, D])
        base = sb("base", [P, 1, D])
        tmp = sb("tmp", [P, G, D])
        numbers = [sb(f"numbers{i}", [P, G], I32) for i in (0, 1)]
        value = [sb(f"value{i}", [P, G]) for i in (0, 1)]
        ones_row, count, std = sb("ones_row", [P, T]), sb("count", [P, T]), sb("std", [P, T])
        carry_ps = ctx.enter_context(nc.psum_tensor("dense_carry", [P, 512], F32))
        count_ps = ctx.enter_context(nc.psum_tensor("dense_count_carry", [P, 512], F32))
        s_in, s_out = [sem(f"rows_in{i}") for i in (0, 1)], [sem(f"rows_out{i}") for i in (0, 1)]
        s_sum, s_step, s_rest, s_rest_in, s_rest_out, s_spread, s_carry, s_count, s_carried, s_deg, s_std, s_dinv = (
            sem(n) for n in ("summed", "step", "rest_summed", "rest_in", "rest_out", "spread", "carry", "counted", "count_carry",
                             "degrees", "degrees_root", "dinv"))
        s_num, s_val = sem("numbers_staged"), sem("values_staged")
        s_io = [m.lasting_sem(f"dense_dinv_moved{i}") for i in (0, 1)]
        s_copied = sem("dinv_copied")
        x3, out3 = (t[0:BULK_MAIN, :].rearrange("(p r) d -> p r d", p=P) for t in (x, out))
        block = ctx.enter_context(nc.Block())
        steps_of_dense = BULK_STEPS
        halves = steps_of_dense // 2

        @block.sync
        def _(sp):
            sp.dma_start(rest_in[:, :], x[BULK_MAIN:N, :]).then_inc(s_rest_in, 16)
            sp.dma_start(xin[0][:, :, :], x3[:, 0:BULK_ROWS, :]).then_inc(s_in[0], 16)
            sp.dma_start(xin[1][:, :, :], x3[:, BULK_ROWS:2 * BULK_ROWS, :]).then_inc(s_in[1], 16)
            with sp.Fori(1, halves) as i:
                for slot in (0, 1):
                    sp.wait_ge(s_sum, i * 2 + (slot - 1))
                    sp.dma_start(xin[slot][:, :, :], x3[:, bass.ds((i * 2 + slot) * BULK_ROWS, BULK_ROWS), :]).then_inc(s_in[slot], 16)
            sp.wait_ge(s_sum, 2 * halves - 1)
            sp.dma_start(xin[0][:, :, :], x3[:, 2 * halves * BULK_ROWS:, :]).then_inc(s_in[0], 16)

        @block.scalar
        def _(act):
            act.wait_ge(s_deg, 1)
            nc.scalar.activation(std[:, :], count[:, :], ACT.Sqrt).then_inc(s_std, 1)
            with act.Fori(0, halves) as i:
                for slot in (0, 1):
                    act.wait_ge(s_sum, i * 2 + (slot + 1))
                    act.dma_start(out3[:, bass.ds((i * 2 + slot) * BULK_ROWS, BULK_ROWS), :], xout[slot][:, :, :]).then_inc(s_out[slot], 16)
            act.wait_ge(s_sum, 2 * halves + 1)
            act.dma_start(out3[:, 2 * halves * BULK_ROWS:, :], xout[0][:, :, :]).then_inc(s_out[0], 16)
            act.wait_ge(s_rest, 1)
            act.dma_start(out[BULK_MAIN:N, :], rest_out[:, :]).then_inc(s_rest_out, 16)
            act.wait_ge(s_out[0], 16 * (halves + 1))
            act.wait_ge(s_out[1], 16 * halves)
            act.wait_ge(s_rest_out, 16)

        @block.tensor
        def _(pe):
            pe.wait_ge(s_count, 1)
            nc.tensor.matmul(count_ps[:, 0:1], m.before[BY_SRC][:, :], count[:, T - 1:T], start=True, stop=True).then_inc(s_carried, 1)
            pe.wait_ge(s_spread, 1)
            nc.tensor.matmul(carry_ps[:, 0:D], m.after[BY_DST][:, :], m.rows[:, 0, :], start=True, stop=True).then_inc(s_carry, 1)

        @block.gpsimd
        def _(pool):
            pool.wait_ge(s_dinv, 1)

            def put(i, first):
                for slot in (0, 1):
                    g = i * 2 + slot
                    if not first:
                        hold(pool, m.passed, s_io[slot], i * (16 * G))
                    nc.gpsimd.tensor_copy(value[slot][:, :], m.dinv_src[:, group(i, slot), 0]).then_inc(s_val, 1)
                    hold(pool, m.passed, s_val, g + 1)
                    stage_columns(pool, nc, m, numbers, m.tail_idx[BY_SRC], i, slot, s_num, g + 1)
                    for k in range(G):
                        pool.indirect_dma_start(m.dinv_table, bass.IndirectOffsetOnAxis(ap=numbers[slot][:, k:k + 1], axis=0),
                                                value[slot][:, k:k + 1], None, bounds_check=N - 1,
                                                oob_is_err=False).then_inc(s_io[slot], 16)
            turns(pool, put)
            for slot in (0, 1):
                pool.wait_ge(s_io[slot], 16 * G * PAIRS)

            def get(i, first):
                for slot in (0, 1):
                    g = i * 2 + slot
                    if not first:
                        hold(pool, m.passed, s_copied, g - 1)
                    stage_columns(pool, nc, m, numbers, m.dst_idx[BY_SRC], i, slot, s_num, g + (NG + 1))
                    for k in range(G):
                        pool.indirect_dma_start(value[slot][:, k:k + 1], None, m.dinv_table,
                                                bass.IndirectOffsetOnAxis(ap=numbers[slot][:, k:k + 1], axis=0)
                                                ).then_inc(s_io[slot], 16)
                    if not (first and slot == 0):
                        take(i - (1 - slot), 1 - slot)

            def take(i, slot):
                hold(pool, m.passed, s_io[slot], i * (16 * G) + 16 * G * (PAIRS + 1))
                nc.gpsimd.tensor_copy(m.dinv_dst[:, group(i, slot), 0], value[slot][:, :]).then_inc(s_copied, 1)
            turns(pool, get)
            take(PAIRS - 1, 1)
            pool.wait_ge(s_copied, NG)

        @block.vector
        def _(dve):
            v = nc.vector
            steps = Steps(dve, s_step)
            steps.inc(v.memset(ones_row[:, :], 1.0))
            steps.link(v.tensor_tensor(base[:, :, :], m.shift0[:, :, :], m.rb2[:, :, :], ALU.add))
            v.tensor_tensor_scan(count[:, :], m.same[BY_SRC][:, 0:T], ones_row[:, :], 0.0, ALU.mult, ALU.add).then_inc(s_count, 1)
            dve.wait_ge(s_carried, 1)
            v.scalar_tensor_tensor(count[:, :], m.first[BY_SRC][:, :, 0], count_ps[:, 0:1], count[:, :], ALU.mult,
                                   ALU.add).then_inc(s_deg, 1)
            dve.wait_ge(s_std, 1)
            v.reciprocal(m.dinv_src[:, :, 0], std[:, :]).then_inc(s_dinv, 1)

            per_turn = 5
            with dve.Fori(0, (T - 1) // per_turn) as i:
                steps.base, steps.k = i * per_turn + 2, 0
                for k in range(per_turn):
                    later, here = bass.ds(T - 1 - k - i * per_turn, 1), bass.ds(T - 2 - k - i * per_turn, 1)
                    steps.inc(v.scalar_tensor_tensor(m.rows[:, here, :], m.rows[:, later, :], m.same[BY_DST][:, later],
                                                     m.rows[:, here, :], ALU.mult, ALU.add))
                    steps.hold(m.passed)
            steps.base, steps.k = 2 + T - 1, 0
            v.nop().then_inc(s_spread, 1)
            dve.wait_ge(s_carry, 1)
            steps.link(v.tensor_copy(m.carry[:, 0, :], carry_ps[:, 0:D]))
            with dve.Fori(0, NG) as g:
                steps.base, steps.k = g * 2 + (2 + T), 0
                here = bass.ds(g * G, G)
                steps.link(v.tensor_tensor(tmp[:, :, :], m.carry[:, :, :].to_broadcast([P, G, D]),
                                           m.last[BY_DST][:, here, :].to_broadcast([P, G, D]), ALU.mult))
                steps.link(v.tensor_tensor(m.rows[:, here, :], tmp[:, :, :], m.rows[:, here, :], ALU.add))
            steps.base, steps.k = 2 + T + 2 * NG, 0

            def add(slot, n):
                v.tensor_tensor(xout[slot][:, :, :], xin[slot][:, :, :], base[:, :, :].to_broadcast([P, BULK_ROWS, D]),
                                ALU.add).then_inc(s_sum, 1)

            dve.wait_ge(s_rest_in, 16)
            v.tensor_tensor(rest_out[:, :], rest_in[:, :], base[0:N - BULK_MAIN, 0, :], ALU.add).then_inc(s_rest, 1)
            for slot in (0, 1):
                dve.wait_ge(s_in[slot], 16)
                add(slot, slot)
            with dve.Fori(1, halves) as i:
                for slot in (0, 1):
                    dve.wait_ge(s_in[slot], i * 16 + 16)
                    dve.wait_ge(s_out[slot], i * 16)
                    add(slot, i)
            dve.wait_ge(s_in[0], 16 * (halves + 1))
            dve.wait_ge(s_out[0], 16 * halves)
            add(0, halves)


def attend(nc, m, scores):
    with ExitStack() as ctx:
        def sb(nm, shape, dt=F32):
            return ctx.enter_context(nc.sbuf_tensor("at_" + nm, shape, dt))

        def two(nm, shape, dt=F32):
            return [sb(f"{nm}{i}", shape, dt) for i in (0, 1)]

        def sem(nm):
            return m.sem("at_" + nm)

        o = BY_DST
        numbers = two("numbers", [P, G], I32)
        hg, xs, xd = two("hg", [P, G, D]), two("xs", [P, G, D]), two("xd", [P, G, D])
        h = sb("h", [P, 2 * G, D])
        ht = sb("ht", [P, 2, G * D])
        tmp, qk = sb("tmp", [P, G, D]), sb("qk", [P, G, D])
        stats, mv, std, rstd, shift = (sb(n, [P, 2 * G, w]) for n, w in (("stats", 6), ("mv", 2), ("std", 1), ("rstd", 1), ("shift", 1)))
        turned = ctx.enter_context(nc.psum_tensor("at_turned", [P, 8 * D], F32))
        key = ctx.enter_context(nc.psum_tensor("at_key", [P, 8, D], F32))
        value = ctx.enter_context(nc.psum_tensor("at_value", [P, 8, D], F32))
        q = ctx.enter_context(nc.psum_tensor("at_q", [P, 8, D], F32))
        s_num, s_step, s_x1, s_var, s_std, s_norm, s_h, s_turned, s_ht, s_kvq, s_used, s_val = (
            sem(n) for n in ("numbers_staged", "step", "x1_made", "variance", "std", "norm", "h_made", "h_turned", "ht_made",
                             "kvq_made", "kvq_used", "values_kept"))
        s_hg = [m.lasting_sem(f"at_hg_in{i}") for i in (0, 1)]
        s_xs, s_xd, s_x1d = ([sem(f"{n}{i}") for i in (0, 1)] for n in ("xs_in", "xd_in", "x1d_stored"))
        block = ctx.enter_context(nc.Block())

        @block.gpsimd
        def _(pool):
            def body(i, first):
                for slot in (0, 1):
                    g = i * 2 + slot
                    if not first:
                        hold(pool, m.passed, s_h, g - 1)
                    stage_columns(pool, nc, m, numbers, m.src_idx[o], i, slot, s_num, g + 1)
                    gather(pool, hg[slot], m.h0_table, numbers[slot], s_hg[slot])
            turns(pool, body)

        @block.sync
        def _(sp):
            def body(i, first):
                for slot in (0, 1):
                    g = i * 2 + slot
                    if not first:
                        hold(sp, m.passed, s_h, g - 1)
                        hold(sp, m.passed, s_x1d[slot], i * 16)
                    sp.dma_start(xs[slot][:, :, :], chunk(m.x_src, i, slot)).then_inc(s_xs[slot], 16)
                    sp.dma_start(xd[slot][:, :, :], chunk(m.x_dst, i, slot)).then_inc(s_xd[slot], 16)
                    if not (first and slot == 0):
                        store(i - (1 - slot), 1 - slot, g)

            def store(i, slot, count):
                sp.wait_ge(s_x1, count)
                sp.dma_start(chunk(m.x1_dst, i, slot), xd[slot][:, :, :]).then_inc(s_x1d[slot], 16)
            turns(sp, body)
            store(PAIRS - 1, 1, NG)
            for slot in (0, 1):
                sp.wait_ge(s_x1d[slot], 16 * PAIRS)

        @block.vector
        def _(dve):
            v = nc.vector
            steps = Steps(dve, s_step)
            scale, shift0 = (r[:, :, :].to_broadcast([P, G, D]) for r in (m.scale0, m.shift0))

            def normalise(i, slot, first):
                g = i * 2 + slot
                dve.wait_ge(s_hg[slot], i * (16 * G) + 16 * G)
                steps.inc(v.tensor_tensor(hg[slot][:, :, :], hg[slot][:, :, :], scale, ALU.mult))
                steps.link(v.tensor_tensor(tmp[:, :, :], m.rows[:, group(i, slot), :], scale, ALU.mult))
                dve.wait_ge(s_xs[slot], i * 16 + 16)
                dve.wait_ge(s_xd[slot], i * 16 + 16)
                steps.inc(v.tensor_tensor(hg[slot][:, :, :], hg[slot][:, :, :], xs[slot][:, :, :], ALU.add))
                steps.link(v.tensor_tensor(tmp[:, :, :], tmp[:, :, :], xd[slot][:, :, :], ALU.add))
                steps.link(v.tensor_tensor(hg[slot][:, :, :], hg[slot][:, :, :], shift0, ALU.add))
                v.tensor_tensor(xd[slot][:, :, :], tmp[:, :, :], shift0, ALU.add).then_inc(s_x1, 1)
                dve.wait_ge(s_x1, g + 1)
                for k in range(G):
                    steps.inc(v.bn_stats(stats[:, k, :], hg[slot][:, k, :]))
                    steps.inc(v.bn_stats(stats[:, G + k, :], xd[slot][:, k, :]))
                steps.hold(m.passed)
                for k in range(2 * G):
                    ins = v.bn_aggr(mv[:, k, :], stats[:, k, :])
                    if k < 2 * G - 1:
                        steps.inc(ins)
                ins.then_inc(s_var, 1)
                dve.wait_ge(s_std, g + 1)
                steps.link(v.reciprocal(rstd[:, :, :], std[:, :, :]))
                v.scalar_tensor_tensor(shift[:, :, :], mv[:, :, 0:1], -1.0, rstd[:, :, :], ALU.mult, ALU.mult).then_inc(s_norm, 1)

            def score(i, slot):
                g = i * 2 + slot
                steps.link(v.tensor_tensor(qk[:, :, :], m.rel[:, :, :].to_broadcast([P, G, D]),
                                           m.weight[:, group(i, slot), :].to_broadcast([P, G, D]), ALU.mult))
                dve.wait_ge(s_kvq, g + 1)
                steps.link(v.tensor_tensor(qk[:, :, :], qk[:, :, :], q[:, 0:G, :], ALU.add))
                steps.link(v.tensor_tensor(qk[:, :, :], qk[:, :, :], key[:, 0:G, :], ALU.mult))
                v.tensor_reduce(scores[:, group(i, slot), :], qk[:, :, :].rearrange("p g (h c) -> p g h c", c=DK),
                                AX.X, ALU.add).then_inc(s_used, 1)
                dve.wait_ge(s_used, g + 1)

            def body(i, first):
                for slot in (0, 1):
                    normalise(i, slot, first)
                    if not (first and slot == 0):
                        score(i - (1 - slot), 1 - slot)
            turns(dve, body, steps, 2 * (5 + 2 * G + 2 * G - 1 + 1 + 3))
            score(PAIRS - 1, 1)

        @block.scalar
        def _(act):
            def body(i, first):
                for slot in (0, 1):
                    g = i * 2 + slot
                    act.wait_ge(s_var, g + 1)
                    nc.scalar.activation(std[:, :, :], mv[:, :, 1:2], ACT.Sqrt, bias=m.epsilon[:, 0:1]).then_inc(s_std, 1)
                    act.wait_ge(s_norm, g + 1)
                    if not (first and slot == 0):
                        act.wait_ge(s_turned, g * 2)
                    for k in range(G):
                        nc.scalar.activation(h[:, k, :], hg[slot][:, k, :], ACT.Relu, bias=shift[:, k, :], scale=rstd[:, k, :])
                        ins = nc.scalar.activation(h[:, G + k, :], xd[slot][:, k, :], ACT.Relu, bias=shift[:, G + k, :],
                                                   scale=rstd[:, G + k, :])
                    ins.then_inc(s_h, 1)
                    for side in (0, 1):
                        act.wait_ge(s_turned, g * 2 + (side + 1))
                        if side == 0 and not (first and slot == 0):
                            act.wait_ge(s_kvq, g)
                        nc.scalar.activation(ht[:, side, :], turned[:, 0:G * D], ACT.Copy).then_inc(s_ht, 1)
                    act.wait_ge(s_kvq, g + 1)
                    nc.scalar.activation(m.rows[:, group(i, slot), :], value[:, 0:G, :], ACT.Copy).then_inc(s_val, 1)
            turns(act, body)

        @block.tensor
        def _(pe):
            def body(i, first):
                for slot in (0, 1):
                    g = i * 2 + slot
                    pe.wait_ge(s_h, g + 1)
                    for side in (0, 1):
                        if side or not (first and slot == 0):
                            pe.wait_ge(s_ht, g * 2 + side)
                        for k in range(G):
                            ins = nc.tensor.transpose(turned[:, k * D:(k + 1) * D], h[:, side * G + k, :], m.ident[:, :])
                        ins.then_inc(s_turned, 1)
                    pe.wait_ge(s_ht, g * 2 + 2)
                    if not (first and slot == 0):
                        pe.wait_ge(s_used, g)
                        pe.wait_ge(s_val, g)
                    for k in range(G):
                        for n, (product, side, weights) in enumerate(((key, 0, m.wkv[:, 0:D]), (value, 0, m.wkv[:, D:2 * D]),
                                                                      (q, 1, m.wq[:, :]))):
                            nc.tensor.matmul(product[:, k, :], ht[:, side, k * D:(k + 1) * D], weights, start=True, stop=False)
                            ins = nc.tensor.matmul(product[:, k, :], m.ones[0:1, 0:P], m.bias_kvq[0:1, n * D:(n + 1) * D],
                                                   start=False, stop=True)
                    ins.then_inc(s_kvq, 1)
            turns(pe, body)


def softmax(nc, m, o, score, heads, scale, name):
    with ExitStack() as ctx:
        def sb(nm, shape, dt=F32):
            return ctx.enter_context(nc.sbuf_tensor(name + nm, shape, dt))

        top, top_back = sb("top", [P, T, heads]), sb("top_back", [P, T, heads])
        cut, cut_back = sb("cut", [P, T]), sb("cut_back", [P, T])
        cut_first, cut_last = sb("cut_first", [P, T]), sb("cut_last", [P, T])
        cut_chunks = [sb(f"cut_chunks{i}", [P, 1, P]) for i in (0, 1)]
        ends = sb("ends", [P, heads, P])
        all_ends = [ctx.enter_context(nc.psum_tensor(f"{name}all_ends{i}", [P, max(heads, 4), P], F32)) for i in (0, 1)]
        masked = sb("masked", [P, heads, P])
        reach = [sb(f"reach{i}", [P, heads]) for i in (0, 1)]
        s_step, s_ends, s_all, s_shifted, s_exp = (m.sem(name + n) for n in ("step", "ends", "all_ends", "shifted", "exp"))
        block = ctx.enter_context(nc.Block())

        @block.vector
        def _(dve):
            v = nc.vector
            steps = Steps(dve, s_step)
            for out, mark in ((cut[:, :], m.same[o][:, 0:T]), (cut_back[:, :], m.same[o][:, 1:T + 1]), (cut_first[:, :], m.first[o][:, :, 0]),
                              (cut_last[:, :], m.last[o][:, :, 0]), (cut_chunks[0][:, 0, :], m.after[o][:, :]),
                              (cut_chunks[1][:, 0, :], m.before[o][:, :])):
                steps.inc(v.tensor_scalar(out, mark, -1.0, BIG, ALU.add, ALU.mult))
            steps.wait()
            for h in range(heads):
                steps.inc(v.tensor_tensor_scan(top[:, :, h], cut[:, :], score[:, :, h], -BIG, ALU.add, ALU.max))
            steps.wait()
            for h in range(heads):
                steps.inc(v.tensor_tensor_scan(top_back[:, ::-1, h], cut_back[:, ::-1], top[:, ::-1, h], -BIG, ALU.add, ALU.max))
            steps.wait()
            for side, t in ((0, T - 1), (1, 0)):
                v.tensor_copy(ends[:, :, :], top_back[:, t, :].unsqueeze(2).to_broadcast([P, heads, P])).then_inc(s_ends, 1)
                dve.wait_ge(s_all, side + 1)
                steps.link(v.tensor_tensor(masked[:, :, :], all_ends[side][:, 0:heads, :],
                                           cut_chunks[side][:, :, :].to_broadcast([P, heads, P]), ALU.add))
                steps.link(v.tensor_reduce(reach[side][:, :], masked[:, :, :], AX.X, ALU.max))
            for side, marks in ((0, cut_first), (1, cut_last)):
                for h in range(heads):
                    steps.inc(v.scalar_tensor_tensor(top_back[:, :, h], marks[:, :], reach[side][:, h:h + 1], top_back[:, :, h],
                                                     ALU.add, ALU.max))
                steps.wait()
            v.tensor_tensor(score[:, :, :], score[:, :, :], top_back[:, :, :], ALU.subtract).then_inc(s_shifted, 1)

        @block.tensor
        def _(pe):
            for side in (0, 1):
                pe.wait_ge(s_ends, side + 1)
                for h in range(heads):
                    ins = nc.tensor.transpose(all_ends[side][:, h, :], ends[:, h, :], m.ident[:, :])
                ins.then_inc(s_all, 1)

        @block.scalar
        def _(act):
            act.wait_ge(s_shifted, 1)
            nc.scalar.activation(score[:, :, :], score[:, :, :], ACT.Exp, scale=scale).then_inc(s_exp, 1)


def weigh(nc, m, o, score, heads, total, name):
    with ExitStack() as ctx:
        def sb(nm, shape, dt=F32):
            return ctx.enter_context(nc.sbuf_tensor(name + nm, shape, dt))

        width = D // heads
        part = [sb(f"part{i}", [P, G, D]) for i in (0, 1)]
        carry_ps = ctx.enter_context(nc.psum_tensor(name + "carry", [P, 512], F32))
        total_ps = ctx.enter_context(nc.psum_tensor(name + "total", [P, 512], F32))
        s_step, s_sum, s_kept, s_ends, s_carry = (m.sem(name + n) for n in ("step", "summed", "kept", "ends", "carry"))
        same_g = [sb(f"same{i}", [P, G]) for i in (0, 1)]
        block = ctx.enter_context(nc.Block())

        @block.vector
        def _(dve):
            v = nc.vector
            steps = Steps(dve, s_step)
            for h in range(heads):
                steps.inc(v.tensor_tensor_scan(total[:, :, h], m.same[o][:, 0:T], score[:, :, h], 0.0, ALU.mult, ALU.add))
            steps.wait()

            def body(i, first):
                for slot in (0, 1):
                    g = i * 2 + slot
                    if not first:
                        dve.wait_ge(s_kept, g - 1)
                    steps.inc(v.tensor_copy(same_g[slot][:, :], m.same[o][:, group(i, slot)]))
                    weighed = (part[slot][:, :, :], m.rows[:, group(i, slot), :], score[:, group(i, slot), :])
                    if heads > 1:
                        out, row = (a.rearrange("p g (h c) -> p (g h) c", c=width) for a in weighed[0:2])
                        s = weighed[2].rearrange("p g h -> p (g h)").unsqueeze(2).to_broadcast([P, G * heads, width])
                    else:
                        out, row, s = weighed[0], weighed[1], weighed[2].to_broadcast([P, G, D])
                    steps.link(v.tensor_tensor(out, row, s, ALU.mult))
                    for k in range(G):
                        if first and slot == 0 and k == 0:
                            continue
                        before = part[slot][:, k - 1, :] if k else part[1 - slot][:, G - 1, :]
                        ins = v.scalar_tensor_tensor(part[slot][:, k, :], before, same_g[slot][:, k:k + 1], part[slot][:, k, :],
                                                     ALU.mult, ALU.add)
                        if k < G - 1:
                            steps.link(ins)
                        else:
                            ins.then_inc(s_sum, 1)
                            dve.wait_ge(s_sum, g + 1)
            turns(dve, body, steps, 2 * (G + 1))
            dve.wait_ge(s_carry, 1)
            steps.inc(v.tensor_copy(m.carry[:, 0, :], carry_ps[:, 0:D]))
            for h in range(heads):
                steps.inc(v.scalar_tensor_tensor(total[:, :, h], m.first[o][:, :, 0], total_ps[:, h:h + 1], total[:, :, h],
                                                 ALU.mult, ALU.add))
            steps.wait()
            steps.link(v.tensor_scalar(total[:, :, :], total[:, :, :], 1e-30, None, ALU.max))
            steps.link(v.reciprocal(total[:, :, :], total[:, :, :]))

        @block.scalar
        def _(act):
            def body(i, first):
                for slot in (0, 1):
                    g = i * 2 + slot
                    act.wait_ge(s_sum, g + 1)
                    nc.scalar.activation(m.rows[:, group(i, slot), :], part[slot][:, :, :], ACT.Copy).then_inc(s_kept, 1)
            turns(act, body)

        @block.tensor
        def _(pe):
            pe.wait_ge(s_kept, NG)
            nc.tensor.matmul(carry_ps[:, 0:D], m.before[o][:, :], m.rows[:, T - 1, :], start=True, stop=True)
            nc.tensor.matmul(total_ps[:, 0:heads], m.before[o][:, :], total[:, T - 1, :], start=True, stop=True).then_inc(s_carry, 1)


def finish(nc, m, o, total, heads, rectify, base_rows, table, name):
    with ExitStack() as ctx:
        def sb(nm, shape, dt=F32):
            return ctx.enter_context(nc.sbuf_tensor(name + nm, shape, dt))

        numbers = [sb(f"numbers{i}", [P, G], I32) for i in (0, 1)]
        base = [sb(f"base{i}", [P, G, D]) for i in (0, 1)]
        row = [sb(f"row{i}", [P, G, D]) for i in (0, 1)]
        tmp = sb("tmp", [P, G, D])
        s_num, s_step, s_row = (m.sem(name + n) for n in ("numbers_staged", "step", "rows_made"))
        s_base = [m.sem(f"{name}base_in{i}") for i in (0, 1)]
        s_scat = [m.lasting_sem(f"{name}scattered{i}") for i in (0, 1)]
        block = ctx.enter_context(nc.Block())

        @block.sync
        def _(sp):
            def body(i, first):
                for slot in (0, 1):
                    g = i * 2 + slot
                    if not first:
                        sp.wait_ge(s_row, g - 1)
                    sp.dma_start(base[slot][:, :, :], chunk(base_rows, i, slot)).then_inc(s_base[slot], 16)
            turns(sp, body)

        @block.gpsimd
        def _(pool):
            def body(i, first):
                for slot in (0, 1):
                    g = i * 2 + slot
                    if not first:
                        hold(pool, m.passed, s_scat[slot], i * (16 * G))
                    stage_columns(pool, nc, m, numbers, m.tail_idx[o], i, slot, s_num, g + 1)
                    hold(pool, m.passed, s_row, g + 1)
                    scatter(pool, table, row[slot], numbers[slot], s_scat[slot])
            turns(pool, body)
            for slot in (0, 1):
                pool.wait_ge(s_scat[slot], 16 * G * PAIRS)

        @block.vector
        def _(dve):
            v = nc.vector
            steps = Steps(dve, s_step)
            width = D // heads

            def body(i, first):
                for slot in (0, 1):
                    g = i * 2 + slot
                    steps.link(v.tensor_tensor(tmp[:, :, :], m.carry[:, :, :].to_broadcast([P, G, D]),
                                               m.first[o][:, group(i, slot), :].to_broadcast([P, G, D]), ALU.mult))
                    steps.link(v.tensor_tensor(tmp[:, :, :], tmp[:, :, :], m.rows[:, group(i, slot), :], ALU.add))
                    if heads > 1:
                        split = tmp[:, :, :].rearrange("p g (h c) -> p (g h) c", c=width)
                        per_head = total[:, group(i, slot), :].rearrange("p g h -> p (g h)").unsqueeze(2).to_broadcast([P, G * heads, width])
                    else:
                        split, per_head = tmp[:, :, :], total[:, group(i, slot), :].to_broadcast([P, G, D])
                    steps.link(v.tensor_tensor(split, split, per_head, ALU.mult))
                    dve.wait_ge(s_base[slot], i * 16 + 16)
                    if not first:
                        dve.wait_ge(s_scat[slot], i * (16 * G))
                    if rectify:
                        steps.link(v.scalar_tensor_tensor(tmp[:, :, :], tmp[:, :, :], 0.0, base[slot][:, :, :], ALU.max, ALU.add))
                        ins = v.tensor_tensor(row[slot][:, :, :], tmp[:, :, :], m.rb2[:, :, :].to_broadcast([P, G, D]), ALU.add)
                    else:
                        ins = v.tensor_tensor(row[slot][:, :, :], tmp[:, :, :], base[slot][:, :, :], ALU.add)
                    ins.then_inc(s_row, 1)
                    dve.wait_ge(s_row, g + 1)
            turns(dve, body, steps, 2 * (4 if rectify else 3))


def sum_neighbour_rows(nc, m, out):
    with ExitStack() as ctx:
        def sb(nm, shape, dt=F32):
            return ctx.enter_context(nc.sbuf_tensor("l2_" + nm, shape, dt))

        def two(nm, shape, dt=F32):
            return [sb(f"{nm}{i}", shape, dt) for i in (0, 1)]

        def sem(nm):
            return m.sem("l2_" + nm)

        o = BY_SRC
        dst_numbers, src_numbers = two("dst_numbers", [P, G], I32), two("src_numbers", [P, G], I32)
        yd, ys, x2, h = two("yd", [P, G, D]), two("ys", [P, G, D]), two("x2", [P, G, D]), two("h", [P, G, D])
        same_g, mv, std, rstd, shift = two("same", [P, G]), two("mv", [P, G, 2]), two("std", [P, G, 1]), two("rstd", [P, G, 1]), two("shift", [P, G, 1])
        stats = sb("stats", [P, G, 6])
        s_dst, s_src, s_step, s_x2, s_var, s_std, s_norm, s_h, s_sum, s_kept = (
            sem(n) for n in ("dst_staged", "src_staged", "step", "x2_made", "variance", "std", "norm", "h_made", "summed", "kept"))
        s_yd, s_ys = ([m.lasting_sem(f"l2_{n}{i}") for i in (0, 1)] for n in ("yd_in", "ys_in"))
        s_stored, s_ys_stored = ([sem(f"{n}{i}") for i in (0, 1)] for n in ("yd_stored", "ys_stored"))
        block = ctx.enter_context(nc.Block())

        @block.gpsimd
        def _(pool):
            def body(i, first):
                for slot in (0, 1):
                    g = i * 2 + slot
                    if not first:
                        hold(pool, m.passed, s_x2, g - 1)
                        hold(pool, m.passed, s_stored[slot], i * 16)
                    stage_columns(pool, nc, m, dst_numbers, m.dst_idx[o], i, slot, s_dst, g + 1)
                    gather(pool, yd[slot], out, dst_numbers[slot], s_yd[slot])
                    if not first:
                        hold(pool, m.passed, s_ys_stored[slot], i * 16)
                    stage_columns(pool, nc, m, src_numbers, m.src_idx[o], i, slot, s_src, g + 1)
                    gather(pool, ys[slot], out, src_numbers[slot], s_ys[slot])
            turns(pool, body)

        @block.sync
        def _(sp):
            with sp.Fori(0, PAIRS) as i:
                for slot in (0, 1):
                    sp.wait_ge(s_yd[slot], i * (16 * G) + 16 * G)
                    sp.dma_start(chunk(m.y_dst, i, slot), yd[slot][:, :, :]).then_inc(s_stored[slot], 16)
                    sp.wait_ge(s_ys[slot], i * (16 * G) + 16 * G)
                    sp.dma_start(chunk(m.y_src, i, slot), ys[slot][:, :, :]).then_inc(s_ys_stored[slot], 16)
            for slot in (0, 1):
                sp.wait_ge(s_stored[slot], 16 * PAIRS)
                sp.wait_ge(s_ys_stored[slot], 16 * PAIRS)

        @block.scalar
        def _(act):
            def body(i, first):
                for slot in (0, 1):
                    g = i * 2 + slot
                    act.wait_ge(s_var, g + 1)
                    nc.scalar.activation(std[slot][:, :, :], mv[slot][:, :, 1:2], ACT.Sqrt, bias=m.epsilon[:, 0:1]).then_inc(s_std, 1)
                    act.wait_ge(s_norm, g + 1)
                    if not first:
                        act.wait_ge(s_kept, g - 1)
                    for k in range(G):
                        ins = nc.scalar.activation(h[slot][:, k, :], x2[slot][:, k, :], ACT.Relu,
                                                   bias=shift[slot][:, k, :], scale=rstd[slot][:, k, :])
                    ins.then_inc(s_h, 1)
                    act.wait_ge(s_sum, g + 1)
                    nc.scalar.activation(m.rows[:, group(i, slot), :], h[slot][:, :, :], ACT.Copy).then_inc(s_kept, 1)
            turns(act, body)

        @block.vector
        def _(dve):
            v = nc.vector
            steps = Steps(dve, s_step)

            def body(i, first):
                for slot in (0, 1):
                    g = i * 2 + slot
                    dve.wait_ge(s_yd[slot], i * (16 * G) + 16 * G)
                    v.tensor_tensor(x2[slot][:, :, :], yd[slot][:, :, :], m.rb2[:, :, :].to_broadcast([P, G, D]),
                                    ALU.subtract).then_inc(s_x2, 1)
                    dve.wait_ge(s_x2, g + 1)
                    row_stats(v, m, steps, x2[slot], G, stats, mv[slot]).then_inc(s_var, 1)
                    steps.inc(v.tensor_copy(same_g[slot][:, :], m.same[o][:, group(i, slot)]))
                    dve.wait_ge(s_std, g + 1)
                    steps.link(v.reciprocal(rstd[slot][:, :, :], std[slot][:, :, :]))
                    steps.link(v.tensor_tensor(rstd[slot][:, :, :], rstd[slot][:, :, :], m.dinv_dst[:, group(i, slot), :], ALU.mult))
                    v.scalar_tensor_tensor(shift[slot][:, :, :], mv[slot][:, :, 0:1], -1.0, rstd[slot][:, :, :],
                                           ALU.mult, ALU.mult).then_inc(s_norm, 1)
                    dve.wait_ge(s_h, g + 1)
                    for k in range(G):
                        if first and slot == 0 and k == 0:
                            continue
                        before = h[slot][:, k - 1, :] if k else h[1 - slot][:, G - 1, :]
                        ins = v.scalar_tensor_tensor(h[slot][:, k, :], before, same_g[slot][:, k:k + 1], h[slot][:, k, :],
                                                     ALU.mult, ALU.add)
                        if k < G - 1:
                            steps.link(ins)
                        else:
                            ins.then_inc(s_sum, 1)
                            dve.wait_ge(s_sum, g + 1)
            turns(dve, body, steps, 2 * (3 * G + 1))


def transform_sums2(nc, m):
    with ExitStack() as ctx:
        def sb(nm, shape, dt=F32):
            return ctx.enter_context(nc.sbuf_tensor("t2_" + nm, shape, dt))

        def two(nm, shape, dt=F32):
            return [sb(f"{nm}{i}", shape, dt) for i in (0, 1)]

        def psum(nm, cols):
            return ctx.enter_context(nc.psum_tensor("t2_" + nm, [P, cols], F32))

        def sem(nm):
            return m.sem("t2_" + nm)

        o = BY_SRC
        numbers = two("numbers", [P, G], I32)
        u, d, uts, ys, h = two("u", [P, G, D]), two("d", [P, G, D]), two("uts", [P, G * D]), two("ys", [P, G, D]), two("h", [P, G, D])
        mv, std, rstd, shift = two("mv", [P, G, 2]), two("std", [P, G, 1]), two("rstd", [P, G, 1]), two("shift", [P, G, 1])
        tmp, stats = sb("tmp", [P, G, D]), sb("stats", [P, G, 6])
        ut, z, carry_ps, end_ps = [psum(f"ut{i}", 8 * D) for i in (0, 1)], psum("z", 8 * D), psum("carry", 512), psum("end", 512)
        s_num, s_step, s_carry, s_u, s_turned, s_uts, s_z, s_d, s_x3, s_var, s_std, s_norm, s_h, s_spread, s_end = (
            sem(n) for n in ("numbers_staged", "step", "carry_made", "u_made", "u_turned", "uts_made", "z_made", "d_made",
                             "x3_made", "variance", "std", "norm", "h_made", "scores_spread", "scores_carried"))
        s_scat = [m.lasting_sem(f"t2_scattered{i}") for i in (0, 1)]
        s_ys, s_stored = ([sem(f"{n}{i}") for i in (0, 1)] for n in ("ys_in", "x3_stored"))
        block = ctx.enter_context(nc.Block())

        @block.gpsimd
        def _(pool):
            def body(i, first):
                for slot in (0, 1):
                    g = i * 2 + slot
                    if not first:
                        hold(pool, m.passed, s_scat[slot], i * (16 * G))
                    stage_columns(pool, nc, m, numbers, m.tail_idx[o], i, slot, s_num, g + 1)
                    hold(pool, m.passed, s_d, g + 1)
                    scatter(pool, m.h2_table, d[slot], numbers[slot], s_scat[slot])
            turns(pool, body)
            for slot in (0, 1):
                pool.wait_ge(s_scat[slot], 16 * G * PAIRS)

        @block.sync
        def _(sp):
            def body(i, first):
                for slot in (0, 1):
                    g = i * 2 + slot
                    if not first:
                        sp.wait_ge(s_stored[slot], i * 16)
                        sp.wait_ge(s_h, g - 1)
                    sp.dma_start(ys[slot][:, :, :], chunk(m.y_src, i, slot)).then_inc(s_ys[slot], 16)
                    if not (first and slot == 0):
                        store(i - (1 - slot), 1 - slot, g)

            def store(i, slot, count):
                sp.wait_ge(s_x3, count)
                sp.dma_start(chunk(m.x3_src, i, slot), ys[slot][:, :, :]).then_inc(s_stored[slot], 16)
            turns(sp, body)
            store(PAIRS - 1, 1, NG)
            for slot in (0, 1):
                sp.wait_ge(s_stored[slot], 16 * PAIRS)

        @block.tensor
        def _(pe):
            nc.tensor.matmul(carry_ps[:, 0:D], m.before[o][:, :], m.rows[:, T - 1, :], start=True, stop=True).then_inc(s_carry, 1)

            def body(i, first):
                for slot in (0, 1):
                    g = i * 2 + slot
                    pe.wait_ge(s_u, g + 1)
                    for k in range(G):
                        ins = nc.tensor.transpose(ut[slot][:, k * D:(k + 1) * D], u[slot][:, k, :], m.ident[:, :])
                    ins.then_inc(s_turned, 1)
                    pe.wait_ge(s_uts, g + 1)
                    if not (first and slot == 0):
                        pe.wait_ge(s_d, g)
                    for k in range(G):
                        ins = nc.tensor.matmul(z[:, k * D:(k + 1) * D], uts[slot][:, k * D:(k + 1) * D], m.w2[:, :],
                                               start=True, stop=True)
                    ins.then_inc(s_z, 1)
            turns(pe, body)
            pe.wait_ge(s_spread, 1)
            nc.tensor.matmul(end_ps[:, 0:1], m.after[o][:, :], m.to_self[:, 0, :], start=True, stop=True).then_inc(s_end, 1)

        @block.scalar
        def _(act):
            def body(i, first):
                for slot in (0, 1):
                    g = i * 2 + slot
                    act.wait_ge(s_turned, g + 1)
                    nc.scalar.activation(uts[slot][:, :], ut[slot][:, 0:G * D], ACT.Copy).then_inc(s_uts, 1)
                    act.wait_ge(s_var, g + 1)
                    nc.scalar.activation(std[slot][:, :, :], mv[slot][:, :, 1:2], ACT.Sqrt, bias=m.epsilon[:, 0:1]).then_inc(s_std, 1)
                    act.wait_ge(s_norm, g + 1)
                    for k in range(G):
                        ins = nc.scalar.activation(h[slot][:, k, :], ys[slot][:, k, :], ACT.Relu,
                                                   bias=shift[slot][:, k, :], scale=rstd[slot][:, k, :])
                    ins.then_inc(s_h, 1)
            turns(act, body)

        @block.vector
        def _(dve):
            v = nc.vector
            steps = Steps(dve, s_step)
            dve.wait_ge(s_carry, 1)
            steps.link(v.tensor_copy(m.carry[:, 0, :], carry_ps[:, 0:D]))

            def body(i, first):
                for slot in (0, 1):
                    g = i * 2 + slot
                    steps.link(v.tensor_tensor(tmp[:, :, :], m.carry[:, :, :].to_broadcast([P, G, D]),
                                               m.first[o][:, group(i, slot), :].to_broadcast([P, G, D]), ALU.mult))
                    v.tensor_tensor(u[slot][:, :, :], tmp[:, :, :], m.rows[:, group(i, slot), :], ALU.add).then_inc(s_u, 1)
                    dve.wait_ge(s_u, g + 1)
                    dve.wait_ge(s_z, g + 1)
                    z3 = z[:, 0:G * D].rearrange("p (g d) -> p g d", d=D)
                    steps.link(v.tensor_tensor(tmp[:, :, :], z3, m.dinv_src[:, group(i, slot), :].to_broadcast([P, G, D]), ALU.mult))
                    steps.link(v.tensor_tensor(tmp[:, :, :], tmp[:, :, :], m.b2[:, :, :].to_broadcast([P, G, D]), ALU.add))
                    if not first:
                        dve.wait_ge(s_scat[slot], i * (16 * G))
                    v.scalar_tensor_tensor(d[slot][:, :, :], tmp[:, :, :], 0.0, m.rb2[:, :, :].to_broadcast([P, G, D]),
                                           ALU.max, ALU.subtract).then_inc(s_d, 1)
                    dve.wait_ge(s_d, g + 1)
                    dve.wait_ge(s_ys[slot], i * 16 + 16)
                    v.tensor_tensor(ys[slot][:, :, :], ys[slot][:, :, :], d[slot][:, :, :], ALU.add).then_inc(s_x3, 1)
                    dve.wait_ge(s_x3, g + 1)
                    row_stats(v, m, steps, ys[slot], G, stats, mv[slot]).then_inc(s_var, 1)
                    dve.wait_ge(s_std, g + 1)
                    steps.link(v.reciprocal(rstd[slot][:, :, :], std[slot][:, :, :]))
                    v.scalar_tensor_tensor(shift[slot][:, :, :], mv[slot][:, :, 0:1], -1.0, rstd[slot][:, :, :],
                                           ALU.mult, ALU.mult).then_inc(s_norm, 1)
                    dve.wait_ge(s_h, g + 1)
                    steps.link(v.tensor_tensor(tmp[:, :, :], h[slot][:, :, :], m.to_src[:, :, :].to_broadcast([P, G, D]), ALU.mult))
                    steps.link(v.tensor_reduce(m.to_self[:, group(i, slot), 0], tmp[:, :, :], AX.X, ALU.add))
            turns(dve, body, steps, 2 * (3 + 2 * G - 1 + 3))
            steps.link(v.tensor_tensor(m.to_self[:, :, 0], m.to_self[:, :, 0], m.tail[o][:, :, 0], ALU.mult))
            steps.link(v.tensor_tensor_scan(m.score3[:, ::-1, 0], m.same[o][:, T:0:-1], m.to_self[:, ::-1, 0], 0.0, ALU.mult, ALU.add))
            v.tensor_copy(m.to_self[:, :, 0], m.score3[:, :, 0]).then_inc(s_spread, 1)
            dve.wait_ge(s_end, 1)
            steps.link(v.scalar_tensor_tensor(m.to_self[:, :, 0], m.last[o][:, :, 0], end_ps[:, 0:1], m.score3[:, :, 0],
                                              ALU.mult, ALU.add))


def kan(nc, m):
    with ExitStack() as ctx:
        def sb(nm, shape, dt=F32):
            return ctx.enter_context(nc.sbuf_tensor("kan_" + nm, shape, dt))

        def two(nm, shape, dt=F32):
            return [sb(f"{nm}{i}", shape, dt) for i in (0, 1)]

        def sem(nm):
            return m.sem("kan_" + nm)

        o = BY_SRC
        numbers = two("numbers", [P, G], I32)
        hd, yd, h = two("hd", [P, G, D]), two("yd", [P, G, D]), two("h", [P, G, D])
        mv, std, rstd, shift = two("mv", [P, G, 2]), two("std", [P, G, 1]), two("rstd", [P, G, 1]), two("shift", [P, G, 1])
        tmp, stats, knots = sb("tmp", [P, G, D]), sb("stats", [P, G, 6]), sb("knots", [P, KNOTS])
        gate, silu = sb("gate", [P, G * D]), sb("silu", [P, G * D])
        ht = sb("ht", [P, G * D])
        near = two("near", [P, G * D])
        cube = [sb(f"cube{i}", [P, G * D]) for i in range(KNOTS)]
        turned = [ctx.enter_context(nc.psum_tensor(f"kan_turned{i}", [P, 8 * D], F32)) for i in (0, 1)]
        val = [ctx.enter_context(nc.psum_tensor(f"kan_val{i}", [P, 8, D], F32)) for i in (0, 1)]
        s_num, s_step, s_x3, s_var, s_std, s_norm, s_h, s_turned, s_ht, s_exp, s_silu, s_near, s_square, s_cube, s_val, s_kept, s_knots = (
            sem(n) for n in ("numbers_staged", "step", "x3_made", "variance", "std", "norm", "h_made", "h_turned", "ht_made",
                             "exp_made", "silu_made", "near_made", "squared", "cubed", "values_made", "values_kept", "knots_made"))
        s_hd = [m.lasting_sem(f"kan_hd_in{i}") for i in (0, 1)]
        s_yd = [sem(f"yd_in{i}") for i in (0, 1)]
        block = ctx.enter_context(nc.Block())

        @block.gpsimd
        def _(pool):
            for n in range(KNOTS):
                nc.gpsimd.memset(knots[:, n:n + 1], n + 0.5).then_inc(s_knots, 1)

            def body(i, first):
                for slot in (0, 1):
                    g = i * 2 + slot
                    if not first:
                        hold(pool, m.passed, s_x3, g - 1)
                    stage_columns(pool, nc, m, numbers, m.dst_idx[o], i, slot, s_num, g + 1)
                    gather(pool, hd[slot], m.h2_table, numbers[slot], s_hd[slot])
            turns(pool, body)

        @block.sync
        def _(sp):
            def body(i, first):
                for slot in (0, 1):
                    g = i * 2 + slot
                    if not first:
                        sp.wait_ge(s_h, g - 1)
                    sp.dma_start(yd[slot][:, :, :], chunk(m.y_dst, i, slot)).then_inc(s_yd[slot], 16)
            turns(sp, body)

        @block.vector
        def _(dve):
            v = nc.vector
            steps = Steps(dve, s_step)

            def front(i, slot, first):
                g = i * 2 + slot
                dve.wait_ge(s_hd[slot], i * (16 * G) + 16 * G)
                dve.wait_ge(s_yd[slot], i * 16 + 16)
                v.tensor_tensor(yd[slot][:, :, :], yd[slot][:, :, :], hd[slot][:, :, :], ALU.add).then_inc(s_x3, 1)
                dve.wait_ge(s_x3, g + 1)
                row_stats(v, m, steps, yd[slot], G, stats, mv[slot]).then_inc(s_var, 1)
                dve.wait_ge(s_std, g + 1)
                steps.link(v.reciprocal(rstd[slot][:, :, :], std[slot][:, :, :]))
                v.scalar_tensor_tensor(shift[slot][:, :, :], mv[slot][:, :, 0:1], -1.0, rstd[slot][:, :, :],
                                       ALU.mult, ALU.mult).then_inc(s_norm, 1)

            def back(i, slot, g, first):
                dve.wait_ge(s_h, g + 1)
                steps.link(v.tensor_tensor(tmp[:, :, :], h[slot][:, :, :], m.to_dst[:, :, :].to_broadcast([P, G, D]), ALU.mult))
                steps.inc(v.tensor_reduce(m.score3[:, group(i, slot), 0], tmp[:, :, :], AX.X, ALU.add))
                dve.wait_ge(s_exp, g + 1)
                steps.link(v.tensor_scalar(gate[:, :], gate[:, :], 1.0, None, ALU.add))
                steps.link(v.reciprocal(gate[:, :], gate[:, :]))
                dve.wait_ge(s_ht, g + 1)
                if not first:
                    dve.wait_ge(s_val, g)
                v.tensor_tensor(silu[:, :], gate[:, :], ht[:, :], ALU.mult).then_inc(s_silu, 1)
                for n in range(KNOTS):
                    dve.wait_ge(s_square, g * KNOTS + (n + 1))
                    v.tensor_tensor(cube[n][:, :], cube[n][:, :], near[n % 2][:, :], ALU.mult).then_inc(s_cube, 1)

            def body(i, first):
                for slot in (0, 1):
                    front(i, slot, first)
                    if not (first and slot == 0):
                        back(i - (1 - slot), 1 - slot, i * 2 + (slot - 1), first and slot == 1)
            turns(dve, body, steps, 2 * (2 * G - 1 + 1 + 4))
            back(PAIRS - 1, 1, NG - 1, False)

        @block.scalar
        def _(act):
            act.wait_ge(s_knots, KNOTS)

            def front(i, slot, first):
                g = i * 2 + slot
                act.wait_ge(s_var, g + 1)
                nc.scalar.activation(std[slot][:, :, :], mv[slot][:, :, 1:2], ACT.Sqrt, bias=m.epsilon[:, 0:1]).then_inc(s_std, 1)
                act.wait_ge(s_norm, g + 1)
                for k in range(G):
                    ins = nc.scalar.activation(h[slot][:, k, :], yd[slot][:, k, :], ACT.Relu,
                                               bias=shift[slot][:, k, :], scale=rstd[slot][:, k, :])
                ins.then_inc(s_h, 1)

            def back(i, slot, g, first):
                act.wait_ge(s_turned, g + 1)
                if not first:
                    act.wait_ge(s_silu, g)
                nc.scalar.activation(gate[:, :], turned[slot][:, 0:G * D], ACT.Exp, scale=-1.0).then_inc(s_exp, 1)
                nc.scalar.activation(ht[:, :], turned[slot][:, 0:G * D], ACT.Copy).then_inc(s_ht, 1)
                act.wait_ge(s_ht, g + 1)
                for n in range(KNOTS):
                    if not (first and n < 2):
                        act.wait_ge(s_cube, g * KNOTS + (n - 1))
                    nc.scalar.activation(near[n % 2][:, :], ht[:, :], ACT.Relu, bias=knots[:, n:n + 1], scale=-2.5).then_inc(s_near, 1)
                    act.wait_ge(s_near, g * KNOTS + (n + 1))
                    if n == 0 and not first:
                        act.wait_ge(s_val, g)
                    nc.scalar.activation(cube[n][:, :], near[n % 2][:, :], ACT.Square).then_inc(s_square, 1)
                act.wait_ge(s_val, g + 1)
                nc.scalar.activation(m.rows[:, group(i, slot), :], val[slot][:, 0:G, :], ACT.Copy).then_inc(s_kept, 1)

            def body(i, first):
                for slot in (0, 1):
                    front(i, slot, first)
                    if not (first and slot == 0):
                        back(i - (1 - slot), 1 - slot, i * 2 + (slot - 1), first and slot == 1)
            turns(act, body)
            back(PAIRS - 1, 1, NG - 1, False)

        @block.tensor
        def _(pe):
            def front(i, slot, first):
                g = i * 2 + slot
                pe.wait_ge(s_h, g + 1)
                if not first:
                    pe.wait_ge(s_ht, g - 1)
                for k in range(G):
                    ins = nc.tensor.transpose(turned[slot][:, k * D:(k + 1) * D], h[slot][:, k, :], m.ident[:, :])
                ins.then_inc(s_turned, 1)

            def back(i, slot, g, first):
                pe.wait_ge(s_silu, g + 1)
                if not first:
                    pe.wait_ge(s_kept, g - 1)
                pe.wait_ge(s_cube, g * KNOTS + KNOTS)
                for k in range(G):
                    cols = slice(k * D, (k + 1) * D)
                    nc.tensor.matmul(val[slot][:, k, :], silu[:, cols], m.w_kan[:, 0, :], start=True, stop=False)
                    for n in range(KNOTS):
                        ins = nc.tensor.matmul(val[slot][:, k, :], cube[n][:, cols], m.w_kan[:, 1 + n, :], start=False,
                                               stop=(n == KNOTS - 1))
                ins.then_inc(s_val, 1)

            def body(i, first):
                for slot in (0, 1):
                    front(i, slot, first)
                    if not (first and slot == 0):
                        back(i - (1 - slot), 1 - slot, i * 2 + (slot - 1), first)
            turns(pe, body)
            back(PAIRS - 1, 1, NG - 1, False)


def score_edges3(nc, m):
    with ExitStack() as ctx:
        s_step = m.sem("leaky_step")
        block = ctx.enter_context(nc.Block())

        @block.vector
        def _(dve):
            steps = Steps(dve, s_step)
            steps.link(nc.vector.tensor_tensor(m.score3[:, :, :], m.score3[:, :, :], m.to_self[:, :, :], ALU.add))
            steps.link(nc.vector.scalar_tensor_tensor(m.score3[:, :, :], m.score3[:, :, :], 0.2, m.score3[:, :, :], ALU.mult, ALU.max))


def build(nc, x, records, src, dst, w, out):
    with ExitStack() as ctx:
        m = Memory(nc, ctx)
        sort_edges(nc, m, src, dst)
        m.end_phase()
        index_edges(nc, m, records)
        m.end_phase()
        load_weights(nc, m, w)
        m.end_phase()
        sum_source_rows(nc, m, x)
        m.end_phase()
        transform_sums0(nc, m, x)
        m.end_phase()
        batch_norm_rows(nc, m)
        m.end_phase()
        dense_pass(nc, m, x, out)
        m.end_phase()
        with nc.sbuf_tensor("scores", [P, T, H], F32) as scores, nc.sbuf_tensor("totals1", [P, T, H], F32) as totals:
            attend(nc, m, scores)
            m.end_phase()
            softmax(nc, m, BY_DST, scores, H, DK ** -0.5, "sm1_")
            m.end_phase()
            weigh(nc, m, BY_DST, scores, H, totals, "w1_")
            m.end_phase()
            finish(nc, m, BY_DST, totals, H, True, m.x1_dst, out, "f1_")
            m.end_phase()
        sum_neighbour_rows(nc, m, out)
        m.end_phase()
        transform_sums2(nc, m)
        m.end_phase()
        kan(nc, m)
        m.end_phase()
        score_edges3(nc, m)
        m.end_phase()
        softmax(nc, m, BY_SRC, m.score3, 1, 1.0, "sm3_")
        m.end_phase()
        weigh(nc, m, BY_SRC, m.score3, 1, m.total3, "w3_")
        m.end_phase()
        finish(nc, m, BY_SRC, m.total3, 1, False, m.x3_src, out, "f3_")
        m.end_phase()


def kernel(**inputs):
    import numpy as np
    import concourse.bacc as bacc
    from concourse.bass_utils import run_bass_kernel_spmd as run

    def array(name):
        return np.ascontiguousarray(inputs[name])

    records = np.zeros((E, 4), np.int32)
    records[:, SRC], records[:, DST], records[:, WEIGHT] = array("src"), array("dst"), array("edge_weight").view(np.int32)
    arrays = {
        "x": array("x"), "records": records, "src": array("src"), "dst": array("dst"),
        "w0": array("L0_gnn_W").T, "b0": array("L0_gnn_b"), "gamma": array("L0_gnn_gamma"), "beta": array("L0_gnn_beta"),
        "wk": array("L1_gnn_Wk").T, "bk": array("L1_gnn_bk"), "wq": array("L1_gnn_Wq").T, "bq": array("L1_gnn_bq"),
        "wv": array("L1_gnn_Wv"), "bv": array("L1_gnn_bv"), "rel": array("L1_gnn_rel_att").reshape(D),
        "rel_msg": array("L1_gnn_rel_msg"), "w2": array("L2_gnn_kernel"), "b2": array("L2_gnn_bias"),
        "w3t": array("L3_gnn_W").T, "a": array("L3_gnn_a"), "base": array("L3_gnn_base_weight").T,
        "spline": array("L3_gnn_spline_weight").transpose(2, 1, 0),
    }
    arrays = {"in_" + name: np.ascontiguousarray(a) for name, a in arrays.items()}
    nc = bacc.Bacc("TRN2", target_bir_lowering=False, num_devices=1)
    aps = {name[3:]: nc.dram_tensor(name, a.shape, mybir.dt.from_np(a.dtype), kind="ExternalInput").ap()
           for name, a in arrays.items()}
    out = nc.dram_tensor("out_x", (N, D), F32, kind="ExternalOutput").ap()
    x, records, src, dst = (aps.pop(name) for name in ("x", "records", "src", "dst"))
    build(nc, x, records, src, dst, aps, out)
    return run(nc, [arrays], core_ids=[0]).results[0]["out_x"]
```

```python
import concourse.bass as bass
from concourse import mybir
from contextlib import ExitStack

F32 = mybir.dt.float32
I32 = mybir.dt.int32
ALU = mybir.AluOpType
ACT = mybir.ActivationFunctionType
AX = mybir.AxisListType

N = 100000
E = 25000
D = 128
H = 8
DK = D // H
P = 128
T = -(-E // P)
G = 7
NG = T // G
PAIRS = NG // 2
SORT = 32768
SF = SORT // P
ID_BITS = 15
HALF = N // 2
CODE = 15000
PAD_NODE = N + 1
PAD_CODE = PAD_NODE - HALF + CODE
OUT_OF_RANGE = 200000
BIG = 1.0e38
EPS = 1e-5
BY_DST, BY_SRC = 0, 1
SRC, DST, WEIGHT = 0, 1, 2
BULK_ROWS = 11
BULK_MAIN = P * (N // P)
BULK_STEPS = N // P // BULK_ROWS
BACK_STEPS = 13
BACK_TURNS = (T - 1) // BACK_STEPS
KNOTS = 6
DVE_KNOTS = 3
GRID_STEP = 0.4
SPLINES = 8


class Steps:

    def __init__(self, eng, sem):
        self.eng, self.sem, self.base, self.k = eng, sem, 0, 0

    def inc(self, ins):
        ins.then_inc(self.sem, 1)
        self.k += 1

    def wait(self):
        self.eng.wait_ge(self.sem, self.base + self.k)

    def hold(self, passed):
        hold(self.eng, passed, self.sem, self.base + self.k)

    def link(self, ins):
        self.inc(ins)
        self.wait()


def hold(eng, passed, sem, value):
    eng.wait_ge(sem, value)
    if not isinstance(value, int):
        eng.sem_inc(passed, 1)


def turns(eng, body, steps=None, per=0):
    body(0, True)
    before = steps.base + steps.k if steps else 0
    with eng.Fori(1, PAIRS) as i:
        if steps:
            steps.base, steps.k = i * per + (before - per), 0
        body(i, False)
        assert not steps or steps.k == per, (steps.k, per)
    if steps:
        steps.base, steps.k = before + per * (PAIRS - 1), 0


def group(i, slot):
    return bass.ds((i * 2 + slot) * G, G)


def chunk(rows, i, slot):
    return rows[:, group(i, slot), :]


class Memory:

    def __init__(self, nc, ctx):
        def sb(name, shape, dt=F32):
            return ctx.enter_context(nc.sbuf_tensor(name, shape, dt))

        self.nc, self.ctx, self.sb = nc, ctx, sb
        self.words_dram = nc.dram_tensor("sorted_words", (2, SORT + P), I32).ap()
        self.h0_table = nc.dram_tensor("h0_table", (N, D), F32).ap()
        self.h2_table = nc.dram_tensor("h2_table", (N, D), F32).ap()
        self.dinv_table = nc.dram_tensor("dinv_table", (N, 1), F32).ap()
        def edge_rows(name):
            return nc.dram_tensor(name, (P, T, D), F32).ap()

        self.x_src, self.x_dst, self.x1_dst = edge_rows("x_src"), edge_rows("x_dst"), edge_rows("x1_dst")
        self.y_src, self.y_dst, self.x3_src = edge_rows("y_src"), edge_rows("y_dst"), edge_rows("x3_src")
        self.rows = sb("rows", [P, T, D])
        self.ident = sb("ident", [P, P])
        self.ones = sb("ones", [P, P])
        self.epsilon = sb("epsilon", [P, 1])
        self.edge_no = [sb(f"edge_no{o}", [P, T], I32) for o in (0, 1)]
        self.code = [sb(f"code{o}", [P, T + 2]) for o in (0, 1)]
        self.same = [sb(f"same{o}", [P, T + 1]) for o in (0, 1)]
        self.tail = [sb(f"tail{o}", [P, T, 1]) for o in (0, 1)]
        self.first = [sb(f"first{o}", [P, T, 1]) for o in (0, 1)]
        self.last = [sb(f"last{o}", [P, T, 1]) for o in (0, 1)]
        self.before = [sb(f"before{o}", [P, P]) for o in (0, 1)]
        self.after = [sb(f"after{o}", [P, P]) for o in (0, 1)]
        self.src_idx = [sb(f"src_idx{o}", [P, T], I32) for o in (0, 1)]
        self.dst_idx = [sb(f"dst_idx{o}", [P, T], I32) for o in (0, 1)]
        self.tail_idx = [sb(f"tail_idx{o}", [P, T], I32) for o in (0, 1)]
        self.weight = sb("weight", [P, T, 1])
        self.carry = sb("carry", [P, 1, D])
        def spread(name, cols=D):
            return sb(name, [P, 1, cols])

        self.b0, self.rb0, self.scale0, self.shift0 = spread("b0"), spread("rb0"), spread("scale0"), spread("shift0")
        self.b2, self.rb2, self.rel = spread("b2"), spread("rb2"), spread("rel")
        self.to_src = spread("to_src")
        self.gamma_beta = sb("gamma_beta", [1, 2 * D])
        self.totals = sb("totals", [1, 2 * D])
        self.w0, self.wq, self.w2 = sb("w0", [D, D]), sb("wq", [D, D]), sb("w2", [D, D])
        self.to_dst = sb("to_dst", [D, 1])
        self.wkv = sb("wkv", [D, 2 * D])
        self.bias_kvq = sb("bias_kvq", [1, 3 * D])
        self.w_kan = sb("w_kan", [D, KNOTS + 1, D])
        self.score3 = sb("score3", [P, T, 1])
        self.total3 = sb("total3", [P, T, 1])
        self.to_self = sb("to_self", [P, T, 1])
        self.dinv_src = sb("dinv_src", [P, T, 1])
        self.dinv_dst = sb("dinv_dst", [P, T, 1])
        self.phase_sems = []
        self.passed = self.lasting_sem("passed")

    def sem(self, name):
        sem = self.nc.alloc_semaphore(name=name)
        self.phase_sems.append(sem)
        return sem

    def lasting_sem(self, name):
        return self.nc.alloc_semaphore(name=name)

    def end_phase(self):
        for sem in self.phase_sems:
            self.nc.sync.sem_clear(sem)
            self.nc.release_semaphore(sem)
        self.phase_sems = []
        self.nc.all_engine_barrier()


def sort_edges(nc, m, src, dst):
    with ExitStack() as ctx:
        def sb(name, shape, dt=F32):
            return ctx.enter_context(nc.sbuf_tensor(name, shape, dt))

        key = sb("sort_key", [P, 2, SF], I32)
        key_f = sb("sort_key_f", [P, 2, SF])
        low = sb("sort_low", [P, 2, SF])
        code = sb("sort_code", [P, 2, SF], I32)
        slot = sb("sort_slot", [P, 2, SF], I32)
        gray = sb("sort_gray", [P, 2, SF], I32)
        flips = sb("sort_flips", [P, 2, SF], I32)
        zero_row = sb("sort_zero", [1, 2], I32)
        words = [sb(f"sort_words{i}", [P, 2 * SF]) for i in (0, 1)]
        turned = [ctx.enter_context(nc.psum_tensor(f"sort_turned{i}", [P, 2 * SF], F32)) for i in (0, 1)]
        s_key_pad, s_keys, s_ident, s_slot = (m.sem(n) for n in ("key_pad", "keys_in", "ident_made", "slot_made"))
        s_step, s_ready, s_turned = m.sem("sort_step"), m.sem("sort_ready"), m.sem("sort_turned_done")
        zeros = sb("table_zeros", [P, BULK_ROWS * D])
        s_zero, s_tables = m.sem("zeros_made"), m.sem("tables_zeroed")
        s_out, s_zero_row = m.sem("words_out"), m.sem("zero_row_made")
        full = E // SF
        rest = E - full * SF
        s_sorted = m.sem("sorted")

        block = ctx.enter_context(nc.Block())

        @block.sync
        def _(sp):
            sp.wait_ge(s_key_pad, 1)
            for o, keys in ((BY_DST, dst), (BY_SRC, src)):
                sp.dma_start(key[0:full, o, :], keys[0:full * SF].rearrange("(p f) -> p f", f=SF)).then_inc(s_keys, 16)
                sp.dma_start(key[full:full + 1, o, 0:rest],
                             keys[full * SF:E].rearrange("(p f) -> p f", p=1)).then_inc(s_keys, 16)
            sp.wait_ge(s_zero, 1)
            whole = m.h0_table[0:BULK_MAIN, :].rearrange("(p r) d -> p (r d)", p=P)
            with sp.Fori(0, BULK_STEPS) as i:
                sp.dma_start(whole[:, bass.ds(i * (BULK_ROWS * D), BULK_ROWS * D)], zeros[:, :]).then_inc(s_tables, 16)
            sp.dma_start(m.h0_table[BULK_MAIN:N, :], zeros[0:N - BULK_MAIN, 0:D]).then_inc(s_tables, 16)
            sp.dma_start(m.dinv_table[0:BULK_MAIN, :].rearrange("(p r) d -> p (r d)", p=P),
                         zeros[:, 0:N // P]).then_inc(s_tables, 16)
            sp.dma_start(m.dinv_table[BULK_MAIN:N, :], zeros[0:N - BULK_MAIN, 0:1]).then_inc(s_tables, 16)
            sp.wait_ge(s_tables, 16 * (BULK_STEPS + 3))

        @block.scalar
        def _(act):
            act.wait_ge(s_zero_row, 1)
            for o in (BY_DST, BY_SRC):
                act.dma_start(m.words_dram[o:o + 1, 0:1], zero_row[0:1, o:o + 1]).then_inc(s_out, 16)
            act.wait_ge(s_sorted, 1)
            for o in (BY_DST, BY_SRC):
                act.dma_start(m.words_dram[o, 1:1 + SORT].rearrange("(p f) -> p f", f=SF),
                              words[0][:, o * SF:(o + 1) * SF].bitcast(I32)).then_inc(s_out, 16)
            act.wait_ge(s_out, 64)

        @block.gpsimd
        def _(pool):
            nc.gpsimd.memset(key[:, :, :], PAD_NODE).then_inc(s_key_pad, 1)
            nc.gpsimd.memset(m.ident[:, :], 0.0).then_inc(s_ident, 1)
            nc.gpsimd.iota(slot[:, :, :], pattern=[[0, 2], [1, SF]], base=0, channel_multiplier=SF).then_inc(s_slot, 1)
            nc.gpsimd.memset(zeros[:, :], 0.0).then_inc(s_zero, 1)
            nc.gpsimd.memset(zero_row[:, :], 0).then_inc(s_zero_row, 1)
            pool.wait_ge(s_ident, 1)
            nc.gpsimd.affine_select(out=m.ident[:, :], in_=m.ident[:, :], compare_op=ALU.not_equal, fill=1.0,
                                    base=0, pattern=[[-1, P]], channel_multiplier=1).then_inc(s_ident, 1)

        @block.vector
        def _(dve):
            steps = Steps(dve, s_step)
            dve.wait_ge(s_slot, 1)
            dve.wait_ge(s_keys, 64)
            v = nc.vector
            steps.inc(v.tensor_scalar(gray[:, :, :], slot[:, :, :], 1, None, ALU.logical_shift_right))
            steps.link(v.tensor_copy(key_f[:, :, :], key[:, :, :]))
            steps.inc(v.tensor_tensor(flips[:, :, :], gray[:, :, :], slot[:, :, :], ALU.bitwise_xor))
            steps.link(v.tensor_scalar(low[:, :, :], key_f[:, :, :], float(HALF), float(2 ** 16 + HALF), ALU.is_lt, ALU.mult))
            steps.inc(v.tensor_copy(gray[:, :, :], flips[:, :, :]))
            steps.link(v.scalar_tensor_tensor(code[:, :, :], key_f[:, :, :], float(CODE - HALF), low[:, :, :], ALU.add, ALU.add))
            steps.inc(v.tensor_scalar(key[:, :, :], code[:, :, :], ID_BITS, None, ALU.logical_shift_left))
            steps.link(v.tensor_scalar(flips[:, :, :], slot[:, :, :], 30, -2 ** 31, ALU.logical_shift_left, ALU.bitwise_and))
            flat = [w[:, :].bitcast(I32) for w in words]
            slot2, key2 = (a[:, :, :].rearrange("p o f -> p (o f)") for a in (slot, key))
            flips2, gray2 = (a[:, :, :].rearrange("p o f -> p (o f)") for a in (flips, gray))
            steps.link(v.tensor_tensor(flat[0], key2, slot2, ALU.bitwise_or))
            turns = 0
            at = 0

            def exchange(a, b, distance):
                x, y = (w[:, :].rearrange("p (a two b) -> p a two b", two=2, b=distance) for w in (words[a], words[b]))
                steps.inc(v.tensor_tensor(y[:, :, 0, :], x[:, :, 0, :], x[:, :, 1, :], ALU.min))
                steps.link(v.tensor_tensor(y[:, :, 1, :], x[:, :, 0, :], x[:, :, 1, :], ALU.max))

            def turn(a, b):
                nonlocal turns
                v.nop().then_inc(s_ready, 1)
                turns += 1
                dve.wait_ge(s_turned, turns)
                steps.link(v.tensor_copy(words[b][:, :], turned[0][:, :]))

            for k in range(1, ID_BITS + 1):
                if k > 1:
                    steps.link(v.tensor_scalar(flips2, gray2, 32 - k, -2 ** 31, ALU.logical_shift_left, ALU.bitwise_and))
                steps.link(v.tensor_tensor(flat[1 - at], flat[at], flips2, ALU.bitwise_xor))
                at = 1 - at
                if k > 8:
                    turn(at, 1 - at)
                    at = 1 - at
                    for j in range(k - 1, 7, -1):
                        exchange(at, 1 - at, 2 ** (j - 8))
                        at = 1 - at
                    exchange(at, 1 - at, P)
                    at = 1 - at
                    turn(at, 1 - at)
                    at = 1 - at
                for j in range(min(k - 1, 6 if k > 8 else 7), -1, -1):
                    exchange(at, 1 - at, 2 ** j)
                    at = 1 - at
            if at:
                steps.link(v.tensor_copy(words[0][:, :], words[1][:, :]))
            v.nop().then_inc(s_sorted, 1)

        @block.tensor
        def _(pe):
            pe.wait_ge(s_ident, 2)
            at, turns = 0, 0
            for k in range(1, ID_BITS + 1):
                at = 1 - at
                if k > 8:
                    for exchanges in (k - 7, 0):
                        turns += 1
                        pe.wait_ge(s_ready, turns)
                        for b in range(4):
                            last = nc.tensor.transpose(turned[0][:, b * P:(b + 1) * P], words[at][:, b * P:(b + 1) * P], m.ident[:, :])
                        last.then_inc(s_turned, 1)
                        at = (at + 1 + exchanges) % 2
                at = (at + (7 if k > 8 else k)) % 2


def record_slots(m, ctx, name):
    stage = [ctx.enter_context(m.nc.sbuf_tensor(f"{name}numbers{i}", [P, G], I32)) for i in (0, 1)]
    got = [ctx.enter_context(m.nc.sbuf_tensor(f"{name}slot{i}", [P, G, 4], I32)) for i in (0, 1)]
    return stage, got, m.sem(name + "staged"), m.sem(name + "taken"), [m.lasting_sem(f"{name}in{i}") for i in (0, 1)]


def fetch_records(nc, m, pool, o, records, fetch):
    stage, got, s_stage, s_taken, s_in = fetch
    other, column = (m.src_idx[o], SRC) if o == BY_DST else (m.dst_idx[o], DST)
    copies = 2 if o == BY_DST else 1

    def take(i, slot):
        hold(pool, m.passed, s_in[slot], i * (16 * G) + 16 * G)
        nc.gpsimd.tensor_copy(other[:, group(i, slot)], got[slot][:, :, column]).then_inc(s_taken, 1)
        if o == BY_DST:
            nc.gpsimd.tensor_copy(m.weight[:, group(i, slot), 0].bitcast(I32), got[slot][:, :, WEIGHT]).then_inc(s_taken, 1)

    def body(i, first):
        for slot in (0, 1):
            g = i * 2 + slot
            if not first:
                hold(pool, m.passed, s_taken, (g - 1) * copies)
            stage_columns(pool, nc, m, stage, m.edge_no[o], i, slot, s_stage, g + 1)
            gather(pool, got[slot], records, stage[slot], s_in[slot])
            if not (first and slot == 0):
                take(i - (1 - slot), 1 - slot)
    turns(pool, body)
    take(PAIRS - 1, 1)
    pool.wait_ge(s_taken, NG * copies)


def index_edges(nc, m, records):
    with ExitStack() as ctx:
        def sb(name, shape, dt=F32):
            return ctx.enter_context(nc.sbuf_tensor(name, shape, dt))

        words = [sb(f"words{o}", [P, T + 2], I32) for o in (0, 1)]
        code_i = sb("code_i", [P, T + 2], I32)
        edge_f = sb("edge_f", [P, T])
        not_pad = sb("not_pad", [P, T])
        end_rows = sb("end_rows", [P, P])
        upper = sb("upper", [P, P])
        row_end = ctx.enter_context(nc.psum_tensor("row_end", [P, P], F32))
        before_t = ctx.enter_context(nc.psum_tensor("before_t", [P, P], F32))
        count_ps = ctx.enter_context(nc.psum_tensor("count_carry", [P, 512], F32))
        row_f, node_f = sb("row_f", [P, T]), sb("node_f", [P, T])
        ones_row, count, root = sb("ones_row", [P, T]), sb("count", [P, T]), sb("root", [P, T])
        s_words, s_step, s_ids, s_upper = m.sem("words_in"), m.sem("index_step"), m.sem("edge_ids"), m.sem("upper_made")
        s_row, s_rowt, s_bef, s_beft = m.sem("end_rows_ready"), m.sem("end_rows_turned"), m.sem("before_ready"), m.sem("before_turned")
        s_count, s_counted, s_root = m.sem("counts"), m.sem("counts_carried"), m.sem("count_roots")
        fetch = record_slots(m, ctx, "rec0_")

        block = ctx.enter_context(nc.Block())

        @block.sync
        def _(sp):
            for o in (BY_DST, BY_SRC):
                w = m.words_dram[o, :]
                src = bass.AP(tensor=w.tensor, offset=w.offset, ap=[[T, P], [1, T + 2]])
                sp.dma_start(words[o][:, :], src).then_inc(s_words, 16)

        @block.gpsimd
        def _(pool):
            nc.gpsimd.memset(upper[:, :], 1.0).then_inc(s_upper, 1)
            pool.wait_ge(s_upper, 1)
            nc.gpsimd.affine_select(out=upper[:, :], in_=upper[:, :], compare_op=ALU.is_gt, fill=0.0,
                                    base=0, pattern=[[1, P]], channel_multiplier=-1).then_inc(s_upper, 1)
            pool.wait_ge(s_ids, 2)
            fetch_records(nc, m, pool, BY_DST, records, fetch)

        @block.vector
        def _(dve):
            v = nc.vector
            steps = Steps(dve, s_step)
            dve.wait_ge(s_words, 32)
            for o in (BY_DST, BY_SRC):
                code = m.code[o]
                steps.inc(v.tensor_scalar(m.edge_no[o][:, :], words[o][:, 1:T + 1], 2 ** ID_BITS - 1, None, ALU.bitwise_and))
                steps.link(v.tensor_scalar(code_i[:, :], words[o][:, :], ID_BITS, None, ALU.logical_shift_right))
                steps.inc(v.tensor_scalar(edge_f[:, :], m.edge_no[o][:, :], float(E - 1), None, ALU.min))
                steps.link(v.tensor_copy(code[:, :], code_i[:, :]))
                v.tensor_copy(m.edge_no[o][:, :], edge_f[:, :]).then_inc(s_ids, 1)
                dve.wait_ge(s_ids, o + 1)
                steps.link(v.tensor_scalar(row_f[:, :], code[:, 1:T + 1], float(2 ** 16), float(-(2 ** 16 + HALF)), ALU.is_ge, ALU.mult))
                steps.link(v.scalar_tensor_tensor(node_f[:, :], code[:, 1:T + 1], float(HALF - CODE), row_f[:, :], ALU.add, ALU.add))
                own = m.dst_idx[o] if o == BY_DST else m.src_idx[o]
                steps.inc(v.tensor_scalar(own[:, :], node_f[:, :], float(N - 1), None, ALU.min))
                steps.inc(v.tensor_tensor(m.same[o][:, :], code[:, 0:T + 1], code[:, 1:T + 2], ALU.is_equal))
                steps.inc(v.tensor_tensor(m.tail[o][:, :, 0], code[:, 1:T + 1], code[:, 2:T + 2], ALU.not_equal))
                steps.inc(v.tensor_scalar(not_pad[:, :], code[:, 1:T + 1], float(PAD_CODE), None, ALU.not_equal))
                steps.inc(v.tensor_scalar(m.first[o][:, :, 0], code[:, 1:T + 1], code[:, 1:2], None, ALU.is_equal))
                steps.inc(v.tensor_scalar(m.last[o][:, :, 0], code[:, 1:T + 1], code[:, T:T + 1], None, ALU.is_equal))
                steps.inc(v.tensor_scalar(end_rows[:, :], m.ident[:, :], 0.0, code[:, 1:2], ALU.mult, ALU.add))
                steps.wait()
                v.tensor_tensor(m.tail[o][:, :, 0], m.tail[o][:, :, 0], not_pad[:, :], ALU.mult).then_inc(s_row, 1)
                dve.wait_ge(s_row, o + 1)
                steps.link(v.tensor_scalar(row_f[:, :], m.tail[o][:, :, 0], float(-OUT_OF_RANGE), float(OUT_OF_RANGE), ALU.mult, ALU.add))
                steps.link(v.tensor_tensor(m.tail_idx[o][:, :], row_f[:, :], node_f[:, :], ALU.add))
                dve.wait_ge(s_rowt, o + 1)
                if o == 0:
                    dve.wait_ge(s_upper, 2)
                steps.link(v.tensor_scalar(m.before[o][:, :], row_end[:, :], code[:, T:T + 1], None, ALU.is_equal))
                v.tensor_tensor(m.before[o][:, :], m.before[o][:, :], upper[:, :], ALU.mult).then_inc(s_bef, 1)
                dve.wait_ge(s_beft, o + 1)
                steps.link(v.tensor_copy(m.after[o][:, :], before_t[:, :]))
            steps.link(v.memset(ones_row[:, :], 1.0))
            v.tensor_tensor_scan(count[:, :], m.same[BY_SRC][:, 0:T], ones_row[:, :], 0.0, ALU.mult, ALU.add).then_inc(s_count, 1)
            dve.wait_ge(s_counted, 1)
            v.scalar_tensor_tensor(count[:, :], m.first[BY_SRC][:, :, 0], count_ps[:, 0:1], count[:, :], ALU.mult,
                                   ALU.add).then_inc(s_count, 1)
            dve.wait_ge(s_root, 1)
            steps.link(v.reciprocal(m.dinv_src[:, :, 0], root[:, :]))

        @block.scalar
        def _(act):
            act.wait_ge(s_count, 2)
            nc.scalar.activation(root[:, :], count[:, :], ACT.Sqrt).then_inc(s_root, 1)

        @block.tensor
        def _(pe):
            for o in (BY_DST, BY_SRC):
                pe.wait_ge(s_row, o + 1)
                nc.tensor.transpose(row_end[:, :], end_rows[:, :], m.ident[:, :]).then_inc(s_rowt, 1)
                pe.wait_ge(s_bef, o + 1)
                nc.tensor.transpose(before_t[:, :], m.before[o][:, :], m.ident[:, :]).then_inc(s_beft, 1)
            pe.wait_ge(s_count, 1)
            nc.tensor.matmul(count_ps[:, 0:1], m.before[BY_SRC][:, :], count[:, T - 1:T], start=True, stop=True).then_inc(s_counted, 1)


def load_weights(nc, m, w):
    with ExitStack() as ctx:
        def sb(name, shape, dt=F32):
            return ctx.enter_context(nc.sbuf_tensor(name, shape, dt))

        wv, mix, bv = sb("wv", [D, D]), sb("mix", [D, D]), sb("bv", [D, 1])
        w3t, a_src, a_dst = sb("w3t", [D, D]), sb("a_src", [D, 1]), sb("a_dst", [D, 1])
        a_wide = sb("a_wide", [D, 1, P])
        base = sb("base", [D, D])
        spline = sb("spline", [D, SPLINES, D])
        scaled = [sb(f"scaled{i}", [D, D]) for i in (0, 1)]
        prod = ctx.enter_context(nc.psum_tensor("weight_products", [P, 4 * D], F32))
        s_zero, s_in, s_step, s_ones, s_wide, s_prod, s_mix = (
            m.sem(n) for n in ("mix_zero", "weights_in", "weight_step", "ones_made", "a_wide_made", "products", "mix_in"))
        block = ctx.enter_context(nc.Block())
        rows = [(m.b0, w["b0"]), (m.b2, w["b2"]), (m.rel, w["rel"])]
        whole = [(m.w0, w["w0"]), (m.wq, w["wq"]), (m.w2, w["w2"]), (wv, w["wv"]), (w3t, w["w3t"])]
        n_in = len(rows) + len(whole) + 10

        @block.sync
        def _(sp):
            for out, row in rows:
                sp.dma_start(out[:, 0, :], row.partition_broadcast(P)).then_inc(s_in, 16)
            for out, mat in whole:
                sp.dma_start(out[:, :], mat).then_inc(s_in, 16)
            sp.dma_start(m.wkv[:, 0:D], w["wk"]).then_inc(s_in, 16)
            sp.dma_start(m.bias_kvq[0:1, 0:D], w["bk"].rearrange("(a d) -> a d", a=1)).then_inc(s_in, 16)
            sp.dma_start(m.bias_kvq[0:1, 2 * D:3 * D], w["bq"].rearrange("(a d) -> a d", a=1)).then_inc(s_in, 16)
            sp.dma_start(bv[:, :], w["bv"].rearrange("(d a) -> d a", a=1)).then_inc(s_in, 16)
            sp.dma_start(a_src[:, :], w["a"][0:D, :]).then_inc(s_in, 16)
            sp.dma_start(a_dst[:, :], w["a"][D:2 * D, :]).then_inc(s_in, 16)
            sp.dma_start(base[:, :], w["base"]).then_inc(s_in, 16)
            sp.dma_start(spline[:, :, :], w["spline"].rearrange("c i o -> i c o")).then_inc(s_in, 16)
            sp.dma_start(m.gamma_beta[0:1, 0:D], w["gamma"].rearrange("(a d) -> a d", a=1)).then_inc(s_in, 16)
            sp.dma_start(m.gamma_beta[0:1, D:2 * D], w["beta"].rearrange("(a d) -> a d", a=1)).then_inc(s_in, 16)
            sp.wait_ge(s_zero, 1)
            for h in range(H):
                sp.dma_start(mix[h * DK:(h + 1) * DK, h * DK:(h + 1) * DK], w["rel_msg"][h, :, :]).then_inc(s_mix, 16)
            sp.wait_ge(s_mix, 16 * H)

        @block.gpsimd
        def _(pool):
            nc.gpsimd.memset(mix[:, :], 0.0).then_inc(s_zero, 1)
            nc.gpsimd.memset(m.ones[:, :], 1.0).then_inc(s_ones, 1)
            nc.gpsimd.memset(m.epsilon[:, :], EPS).then_inc(s_ones, 1)

        @block.tensor
        def _(pe):
            pe.wait_ge(s_in, 16 * n_in)
            pe.wait_ge(s_mix, 16 * H)
            pe.wait_ge(s_wide, 1)
            nc.tensor.matmul(prod[:, 0:D], wv[:, :], mix[:, :], start=True, stop=True)
            nc.tensor.matmul(prod[0:1, D:2 * D], bv[:, 0:1], mix[:, :], start=True, stop=True)
            nc.tensor.matmul(prod[:, 2 * D:3 * D], a_wide[:, 0, :], w3t[:, :], start=True, stop=True)
            nc.tensor.matmul(prod[:, 3 * D:3 * D + 1], w3t[:, :], a_dst[:, 0:1], start=True, stop=True).then_inc(s_prod, 1)

        @block.vector
        def _(dve):
            v = nc.vector
            steps = Steps(dve, s_step)
            dve.wait_ge(s_in, 16 * n_in)
            dve.wait_ge(s_ones, 2)
            v.tensor_scalar(a_wide[:, 0, :], m.ones[:, :], a_src[:, 0:1], None, ALU.mult).then_inc(s_wide, 1)
            steps.inc(v.tensor_scalar(m.rb0[:, :, :], m.b0[:, :, :], 0.0, None, ALU.max))
            steps.inc(v.tensor_scalar(m.rb2[:, :, :], m.b2[:, :, :], 0.0, None, ALU.max))
            steps.inc(v.tensor_scalar(m.w_kan[:, 0, :], base[:, :], 0.5, None, ALU.mult))
            choose = (1, -4, 6, -4, 1)
            for n in range(KNOTS):
                knot = n + 6
                terms = [(j, choose[knot - j] / 6.0 / GRID_STEP ** 3 * (-1 if n < DVE_KNOTS else 1)) for j in range(max(0, knot - 4), min(SPLINES, knot + 1))]
                for at, (j, c) in enumerate(terms):
                    if at == 0:
                        steps.link(v.tensor_scalar(m.w_kan[:, 1 + n, :], spline[:, j, :], c, None, ALU.mult))
                    else:
                        steps.link(v.scalar_tensor_tensor(m.w_kan[:, 1 + n, :], spline[:, j, :], c, m.w_kan[:, 1 + n, :],
                                                          ALU.mult, ALU.add))
            dve.wait_ge(s_prod, 1)
            steps.inc(v.tensor_copy(m.wkv[:, D:2 * D], prod[:, 0:D]))
            steps.inc(v.tensor_copy(m.bias_kvq[0:1, D:2 * D], prod[0:1, D:2 * D]))
            steps.inc(v.tensor_copy(m.to_src[:, 0, :], prod[:, 2 * D:3 * D]))
            steps.inc(v.tensor_copy(m.to_dst[:, :], prod[:, 3 * D:3 * D + 1]))
            steps.wait()


def stage_columns(pool, nc, m, stage, idx, i, slot, s_stage, count):
    nc.gpsimd.tensor_copy(stage[slot][:, :], idx[:, group(i, slot)]).then_inc(s_stage, 1)
    hold(pool, m.passed, s_stage, count)


def gather(pool, out, table, stage, sem):
    for k in range(G):
        pool.indirect_dma_start(out[:, k, :], None, table,
                                bass.IndirectOffsetOnAxis(ap=stage[:, k:k + 1], axis=0)).then_inc(sem, 16)


def scatter(pool, table, rows, stage, sem):
    for k in range(G):
        pool.indirect_dma_start(table, bass.IndirectOffsetOnAxis(ap=stage[:, k:k + 1], axis=0), rows[:, k, :], None,
                                bounds_check=N - 1, oob_is_err=False).then_inc(sem, 16)


def row_stats(v, m, steps, rows, n, stats, mean_var):
    for k in range(n):
        steps.inc(v.bn_stats(stats[:, k, :], rows[:, k, :]))
    steps.hold(m.passed)
    for k in range(n - 1):
        steps.inc(v.bn_aggr(mean_var[:, k, :], stats[:, k, :]))
    return v.bn_aggr(mean_var[:, n - 1, :], stats[:, n - 1, :])


def norm_rows(v, steps, mean_var, work, rstd, shift):
    half, y = work[:, 0, :], rstd
    steps.inc(v.tensor_scalar(half, mean_var[:, :, 1], -0.5, -0.5 * EPS, ALU.mult, ALU.add))
    steps.link(v.tensor_scalar(y, mean_var[:, :, 1], EPS, None, ALU.add))
    steps.link(v.tensor_scalar(y.bitcast(I32), y.bitcast(I32), 1, None, ALU.logical_shift_right))
    steps.link(v.tensor_scalar(y.bitcast(I32), y.bitcast(I32), -1.0, float(0x5f3759df), ALU.mult, ALU.add))
    for _ in range(3):
        steps.link(v.tensor_tensor(work[:, 1, :], y, y, ALU.mult))
        steps.link(v.tensor_tensor(work[:, 1, :], work[:, 1, :], half, ALU.mult))
        steps.link(v.scalar_tensor_tensor(y, work[:, 1, :], 1.5, y, ALU.add, ALU.mult))
    return v.scalar_tensor_tensor(shift, mean_var[:, :, 0], -1.0, y, ALU.mult, ALU.mult)


def sum_source_rows(nc, m, x):
    with ExitStack() as ctx:
        def sb(name, shape, dt=F32):
            return ctx.enter_context(nc.sbuf_tensor(name, shape, dt))

        o = BY_DST
        stage = [sb(f"l0_stage{i}", [P, G], I32) for i in (0, 1)]
        got = [sb(f"l0_got{i}", [P, G, D]) for i in (0, 1)]
        h = [sb(f"l0_h{i}", [P, G, D]) for i in (0, 1)]
        same_g = [sb(f"l0_same{i}", [P, G]) for i in (0, 1)]
        stats, mv, rstd, shift = sb("l0_stats", [P, G, 6]), [sb(f"l0_mv{i}", [P, G, 2]) for i in (0, 1)], \
            [sb(f"l0_rstd{i}", [P, G, 1]) for i in (0, 1)], [sb(f"l0_shift{i}", [P, G, 1]) for i in (0, 1)]
        work = sb("l0_work", [P, 2, G])
        s_stage, s_step, s_norm, s_h, s_sum, s_kept = (
            m.sem("l0_" + n) for n in ("staged", "step", "norm", "h", "summed", "kept"))
        s_got = [m.lasting_sem(f"l0_rows_in{i}") for i in (0, 1)]
        s_stored = [m.sem(f"l0_rows_stored{i}") for i in (0, 1)]
        block = ctx.enter_context(nc.Block())

        @block.gpsimd
        def _(pool):
            def body(i, first):
                for slot in (0, 1):
                    g = i * 2 + slot
                    if not first:
                        hold(pool, m.passed, s_h, g - 1)
                        hold(pool, m.passed, s_stored[slot], i * 16)
                    stage_columns(pool, nc, m, stage, m.src_idx[o], i, slot, s_stage, g + 1)
                    gather(pool, got[slot], x, stage[slot], s_got[slot])
            turns(pool, body)

        @block.sync
        def _(sp):
            with sp.Fori(0, PAIRS) as i:
                for slot in (0, 1):
                    sp.wait_ge(s_got[slot], i * (16 * G) + 16 * G)
                    sp.dma_start(chunk(m.x_src, i, slot), got[slot][:, :, :]).then_inc(s_stored[slot], 16)
            for slot in (0, 1):
                sp.wait_ge(s_stored[slot], 16 * PAIRS)

        @block.scalar
        def _(act):
            def body(i, first):
                for slot in (0, 1):
                    g = i * 2 + slot
                    act.wait_ge(s_norm, g + 1)
                    if not first:
                        act.wait_ge(s_kept, g - 1)
                    for k in range(G):
                        ins = nc.scalar.activation(h[slot][:, k, :], got[slot][:, k, :], ACT.Relu,
                                                   bias=shift[slot][:, k, :], scale=rstd[slot][:, k, :])
                    ins.then_inc(s_h, 1)
                    act.wait_ge(s_sum, g + 1)
                    nc.scalar.copy(m.rows[:, group(i, slot), :], h[slot][:, :, :]).then_inc(s_kept, 1)
            turns(act, body)

        @block.vector
        def _(dve):
            v = nc.vector
            steps = Steps(dve, s_step)

            def body(i, first):
                for slot in (0, 1):
                    g = i * 2 + slot
                    dve.wait_ge(s_got[slot], i * (16 * G) + 16 * G)
                    steps.link(row_stats(v, m, steps, got[slot], G, stats, mv[slot]))
                    steps.inc(v.tensor_copy(same_g[slot][:, :], m.same[o][:, group(i, slot)]))
                    norm_rows(v, steps, mv[slot], work, rstd[slot][:, :, 0], shift[slot][:, :, 0]).then_inc(s_norm, 1)
                    dve.wait_ge(s_h, g + 1)
                    for k in range(G):
                        if first and slot == 0 and k == 0:
                            continue
                        before = h[slot][:, k - 1, :] if k else h[1 - slot][:, G - 1, :]
                        ins = v.scalar_tensor_tensor(h[slot][:, k, :], before, same_g[slot][:, k:k + 1], h[slot][:, k, :],
                                                     ALU.mult, ALU.add)
                        if k < G - 1:
                            steps.link(ins)
                        else:
                            ins.then_inc(s_sum, 1)
                            dve.wait_ge(s_sum, g + 1)
            turns(dve, body, steps, 2 * (3 * G + 13))


def value_slots(m, ctx, name):
    stage = [ctx.enter_context(m.nc.sbuf_tensor(f"{name}numbers{i}", [P, G], I32)) for i in (0, 1)]
    value = [ctx.enter_context(m.nc.sbuf_tensor(f"{name}value{i}", [P, G], F32)) for i in (0, 1)]
    return stage, value, m.sem(name + "staged"), m.sem(name + "copied"), [m.lasting_sem(f"{name}moved{i}") for i in (0, 1)]


def put_dinv(nc, m, pool, i, slot, first, slots):
    stage, value, s_stage, s_value, s_moved = slots
    g = i * 2 + slot
    if not first:
        hold(pool, m.passed, s_moved[slot], i * (16 * G))
    nc.gpsimd.tensor_copy(value[slot][:, :], m.dinv_src[:, group(i, slot), 0]).then_inc(s_value, 1)
    hold(pool, m.passed, s_value, g + 1)
    stage_columns(pool, nc, m, stage, m.tail_idx[BY_SRC], i, slot, s_stage, g + 1)
    for k in range(G):
        pool.indirect_dma_start(m.dinv_table, bass.IndirectOffsetOnAxis(ap=stage[slot][:, k:k + 1], axis=0),
                                value[slot][:, k:k + 1], None, bounds_check=N - 1, oob_is_err=False).then_inc(s_moved[slot], 16)


def get_dinv(nc, m, pool, slots):
    stage, value, s_stage, s_copied, s_moved = slots

    def body(i, first):
        for slot in (0, 1):
            g = i * 2 + slot
            if not first:
                hold(pool, m.passed, s_copied, g - 1)
            stage_columns(pool, nc, m, stage, m.dst_idx[BY_SRC], i, slot, s_stage, g + 1)
            for k in range(G):
                pool.indirect_dma_start(value[slot][:, k:k + 1], None, m.dinv_table,
                                        bass.IndirectOffsetOnAxis(ap=stage[slot][:, k:k + 1], axis=0)).then_inc(s_moved[slot], 16)
            if not (first and slot == 0):
                take(i - (1 - slot), 1 - slot)

    def take(i, slot):
        hold(pool, m.passed, s_moved[slot], i * (16 * G) + 16 * G)
        nc.gpsimd.tensor_copy(m.dinv_dst[:, group(i, slot), 0], value[slot][:, :]).then_inc(s_copied, 1)
    turns(pool, body)
    take(PAIRS - 1, 1)
    pool.wait_ge(s_copied, NG)


def transform_sums0(nc, m, x):
    with ExitStack() as ctx:
        def sb(nm, shape, dt=F32):
            return ctx.enter_context(nc.sbuf_tensor("t0_" + nm, shape, dt))

        def two(nm, shape, dt=F32):
            return [sb(f"{nm}{i}", shape, dt) for i in (0, 1)]

        def psum(nm, cols):
            return ctx.enter_context(nc.psum_tensor("t0_" + nm, [P, cols], F32))

        def sem(nm):
            return m.sem("t0_" + nm)

        o = BY_DST
        numbers, dst_numbers = two("numbers", [P, G], I32), two("dst_numbers", [P, G], I32)
        u, d, sq, xd, uts = two("u", [P, G, D]), two("d", [P, G, D]), two("sq", [P, G, D]), two("xd", [P, G, D]), two("uts", [P, G * D])
        tmp, zero_row, totals = sb("tmp", [P, G, D]), sb("zero_row", [1, 2 * D]), m.totals
        ut, z, carry_ps, sums_ps = [psum(f"ut{i}", 8 * D) for i in (0, 1)], psum("z", 8 * D), psum("carry", 512), psum("sums", 512)
        s_numbers, s_dst_numbers, s_step, s_carry, s_u, s_turned, s_uts, s_z, s_d, s_kept, s_square, s_sums, s_zero_row = (
            sem(n) for n in ("numbers_staged", "dst_numbers_staged", "step", "carry_made", "u_made", "u_turned", "uts_made",
                             "z_made", "d_made", "d_kept", "squared", "summed", "zero_row_made"))
        s_scat = [m.lasting_sem(f"t0_scattered{i}") for i in (0, 1)]
        s_xd, s_stored = [m.lasting_sem(f"t0_xd_in{i}") for i in (0, 1)], [sem(f"xd_stored{i}") for i in (0, 1)]
        block = ctx.enter_context(nc.Block())

        @block.gpsimd
        def _(pool):
            def body(i, first):
                for slot in (0, 1):
                    g = i * 2 + slot
                    if not first:
                        hold(pool, m.passed, s_stored[slot], i * 16)
                    stage_columns(pool, nc, m, dst_numbers, m.dst_idx[o], i, slot, s_dst_numbers, g + 1)
                    gather(pool, xd[slot], x, dst_numbers[slot], s_xd[slot])
                    if not first:
                        hold(pool, m.passed, s_scat[slot], i * (16 * G))
                    stage_columns(pool, nc, m, numbers, m.tail_idx[o], i, slot, s_numbers, g + 1)
                    hold(pool, m.passed, s_d, g + 1)
                    scatter(pool, m.h0_table, d[slot], numbers[slot], s_scat[slot])
            turns(pool, body)
            for slot in (0, 1):
                pool.wait_ge(s_scat[slot], 16 * G * PAIRS)

        @block.sync
        def _(sp):
            with sp.Fori(0, PAIRS) as i:
                for slot in (0, 1):
                    sp.wait_ge(s_xd[slot], i * (16 * G) + 16 * G)
                    sp.dma_start(chunk(m.x_dst, i, slot), xd[slot][:, :, :]).then_inc(s_stored[slot], 16)
            for slot in (0, 1):
                sp.wait_ge(s_stored[slot], 16 * PAIRS)

        @block.tensor
        def _(pe):
            nc.tensor.matmul(carry_ps[:, 0:D], m.before[o][:, :], m.rows[:, T - 1, :], start=True, stop=True).then_inc(s_carry, 1)
            pe.wait_ge(s_zero_row, 1)
            nc.tensor.matmul(sums_ps[0:1, 0:2 * D], m.ones[0:1, 0:1], zero_row[0:1, :], start=True, stop=False)

            def body(i, first):
                for slot in (0, 1):
                    g = i * 2 + slot
                    pe.wait_ge(s_u, g + 1)
                    for k in range(G):
                        ins = nc.tensor.transpose(ut[slot][:, k * D:(k + 1) * D], u[slot][:, k, :], m.ident[:, :])
                    ins.then_inc(s_turned, 1)
                    pe.wait_ge(s_uts, g + 1)
                    if not (first and slot == 0):
                        pe.wait_ge(s_d, g)
                    for k in range(G):
                        ins = nc.tensor.matmul(z[:, k * D:(k + 1) * D], uts[slot][:, k * D:(k + 1) * D], m.w0[:, :],
                                               start=True, stop=True)
                    ins.then_inc(s_z, 1)
                    pe.wait_ge(s_square, g + 1)
                    for k in range(G):
                        nc.tensor.matmul(sums_ps[0:1, 0:D], m.ones[:, 0:1], d[slot][:, k, :], start=False, stop=False)
                        ins = nc.tensor.matmul(sums_ps[0:1, D:2 * D], m.ones[:, 0:1], sq[slot][:, k, :], start=False, stop=False)
                    ins.then_inc(s_sums, 1)
            turns(pe, body)
            nc.tensor.matmul(sums_ps[0:1, 0:2 * D], m.ones[0:1, 0:1], zero_row[0:1, :], start=False, stop=True).then_inc(s_sums, 1)

        @block.scalar
        def _(act):
            def body(i, first):
                for slot in (0, 1):
                    g = i * 2 + slot
                    act.wait_ge(s_turned, g + 1)
                    nc.scalar.activation(uts[slot][:, :], ut[slot][:, 0:G * D], ACT.Copy).then_inc(s_uts, 1)
                    act.wait_ge(s_d, g + 1)
                    if not first:
                        act.wait_ge(s_sums, g - 1)
                    nc.scalar.activation(sq[slot][:, :, :], d[slot][:, :, :], ACT.Square).then_inc(s_square, 1)
                    nc.scalar.activation(m.rows[:, group(i, slot), :], d[slot][:, :, :], ACT.Copy).then_inc(s_kept, 1)
            turns(act, body)

        @block.vector
        def _(dve):
            v = nc.vector
            steps = Steps(dve, s_step)
            v.memset(zero_row[:, :], 0.0).then_inc(s_zero_row, 1)
            dve.wait_ge(s_carry, 1)
            steps.link(v.tensor_copy(m.carry[:, 0, :], carry_ps[:, 0:D]))

            def body(i, first):
                for slot in (0, 1):
                    g = i * 2 + slot
                    steps.link(v.tensor_tensor(tmp[:, :, :], m.carry[:, :, :].to_broadcast([P, G, D]),
                                               m.first[o][:, group(i, slot), :].to_broadcast([P, G, D]), ALU.mult))
                    v.tensor_tensor(u[slot][:, :, :], tmp[:, :, :], m.rows[:, group(i, slot), :], ALU.add).then_inc(s_u, 1)
                    dve.wait_ge(s_u, g + 1)
                    dve.wait_ge(s_z, g + 1)
                    z3 = z[:, 0:G * D].rearrange("p (g d) -> p g d", d=D)
                    steps.link(v.tensor_tensor(tmp[:, :, :], z3, m.b0[:, :, :].to_broadcast([P, G, D]), ALU.add))
                    steps.link(v.scalar_tensor_tensor(tmp[:, :, :], tmp[:, :, :], 0.0, m.rb0[:, :, :].to_broadcast([P, G, D]),
                                                      ALU.max, ALU.subtract))
                    if not first:
                        dve.wait_ge(s_scat[slot], i * (16 * G))
                        dve.wait_ge(s_sums, g - 1)
                        dve.wait_ge(s_kept, g - 1)
                    v.tensor_tensor(d[slot][:, :, :], tmp[:, :, :], m.tail[o][:, group(i, slot), :].to_broadcast([P, G, D]),
                                    ALU.mult).then_inc(s_d, 1)
                    dve.wait_ge(s_d, g + 1)
            turns(dve, body, steps, 2 * 3)
            dve.wait_ge(s_sums, NG + 1)
            steps.link(v.tensor_scalar(m.totals[0:1, 0:2 * D], sums_ps[0:1, 0:2 * D], 1.0 / N, None, ALU.mult))


def batch_norm_rows(nc, m):
    with ExitStack() as ctx:
        work = [ctx.enter_context(nc.sbuf_tensor(f"bn_work{i}", [1, D], F32)) for i in range(4)]
        both = ctx.enter_context(nc.sbuf_tensor("bn_both", [1, 2 * D], F32))
        wide = ctx.enter_context(nc.psum_tensor("bn_wide", [P, 2 * D], F32))
        s_step, s_var, s_std, s_both, s_wide = (m.sem("bn_" + n) for n in ("step", "var", "std", "both", "wide"))
        mean, square = m.totals[0:1, 0:D], m.totals[0:1, D:2 * D]
        block = ctx.enter_context(nc.Block())

        @block.vector
        def _(dve):
            v = nc.vector
            steps = Steps(dve, s_step)
            steps.link(v.tensor_tensor(work[0][:, :], mean, mean, ALU.mult))
            steps.link(v.tensor_tensor(work[1][:, :], square, work[0][:, :], ALU.subtract))
            v.tensor_scalar(work[1][:, :], work[1][:, :], 0.0, None, ALU.max).then_inc(s_var, 1)
            dve.wait_ge(s_std, 1)
            steps.link(v.reciprocal(work[3][:, :], work[2][:, :]))
            steps.link(v.tensor_tensor(both[:, 0:D], work[3][:, :], m.gamma_beta[0:1, 0:D], ALU.mult))
            steps.link(v.tensor_tensor(work[0][:, :], both[:, 0:D], mean, ALU.mult))
            v.tensor_tensor(both[:, D:2 * D], m.gamma_beta[0:1, D:2 * D], work[0][:, :], ALU.subtract).then_inc(s_both, 1)
            dve.wait_ge(s_wide, 1)
            steps.inc(v.tensor_copy(m.scale0[:, 0, :], wide[:, 0:D]))
            steps.inc(v.tensor_copy(m.shift0[:, 0, :], wide[:, D:2 * D]))
            steps.wait()

        @block.scalar
        def _(act):
            act.wait_ge(s_var, 1)
            nc.scalar.activation(work[2][:, :], work[1][:, :], ACT.Sqrt, bias=m.epsilon[0:1, 0:1]).then_inc(s_std, 1)

        @block.tensor
        def _(pe):
            pe.wait_ge(s_both, 1)
            nc.tensor.matmul(wide[:, :], m.ones[0:1, 0:P], both[0:1, :], start=True, stop=True).then_inc(s_wide, 1)


def dense_pass(nc, m, x, out, records):
    with ExitStack() as ctx:
        def sb(nm, shape, dt=F32):
            return ctx.enter_context(nc.sbuf_tensor("dense_" + nm, shape, dt))

        def sem(nm):
            return m.sem("dense_" + nm)

        C = BULK_ROWS * D
        xin, xout = [sb(f"in{i}", [P, BULK_ROWS, D]) for i in (0, 1)], [sb(f"out{i}", [P, BULK_ROWS, D]) for i in (0, 1)]
        rest_in, rest_out = sb("rest_in", [N - BULK_MAIN, D]), sb("rest_out", [N - BULK_MAIN, D])
        base = sb("base", [P, 1, D])
        tmp = sb("tmp", [P, G, D])
        carry_ps = ctx.enter_context(nc.psum_tensor("dense_carry", [P, 512], F32))
        s_in, s_out = [sem(f"rows_in{i}") for i in (0, 1)], [sem(f"rows_out{i}") for i in (0, 1)]
        s_sum, s_step, s_rest, s_rest_in, s_rest_out, s_spread, s_carry = (
            sem(n) for n in ("summed", "step", "rest_summed", "rest_in", "rest_out", "spread", "carry"))
        fetch = record_slots(m, ctx, "rec1_")
        x3, out3 = (t[0:BULK_MAIN, :].rearrange("(p r) d -> p r d", p=P) for t in (x, out))
        block = ctx.enter_context(nc.Block())
        halves = BULK_STEPS // 2

        @block.sync
        def _(sp):
            sp.dma_start(rest_in[:, :], x[BULK_MAIN:N, :]).then_inc(s_rest_in, 16)
            sp.dma_start(xin[0][:, :, :], x3[:, 0:BULK_ROWS, :]).then_inc(s_in[0], 16)
            sp.dma_start(xin[1][:, :, :], x3[:, BULK_ROWS:2 * BULK_ROWS, :]).then_inc(s_in[1], 16)
            with sp.Fori(1, halves) as i:
                for slot in (0, 1):
                    sp.wait_ge(s_sum, i * 2 + (slot - 1))
                    sp.dma_start(xin[slot][:, :, :], x3[:, bass.ds((i * 2 + slot) * BULK_ROWS, BULK_ROWS), :]).then_inc(s_in[slot], 16)
            sp.wait_ge(s_sum, 2 * halves - 1)
            sp.dma_start(xin[0][:, :, :], x3[:, 2 * halves * BULK_ROWS:, :]).then_inc(s_in[0], 16)

        @block.scalar
        def _(act):
            with act.Fori(0, halves) as i:
                for slot in (0, 1):
                    act.wait_ge(s_sum, i * 2 + (slot + 1))
                    act.dma_start(out3[:, bass.ds((i * 2 + slot) * BULK_ROWS, BULK_ROWS), :], xout[slot][:, :, :]).then_inc(s_out[slot], 16)
            act.wait_ge(s_sum, 2 * halves + 1)
            act.dma_start(out3[:, 2 * halves * BULK_ROWS:, :], xout[0][:, :, :]).then_inc(s_out[0], 16)
            act.wait_ge(s_rest, 1)
            act.dma_start(out[BULK_MAIN:N, :], rest_out[:, :]).then_inc(s_rest_out, 16)
            act.wait_ge(s_out[0], 16 * (halves + 1))
            act.wait_ge(s_out[1], 16 * halves)
            act.wait_ge(s_rest_out, 16)

        @block.tensor
        def _(pe):
            pe.wait_ge(s_spread, 1)
            nc.tensor.matmul(carry_ps[:, 0:D], m.after[BY_DST][:, :], m.rows[:, 0, :], start=True, stop=True).then_inc(s_carry, 1)

        @block.gpsimd
        def _(pool):
            fetch_records(nc, m, pool, BY_SRC, records, fetch)

        @block.vector
        def _(dve):
            v = nc.vector
            steps = Steps(dve, s_step)
            steps.link(v.tensor_tensor(base[:, :, :], m.shift0[:, :, :], m.rb2[:, :, :], ALU.add))
            def add(slot):
                v.tensor_tensor(xout[slot][:, :, :], xin[slot][:, :, :], base[:, :, :].to_broadcast([P, BULK_ROWS, D]),
                                ALU.add).then_inc(s_sum, 1)

            def add_next(i, slot):
                dve.wait_ge(s_in[slot], i * 16 + 16)
                dve.wait_ge(s_out[slot], i * 16)
                add(slot)

            dve.wait_ge(s_rest_in, 16)
            v.tensor_tensor(rest_out[:, :], rest_in[:, :], base[0:N - BULK_MAIN, 0, :], ALU.add).then_inc(s_rest, 1)
            for slot in (0, 1):
                dve.wait_ge(s_in[slot], 16)
                add(slot)
            with dve.Fori(1, 1 + BACK_TURNS) as i:
                steps.base, steps.k = i * BACK_STEPS + (1 - BACK_STEPS), 0
                for slot in (0, 1):
                    add_next(i, slot)
                for k in range(BACK_STEPS):
                    later, here = (bass.ds(T - 1 - n + BACK_STEPS - k - i * BACK_STEPS, 1) for n in (0, 1))
                    steps.inc(v.scalar_tensor_tensor(m.rows[:, here, :], m.rows[:, later, :], m.same[BY_DST][:, later],
                                                     m.rows[:, here, :], ALU.mult, ALU.add))
                    steps.hold(m.passed)
            steps.base, steps.k = T, 0
            v.nop().then_inc(s_spread, 1)
            dve.wait_ge(s_carry, 1)
            steps.link(v.tensor_copy(m.carry[:, 0, :], carry_ps[:, 0:D]))
            with dve.Fori(1 + BACK_TURNS, 1 + BACK_TURNS + PAIRS) as i:
                steps.base, steps.k = i * 4 + (1 + T - 4 * (1 + BACK_TURNS)), 0
                for slot in (0, 1):
                    add_next(i, slot)
                    here = bass.ds((i * 2 + (slot - 2 * (1 + BACK_TURNS))) * G, G)
                    steps.link(v.tensor_tensor(tmp[:, :, :], m.carry[:, :, :].to_broadcast([P, G, D]),
                                               m.last[BY_DST][:, here, :].to_broadcast([P, G, D]), ALU.mult))
                    steps.inc(v.tensor_tensor(m.rows[:, here, :], tmp[:, :, :], m.rows[:, here, :], ALU.add))
                    steps.hold(m.passed)
            with dve.Fori(1 + BACK_TURNS + PAIRS, halves) as i:
                for slot in (0, 1):
                    add_next(i, slot)
            dve.wait_ge(s_in[0], 16 * (halves + 1))
            dve.wait_ge(s_out[0], 16 * halves)
            add(0)


def attend(nc, m, scores):
    with ExitStack() as ctx:
        def sb(nm, shape, dt=F32):
            return ctx.enter_context(nc.sbuf_tensor("at_" + nm, shape, dt))

        def two(nm, shape, dt=F32):
            return [sb(f"{nm}{i}", shape, dt) for i in (0, 1)]

        def sem(nm):
            return m.sem("at_" + nm)

        o = BY_DST
        numbers = two("numbers", [P, G], I32)
        hg, xs, xd = two("hg", [P, G, D]), two("xs", [P, G, D]), two("xd", [P, G, D])
        h = sb("h", [P, 2 * G, D])
        ht = sb("ht", [P, 2, G * D])
        tmp, qk = sb("tmp", [P, G, D]), sb("qk", [P, G, D])
        stats, mv, rstd, shift = (sb(n, [P, 2 * G, w]) for n, w in (("stats", 6), ("mv", 2), ("rstd", 1), ("shift", 1)))
        work = sb("work", [P, 2, 2 * G])
        turned = ctx.enter_context(nc.psum_tensor("at_turned", [P, 8 * D], F32))
        key = ctx.enter_context(nc.psum_tensor("at_key", [P, 8, D], F32))
        value = ctx.enter_context(nc.psum_tensor("at_value", [P, 8, D], F32))
        q = ctx.enter_context(nc.psum_tensor("at_q", [P, 8, D], F32))
        s_num, s_step, s_x1, s_norm, s_h, s_turned, s_ht, s_kvq, s_used, s_val = (
            sem(n) for n in ("numbers_staged", "step", "x1_made", "norm", "h_made", "h_turned", "ht_made",
                             "kvq_made", "kvq_used", "values_kept"))
        s_hg = [m.lasting_sem(f"at_hg_in{i}") for i in (0, 1)]
        dinv = value_slots(m, ctx, "dinv0_")
        zero_rows = N // P // NG
        zeros = sb("zeros", [P, zero_rows * D])
        zero_table = m.h2_table[0:BULK_MAIN, :].rearrange("(p r) d -> p (r d)", p=P)
        s_zero, s_zeroed = sem("zeros_made"), sem("table_zeroed")
        s_xs, s_xd, s_x1d = ([sem(f"{n}{i}") for i in (0, 1)] for n in ("xs_in", "xd_in", "x1d_stored"))
        block = ctx.enter_context(nc.Block())

        @block.gpsimd
        def _(pool):
            nc.gpsimd.memset(zeros[:, :], 0.0).then_inc(s_zero, 1)

            def body(i, first):
                for slot in (0, 1):
                    g = i * 2 + slot
                    if not first:
                        hold(pool, m.passed, s_h, g - 1)
                    stage_columns(pool, nc, m, numbers, m.src_idx[o], i, slot, s_num, g + 1)
                    gather(pool, hg[slot], m.h0_table, numbers[slot], s_hg[slot])
                    put_dinv(nc, m, pool, i, slot, first, dinv)
            turns(pool, body)
            for slot in (0, 1):
                pool.wait_ge(dinv[-1][slot], 16 * G * PAIRS)

        @block.sync
        def _(sp):
            def body(i, first):
                for slot in (0, 1):
                    g = i * 2 + slot
                    if not first:
                        hold(sp, m.passed, s_h, g - 1)
                        hold(sp, m.passed, s_x1d[slot], i * 16)
                    sp.dma_start(xs[slot][:, :, :], chunk(m.x_src, i, slot)).then_inc(s_xs[slot], 16)
                    sp.dma_start(xd[slot][:, :, :], chunk(m.x_dst, i, slot)).then_inc(s_xd[slot], 16)
                    sp.dma_start(zero_table[:, bass.ds(g * (zero_rows * D), zero_rows * D)], zeros[:, :]).then_inc(s_zeroed, 16)
                    if not (first and slot == 0):
                        store(i - (1 - slot), 1 - slot, g)

            def store(i, slot, count):
                sp.wait_ge(s_x1, count)
                sp.dma_start(chunk(m.x1_dst, i, slot), xd[slot][:, :, :]).then_inc(s_x1d[slot], 16)
            sp.wait_ge(s_zero, 1)
            turns(sp, body)
            store(PAIRS - 1, 1, NG)
            sp.dma_start(zero_table[:, NG * zero_rows * D:], zeros[:, 0:(N // P - NG * zero_rows) * D]).then_inc(s_zeroed, 16)
            sp.dma_start(m.h2_table[BULK_MAIN:N, :], zeros[0:N - BULK_MAIN, 0:D]).then_inc(s_zeroed, 16)
            sp.wait_ge(s_zeroed, 16 * (NG + 2))
            for slot in (0, 1):
                sp.wait_ge(s_x1d[slot], 16 * PAIRS)

        @block.vector
        def _(dve):
            v = nc.vector
            steps = Steps(dve, s_step)
            scale, shift0 = (r[:, :, :].to_broadcast([P, G, D]) for r in (m.scale0, m.shift0))

            def normalise(i, slot, first):
                g = i * 2 + slot
                dve.wait_ge(s_hg[slot], i * (16 * G) + 16 * G)
                steps.inc(v.tensor_tensor(hg[slot][:, :, :], hg[slot][:, :, :], scale, ALU.mult))
                steps.link(v.tensor_tensor(tmp[:, :, :], m.rows[:, group(i, slot), :], scale, ALU.mult))
                dve.wait_ge(s_xs[slot], i * 16 + 16)
                dve.wait_ge(s_xd[slot], i * 16 + 16)
                steps.inc(v.tensor_tensor(hg[slot][:, :, :], hg[slot][:, :, :], xs[slot][:, :, :], ALU.add))
                steps.link(v.tensor_tensor(tmp[:, :, :], tmp[:, :, :], xd[slot][:, :, :], ALU.add))
                steps.link(v.tensor_tensor(hg[slot][:, :, :], hg[slot][:, :, :], shift0, ALU.add))
                v.tensor_tensor(xd[slot][:, :, :], tmp[:, :, :], shift0, ALU.add).then_inc(s_x1, 1)
                dve.wait_ge(s_x1, g + 1)
                for k in range(G):
                    steps.inc(v.bn_stats(stats[:, k, :], hg[slot][:, k, :]))
                    steps.inc(v.bn_stats(stats[:, G + k, :], xd[slot][:, k, :]))
                steps.hold(m.passed)
                for k in range(2 * G):
                    ins = v.bn_aggr(mv[:, k, :], stats[:, k, :])
                    steps.inc(ins)
                steps.wait()
                if not (first and slot == 0):
                    dve.wait_ge(s_h, g)
                norm_rows(v, steps, mv, work, rstd[:, :, 0], shift[:, :, 0]).then_inc(s_norm, 1)

            def score(i, slot):
                g = i * 2 + slot
                steps.link(v.tensor_tensor(qk[:, :, :], m.rel[:, :, :].to_broadcast([P, G, D]),
                                           m.weight[:, group(i, slot), :].to_broadcast([P, G, D]), ALU.mult))
                dve.wait_ge(s_kvq, g + 1)
                steps.link(v.tensor_tensor(qk[:, :, :], qk[:, :, :], q[:, 0:G, :], ALU.add))
                steps.link(v.tensor_tensor(qk[:, :, :], qk[:, :, :], key[:, 0:G, :], ALU.mult))
                v.tensor_reduce(scores[:, group(i, slot), :], qk[:, :, :].rearrange("p g (h c) -> p g h c", c=DK),
                                AX.X, ALU.add).then_inc(s_used, 1)
                dve.wait_ge(s_used, g + 1)

            def body(i, first):
                for slot in (0, 1):
                    normalise(i, slot, first)
                    if not (first and slot == 0):
                        score(i - (1 - slot), 1 - slot)
            turns(dve, body, steps, 2 * (5 + 2 * G + 2 * G + 13 + 3))
            score(PAIRS - 1, 1)

        @block.scalar
        def _(act):
            def body(i, first):
                for slot in (0, 1):
                    g = i * 2 + slot
                    act.wait_ge(s_norm, g + 1)
                    if not (first and slot == 0):
                        act.wait_ge(s_turned, g * 2)
                    for k in range(G):
                        nc.scalar.activation(h[:, k, :], hg[slot][:, k, :], ACT.Relu, bias=shift[:, k, :], scale=rstd[:, k, :])
                        ins = nc.scalar.activation(h[:, G + k, :], xd[slot][:, k, :], ACT.Relu, bias=shift[:, G + k, :],
                                                   scale=rstd[:, G + k, :])
                    ins.then_inc(s_h, 1)
                    if not (first and slot == 0):
                        keep(i - (1 - slot), 1 - slot, g)
                    for side in (0, 1):
                        act.wait_ge(s_turned, g * 2 + (side + 1))
                        nc.scalar.activation(ht[:, side, :], turned[:, 0:G * D], ACT.Copy).then_inc(s_ht, 1)

            def keep(i, slot, count):
                act.wait_ge(s_kvq, count)
                nc.scalar.activation(m.rows[:, group(i, slot), :], value[:, 0:G, :], ACT.Copy).then_inc(s_val, 1)
            turns(act, body)
            keep(PAIRS - 1, 1, NG)

        @block.tensor
        def _(pe):
            def body(i, first):
                for slot in (0, 1):
                    g = i * 2 + slot
                    pe.wait_ge(s_h, g + 1)
                    for side in (0, 1):
                        if side or not (first and slot == 0):
                            pe.wait_ge(s_ht, g * 2 + side)
                        for k in range(G):
                            ins = nc.tensor.transpose(turned[:, k * D:(k + 1) * D], h[:, side * G + k, :], m.ident[:, :])
                        ins.then_inc(s_turned, 1)
                    pe.wait_ge(s_ht, g * 2 + 2)
                    if not (first and slot == 0):
                        pe.wait_ge(s_used, g)
                        pe.wait_ge(s_val, g)
                    for k in range(G):
                        for n, (product, side, weights) in enumerate(((key, 0, m.wkv[:, 0:D]), (value, 0, m.wkv[:, D:2 * D]),
                                                                      (q, 1, m.wq[:, :]))):
                            nc.tensor.matmul(product[:, k, :], ht[:, side, k * D:(k + 1) * D], weights, start=True, stop=False)
                            ins = nc.tensor.matmul(product[:, k, :], m.ones[0:1, 0:P], m.bias_kvq[0:1, n * D:(n + 1) * D],
                                                   start=False, stop=True)
                    ins.then_inc(s_kvq, 1)
            turns(pe, body)


def softmax(nc, m, o, score, heads, scale, name):
    with ExitStack() as ctx:
        def sb(nm, shape, dt=F32):
            return ctx.enter_context(nc.sbuf_tensor(name + nm, shape, dt))

        top, top_back = sb("top", [P, T, heads]), sb("top_back", [P, T, heads])
        cut, cut_back = sb("cut", [P, T]), sb("cut_back", [P, T])
        cut_first, cut_last = sb("cut_first", [P, T]), sb("cut_last", [P, T])
        cut_chunks = [sb(f"cut_chunks{i}", [P, 1, P]) for i in (0, 1)]
        ends = sb("ends", [P, heads, P])
        all_ends = [ctx.enter_context(nc.psum_tensor(f"{name}all_ends{i}", [P, max(heads, 4), P], F32)) for i in (0, 1)]
        masked = sb("masked", [P, heads, P])
        reach = [sb(f"reach{i}", [P, heads]) for i in (0, 1)]
        s_step, s_ends, s_all, s_shifted, s_exp = (m.sem(name + n) for n in ("step", "ends", "all_ends", "shifted", "exp"))
        block = ctx.enter_context(nc.Block())

        @block.vector
        def _(dve):
            v = nc.vector
            steps = Steps(dve, s_step)
            for out, mark in ((cut[:, :], m.same[o][:, 0:T]), (cut_back[:, :], m.same[o][:, 1:T + 1]), (cut_first[:, :], m.first[o][:, :, 0]),
                              (cut_last[:, :], m.last[o][:, :, 0]), (cut_chunks[0][:, 0, :], m.after[o][:, :]),
                              (cut_chunks[1][:, 0, :], m.before[o][:, :])):
                steps.inc(v.tensor_scalar(out, mark, -1.0, BIG, ALU.add, ALU.mult))
            steps.wait()
            for h in range(heads):
                steps.inc(v.tensor_tensor_scan(top[:, :, h], cut[:, :], score[:, :, h], -BIG, ALU.add, ALU.max))
            steps.wait()
            for h in range(heads):
                steps.inc(v.tensor_tensor_scan(top_back[:, ::-1, h], cut_back[:, ::-1], top[:, ::-1, h], -BIG, ALU.add, ALU.max))
            steps.wait()
            for side, t in ((0, T - 1), (1, 0)):
                v.tensor_copy(ends[:, :, :], top_back[:, t, :].unsqueeze(2).to_broadcast([P, heads, P])).then_inc(s_ends, 1)
                dve.wait_ge(s_all, side + 1)
                steps.link(v.tensor_tensor(masked[:, :, :], all_ends[side][:, 0:heads, :],
                                           cut_chunks[side][:, :, :].to_broadcast([P, heads, P]), ALU.add))
                steps.link(v.tensor_reduce(reach[side][:, :], masked[:, :, :], AX.X, ALU.max))
            for side, marks in ((0, cut_first), (1, cut_last)):
                for h in range(heads):
                    steps.inc(v.scalar_tensor_tensor(top_back[:, :, h], marks[:, :], reach[side][:, h:h + 1], top_back[:, :, h],
                                                     ALU.add, ALU.max))
                steps.wait()
            v.tensor_tensor(score[:, :, :], score[:, :, :], top_back[:, :, :], ALU.subtract).then_inc(s_shifted, 1)

        @block.tensor
        def _(pe):
            for side in (0, 1):
                pe.wait_ge(s_ends, side + 1)
                for h in range(heads):
                    ins = nc.tensor.transpose(all_ends[side][:, h, :], ends[:, h, :], m.ident[:, :])
                ins.then_inc(s_all, 1)

        @block.scalar
        def _(act):
            act.wait_ge(s_shifted, 1)
            nc.scalar.activation(score[:, :, :], score[:, :, :], ACT.Exp, scale=scale).then_inc(s_exp, 1)


def weigh(nc, m, o, score, heads, total, name, with_dinv=False):
    with ExitStack() as ctx:
        def sb(nm, shape, dt=F32):
            return ctx.enter_context(nc.sbuf_tensor(name + nm, shape, dt))

        width = D // heads
        part = [sb(f"part{i}", [P, G, D]) for i in (0, 1)]
        carry_ps = ctx.enter_context(nc.psum_tensor(name + "carry", [P, 512], F32))
        total_ps = ctx.enter_context(nc.psum_tensor(name + "total", [P, 512], F32))
        s_step, s_sum, s_kept, s_ends, s_carry = (m.sem(name + n) for n in ("step", "summed", "kept", "ends", "carry"))
        same_g = [sb(f"same{i}", [P, G]) for i in (0, 1)]
        if with_dinv:
            slots = value_slots(m, ctx, "dinv1_")
        block = ctx.enter_context(nc.Block())

        @block.gpsimd
        def _(pool):
            if with_dinv:
                get_dinv(nc, m, pool, slots)

        @block.vector
        def _(dve):
            v = nc.vector
            steps = Steps(dve, s_step)
            for h in range(heads):
                steps.inc(v.tensor_tensor_scan(total[:, :, h], m.same[o][:, 0:T], score[:, :, h], 0.0, ALU.mult, ALU.add))
            steps.wait()

            def body(i, first):
                for slot in (0, 1):
                    g = i * 2 + slot
                    if not first:
                        dve.wait_ge(s_kept, g - 1)
                    steps.inc(v.tensor_copy(same_g[slot][:, :], m.same[o][:, group(i, slot)]))
                    weighed = (part[slot][:, :, :], m.rows[:, group(i, slot), :], score[:, group(i, slot), :])
                    if heads > 1:
                        out, row = (a.rearrange("p g (h c) -> p (g h) c", c=width) for a in weighed[0:2])
                        s = weighed[2].rearrange("p g h -> p (g h)").unsqueeze(2).to_broadcast([P, G * heads, width])
                    else:
                        out, row, s = weighed[0], weighed[1], weighed[2].to_broadcast([P, G, D])
                    steps.link(v.tensor_tensor(out, row, s, ALU.mult))
                    for k in range(G):
                        if first and slot == 0 and k == 0:
                            continue
                        before = part[slot][:, k - 1, :] if k else part[1 - slot][:, G - 1, :]
                        ins = v.scalar_tensor_tensor(part[slot][:, k, :], before, same_g[slot][:, k:k + 1], part[slot][:, k, :],
                                                     ALU.mult, ALU.add)
                        if k < G - 1:
                            steps.link(ins)
                        else:
                            ins.then_inc(s_sum, 1)
                            dve.wait_ge(s_sum, g + 1)
            turns(dve, body, steps, 2 * (G + 1))
            dve.wait_ge(s_carry, 1)
            steps.inc(v.tensor_copy(m.carry[:, 0, :], carry_ps[:, 0:D]))
            for h in range(heads):
                steps.inc(v.scalar_tensor_tensor(total[:, :, h], m.first[o][:, :, 0], total_ps[:, h:h + 1], total[:, :, h],
                                                 ALU.mult, ALU.add))
            steps.wait()
            steps.link(v.tensor_scalar(total[:, :, :], total[:, :, :], 1e-30, None, ALU.max))
            steps.link(v.reciprocal(total[:, :, :], total[:, :, :]))

        @block.scalar
        def _(act):
            def body(i, first):
                for slot in (0, 1):
                    g = i * 2 + slot
                    act.wait_ge(s_sum, g + 1)
                    nc.scalar.activation(m.rows[:, group(i, slot), :], part[slot][:, :, :], ACT.Copy).then_inc(s_kept, 1)
            turns(act, body)

        @block.tensor
        def _(pe):
            pe.wait_ge(s_kept, NG)
            nc.tensor.matmul(carry_ps[:, 0:D], m.before[o][:, :], m.rows[:, T - 1, :], start=True, stop=True)
            nc.tensor.matmul(total_ps[:, 0:heads], m.before[o][:, :], total[:, T - 1, :], start=True, stop=True).then_inc(s_carry, 1)


def finish(nc, m, o, total, heads, rectify, base_rows, table, name):
    with ExitStack() as ctx:
        def sb(nm, shape, dt=F32):
            return ctx.enter_context(nc.sbuf_tensor(name + nm, shape, dt))

        numbers = [sb(f"numbers{i}", [P, G], I32) for i in (0, 1)]
        base = [sb(f"base{i}", [P, G, D]) for i in (0, 1)]
        row = [sb(f"row{i}", [P, G, D]) for i in (0, 1)]
        tmp = sb("tmp", [P, G, D])
        s_num, s_step, s_row = (m.sem(name + n) for n in ("numbers_staged", "step", "rows_made"))
        s_base = [m.sem(f"{name}base_in{i}") for i in (0, 1)]
        s_scat = [m.lasting_sem(f"{name}scattered{i}") for i in (0, 1)]
        block = ctx.enter_context(nc.Block())

        @block.sync
        def _(sp):
            def body(i, first):
                for slot in (0, 1):
                    g = i * 2 + slot
                    if not first:
                        sp.wait_ge(s_row, g - 1)
                    sp.dma_start(base[slot][:, :, :], chunk(base_rows, i, slot)).then_inc(s_base[slot], 16)
            turns(sp, body)

        @block.gpsimd
        def _(pool):
            def body(i, first):
                for slot in (0, 1):
                    g = i * 2 + slot
                    if not first:
                        hold(pool, m.passed, s_scat[slot], i * (16 * G))
                    stage_columns(pool, nc, m, numbers, m.tail_idx[o], i, slot, s_num, g + 1)
                    hold(pool, m.passed, s_row, g + 1)
                    scatter(pool, table, row[slot], numbers[slot], s_scat[slot])
            turns(pool, body)
            for slot in (0, 1):
                pool.wait_ge(s_scat[slot], 16 * G * PAIRS)

        @block.vector
        def _(dve):
            v = nc.vector
            steps = Steps(dve, s_step)
            width = D // heads

            def body(i, first):
                for slot in (0, 1):
                    g = i * 2 + slot
                    steps.link(v.tensor_tensor(tmp[:, :, :], m.carry[:, :, :].to_broadcast([P, G, D]),
                                               m.first[o][:, group(i, slot), :].to_broadcast([P, G, D]), ALU.mult))
                    steps.link(v.tensor_tensor(tmp[:, :, :], tmp[:, :, :], m.rows[:, group(i, slot), :], ALU.add))
                    if heads > 1:
                        split = tmp[:, :, :].rearrange("p g (h c) -> p (g h) c", c=width)
                        per_head = total[:, group(i, slot), :].rearrange("p g h -> p (g h)").unsqueeze(2).to_broadcast([P, G * heads, width])
                    else:
                        split, per_head = tmp[:, :, :], total[:, group(i, slot), :].to_broadcast([P, G, D])
                    steps.link(v.tensor_tensor(split, split, per_head, ALU.mult))
                    dve.wait_ge(s_base[slot], i * 16 + 16)
                    if not first:
                        dve.wait_ge(s_scat[slot], i * (16 * G))
                    if rectify:
                        steps.link(v.scalar_tensor_tensor(tmp[:, :, :], tmp[:, :, :], 0.0, base[slot][:, :, :], ALU.max, ALU.add))
                        ins = v.tensor_tensor(row[slot][:, :, :], tmp[:, :, :], m.rb2[:, :, :].to_broadcast([P, G, D]), ALU.add)
                    else:
                        ins = v.tensor_tensor(row[slot][:, :, :], tmp[:, :, :], base[slot][:, :, :], ALU.add)
                    ins.then_inc(s_row, 1)
                    dve.wait_ge(s_row, g + 1)
            turns(dve, body, steps, 2 * (4 if rectify else 3))


def sum_neighbour_rows(nc, m, out):
    with ExitStack() as ctx:
        def sb(nm, shape, dt=F32):
            return ctx.enter_context(nc.sbuf_tensor("l2_" + nm, shape, dt))

        def two(nm, shape, dt=F32):
            return [sb(f"{nm}{i}", shape, dt) for i in (0, 1)]

        def sem(nm):
            return m.sem("l2_" + nm)

        o = BY_SRC
        dst_numbers = two("dst_numbers", [P, G], I32)
        yd, x2, h = two("yd", [P, G, D]), two("x2", [P, G, D]), two("h", [P, G, D])
        same_g, mv, rstd, shift = two("same", [P, G]), two("mv", [P, G, 2]), two("rstd", [P, G, 1]), two("shift", [P, G, 1])
        stats, work = sb("stats", [P, G, 6]), sb("work", [P, 2, G])
        s_dst, s_step, s_x2, s_norm, s_h, s_sum, s_kept = (
            sem(n) for n in ("dst_staged", "step", "x2_made", "norm", "h_made", "summed", "kept"))
        s_yd = [m.lasting_sem(f"l2_yd_in{i}") for i in (0, 1)]
        s_stored = [sem(f"yd_stored{i}") for i in (0, 1)]
        block = ctx.enter_context(nc.Block())

        @block.gpsimd
        def _(pool):
            def body(i, first):
                for slot in (0, 1):
                    g = i * 2 + slot
                    if not first:
                        hold(pool, m.passed, s_x2, g - 1)
                        hold(pool, m.passed, s_stored[slot], i * 16)
                    stage_columns(pool, nc, m, dst_numbers, m.dst_idx[o], i, slot, s_dst, g + 1)
                    gather(pool, yd[slot], out, dst_numbers[slot], s_yd[slot])
            turns(pool, body)

        @block.sync
        def _(sp):
            with sp.Fori(0, PAIRS) as i:
                for slot in (0, 1):
                    sp.wait_ge(s_yd[slot], i * (16 * G) + 16 * G)
                    sp.dma_start(chunk(m.y_dst, i, slot), yd[slot][:, :, :]).then_inc(s_stored[slot], 16)
            for slot in (0, 1):
                sp.wait_ge(s_stored[slot], 16 * PAIRS)

        @block.scalar
        def _(act):
            def body(i, first):
                for slot in (0, 1):
                    g = i * 2 + slot
                    act.wait_ge(s_norm, g + 1)
                    if not first:
                        act.wait_ge(s_kept, g - 1)
                    for k in range(G):
                        ins = nc.scalar.activation(h[slot][:, k, :], x2[slot][:, k, :], ACT.Relu,
                                                   bias=shift[slot][:, k, :], scale=rstd[slot][:, k, :])
                    ins.then_inc(s_h, 1)
                    act.wait_ge(s_sum, g + 1)
                    nc.scalar.activation(m.rows[:, group(i, slot), :], h[slot][:, :, :], ACT.Copy).then_inc(s_kept, 1)
            turns(act, body)

        @block.vector
        def _(dve):
            v = nc.vector
            steps = Steps(dve, s_step)

            def body(i, first):
                for slot in (0, 1):
                    g = i * 2 + slot
                    dve.wait_ge(s_yd[slot], i * (16 * G) + 16 * G)
                    v.tensor_tensor(x2[slot][:, :, :], yd[slot][:, :, :], m.rb2[:, :, :].to_broadcast([P, G, D]),
                                    ALU.subtract).then_inc(s_x2, 1)
                    dve.wait_ge(s_x2, g + 1)
                    steps.link(row_stats(v, m, steps, x2[slot], G, stats, mv[slot]))
                    steps.inc(v.tensor_copy(same_g[slot][:, :], m.same[o][:, group(i, slot)]))
                    steps.link(norm_rows(v, steps, mv[slot], work, rstd[slot][:, :, 0], shift[slot][:, :, 0]))
                    steps.inc(v.tensor_tensor(rstd[slot][:, :, :], rstd[slot][:, :, :], m.dinv_dst[:, group(i, slot), :], ALU.mult))
                    v.tensor_tensor(shift[slot][:, :, :], shift[slot][:, :, :], m.dinv_dst[:, group(i, slot), :],
                                    ALU.mult).then_inc(s_norm, 1)
                    steps.wait()
                    dve.wait_ge(s_h, g + 1)
                    for k in range(G):
                        if first and slot == 0 and k == 0:
                            continue
                        before = h[slot][:, k - 1, :] if k else h[1 - slot][:, G - 1, :]
                        ins = v.scalar_tensor_tensor(h[slot][:, k, :], before, same_g[slot][:, k:k + 1], h[slot][:, k, :],
                                                     ALU.mult, ALU.add)
                        if k < G - 1:
                            steps.link(ins)
                        else:
                            ins.then_inc(s_sum, 1)
                            dve.wait_ge(s_sum, g + 1)
            turns(dve, body, steps, 2 * (3 * G + 15))


def transform_sums2(nc, m, out):
    with ExitStack() as ctx:
        def sb(nm, shape, dt=F32):
            return ctx.enter_context(nc.sbuf_tensor("t2_" + nm, shape, dt))

        def two(nm, shape, dt=F32):
            return [sb(f"{nm}{i}", shape, dt) for i in (0, 1)]

        def psum(nm, cols):
            return ctx.enter_context(nc.psum_tensor("t2_" + nm, [P, cols], F32))

        def sem(nm):
            return m.sem("t2_" + nm)

        o = BY_SRC
        numbers, src_numbers = two("numbers", [P, G], I32), two("src_numbers", [P, G], I32)
        u, d, uts, ys, h = two("u", [P, G, D]), two("d", [P, G, D]), two("uts", [P, G * D]), two("ys", [P, G, D]), two("h", [P, G, D])
        mv, rstd, shift = two("mv", [P, G, 2]), two("rstd", [P, G, 1]), two("shift", [P, G, 1])
        tmp, fix, dot, stats, work = sb("tmp", [P, G, D]), sb("fix", [P, G, D]), sb("dot", [P, G, D]), sb("stats", [P, G, 6]), sb("work", [P, 2, G])
        ut, z, carry_ps, end_ps = [psum(f"ut{i}", 8 * D) for i in (0, 1)], psum("z", 8 * D), psum("carry", 512), psum("end", 512)
        s_num, s_step, s_carry, s_u, s_turned, s_uts, s_z, s_d, s_x3, s_norm, s_h, s_spread, s_end, s_src = (
            sem(n) for n in ("numbers_staged", "step", "carry_made", "u_made", "u_turned", "uts_made", "z_made", "d_made",
                             "x3_made", "norm", "h_made", "scores_spread", "scores_carried", "src_staged"))
        s_scat = [m.lasting_sem(f"t2_scattered{i}") for i in (0, 1)]
        s_ys = [m.lasting_sem(f"t2_ys_in{i}") for i in (0, 1)]
        s_stored = [sem(f"x3_stored{i}") for i in (0, 1)]
        block = ctx.enter_context(nc.Block())

        @block.gpsimd
        def _(pool):
            def body(i, first):
                for slot in (0, 1):
                    g = i * 2 + slot
                    if not first:
                        hold(pool, m.passed, s_stored[slot], i * 16)
                        hold(pool, m.passed, s_h, g - 1)
                    stage_columns(pool, nc, m, src_numbers, m.src_idx[o], i, slot, s_src, g + 1)
                    gather(pool, ys[slot], out, src_numbers[slot], s_ys[slot])
                    if not (first and slot == 0):
                        put(i - (1 - slot), 1 - slot, first, g)

            def put(i, slot, first, count):
                if not first:
                    hold(pool, m.passed, s_scat[slot], i * (16 * G))
                stage_columns(pool, nc, m, numbers, m.tail_idx[o], i, slot, s_num, count)
                hold(pool, m.passed, s_d, count)
                scatter(pool, m.h2_table, d[slot], numbers[slot], s_scat[slot])
            turns(pool, body)
            put(PAIRS - 1, 1, False, NG)
            for slot in (0, 1):
                pool.wait_ge(s_scat[slot], 16 * G * PAIRS)

        @block.sync
        def _(sp):
            with sp.Fori(0, PAIRS) as i:
                for slot in (0, 1):
                    hold(sp, m.passed, s_x3, i * 2 + (slot + 1))
                    sp.dma_start(chunk(m.x3_src, i, slot), ys[slot][:, :, :]).then_inc(s_stored[slot], 16)
            for slot in (0, 1):
                sp.wait_ge(s_stored[slot], 16 * PAIRS)

        @block.tensor
        def _(pe):
            nc.tensor.matmul(carry_ps[:, 0:D], m.before[o][:, :], m.rows[:, T - 1, :], start=True, stop=True).then_inc(s_carry, 1)

            def body(i, first):
                for slot in (0, 1):
                    g = i * 2 + slot
                    pe.wait_ge(s_u, g + 1)
                    for k in range(G):
                        ins = nc.tensor.transpose(ut[slot][:, k * D:(k + 1) * D], u[slot][:, k, :], m.ident[:, :])
                    ins.then_inc(s_turned, 1)
                    pe.wait_ge(s_uts, g + 1)
                    if not (first and slot == 0):
                        pe.wait_ge(s_d, g)
                    for k in range(G):
                        ins = nc.tensor.matmul(z[:, k * D:(k + 1) * D], uts[slot][:, k * D:(k + 1) * D], m.w2[:, :],
                                               start=True, stop=True)
                    ins.then_inc(s_z, 1)
            turns(pe, body)
            pe.wait_ge(s_spread, 1)
            nc.tensor.matmul(end_ps[:, 0:1], m.after[o][:, :], m.to_self[:, 0, :], start=True, stop=True).then_inc(s_end, 1)

        @block.scalar
        def _(act):
            def body(i, first):
                for slot in (0, 1):
                    g = i * 2 + slot
                    act.wait_ge(s_turned, g + 1)
                    nc.scalar.activation(uts[slot][:, :], ut[slot][:, 0:G * D], ACT.Copy).then_inc(s_uts, 1)
                    if not (first and slot == 0):
                        normalise(1 - slot, g)

            def normalise(slot, count):
                act.wait_ge(s_norm, count)
                for k in range(G):
                    ins = nc.scalar.activation(h[slot][:, k, :], ys[slot][:, k, :], ACT.Relu,
                                               bias=shift[slot][:, k, :], scale=rstd[slot][:, k, :])
                ins.then_inc(s_h, 1)
            turns(act, body)
            normalise(1, NG)

        @block.vector
        def _(dve):
            v = nc.vector
            steps = Steps(dve, s_step)
            dve.wait_ge(s_carry, 1)
            steps.link(v.tensor_copy(m.carry[:, 0, :], carry_ps[:, 0:D]))

            def sums(i, slot):
                steps.link(v.tensor_tensor(fix[:, :, :], m.carry[:, :, :].to_broadcast([P, G, D]),
                                           m.first[o][:, group(i, slot), :].to_broadcast([P, G, D]), ALU.mult))
                v.tensor_tensor(u[slot][:, :, :], fix[:, :, :], m.rows[:, group(i, slot), :], ALU.add).then_inc(s_u, 1)
                dve.wait_ge(s_u, i * 2 + (slot + 1))

            def rows(i, slot, first, count):
                dve.wait_ge(s_z, count)
                z3 = z[:, 0:G * D].rearrange("p (g d) -> p g d", d=D)
                steps.link(v.tensor_tensor(tmp[:, :, :], z3, m.dinv_src[:, group(i, slot), :].to_broadcast([P, G, D]), ALU.mult))
                steps.link(v.tensor_tensor(tmp[:, :, :], tmp[:, :, :], m.b2[:, :, :].to_broadcast([P, G, D]), ALU.add))
                if not first:
                    dve.wait_ge(s_scat[slot], i * (16 * G))
                v.scalar_tensor_tensor(d[slot][:, :, :], tmp[:, :, :], 0.0, m.rb2[:, :, :].to_broadcast([P, G, D]),
                                       ALU.max, ALU.subtract).then_inc(s_d, 1)
                dve.wait_ge(s_d, count)
                dve.wait_ge(s_ys[slot], i * (16 * G) + 16 * G)
                v.tensor_tensor(ys[slot][:, :, :], ys[slot][:, :, :], d[slot][:, :, :], ALU.add).then_inc(s_x3, 1)
                dve.wait_ge(s_x3, count)
                steps.link(row_stats(v, m, steps, ys[slot], G, stats, mv[slot]))
                norm_rows(v, steps, mv[slot], work, rstd[slot][:, :, 0], shift[slot][:, :, 0]).then_inc(s_norm, 1)

            def part_of_score(i, slot, count):
                dve.wait_ge(s_h, count)
                steps.link(v.tensor_tensor(dot[:, :, :], h[slot][:, :, :], m.to_src[:, :, :].to_broadcast([P, G, D]), ALU.mult))
                steps.link(v.tensor_reduce(m.to_self[:, group(i, slot), 0], dot[:, :, :], AX.X, ALU.add))

            def body(i, first):
                for slot in (0, 1):
                    g = i * 2 + slot
                    sums(i, slot)
                    if not first:
                        part_of_score(i - 1, slot, g - 1)
                    if not (first and slot == 0):
                        rows(i - (1 - slot), 1 - slot, first, g)
            turns(dve, body, steps, 2 * (1 + 2 + 2 + 2 * G + 13))
            part_of_score(PAIRS - 1, 0, NG - 1)
            rows(PAIRS - 1, 1, False, NG)
            part_of_score(PAIRS - 1, 1, NG)
            steps.link(v.tensor_tensor(m.to_self[:, :, 0], m.to_self[:, :, 0], m.tail[o][:, :, 0], ALU.mult))
            steps.link(v.tensor_tensor_scan(m.score3[:, ::-1, 0], m.same[o][:, T:0:-1], m.to_self[:, ::-1, 0], 0.0, ALU.mult, ALU.add))
            v.tensor_copy(m.to_self[:, :, 0], m.score3[:, :, 0]).then_inc(s_spread, 1)
            dve.wait_ge(s_end, 1)
            steps.link(v.scalar_tensor_tensor(m.to_self[:, :, 0], m.last[o][:, :, 0], end_ps[:, 0:1], m.score3[:, :, 0],
                                              ALU.mult, ALU.add))


def kan(nc, m):
    with ExitStack() as ctx:
        def sb(nm, shape, dt=F32):
            return ctx.enter_context(nc.sbuf_tensor("kan_" + nm, shape, dt))

        def two(nm, shape, dt=F32):
            return [sb(f"{nm}{i}", shape, dt) for i in (0, 1)]

        def sem(nm):
            return m.sem("kan_" + nm)

        o = BY_SRC
        parts = KNOTS + 1
        knot = [(n + 0.5) * GRID_STEP for n in range(KNOTS)]
        numbers = two("numbers", [P, G], I32)
        hd, yd, h, ht = two("hd", [P, G, D]), two("yd", [P, G, D]), two("h", [P, G, D]), two("ht", [P, G * D])
        mv, rstd, shift = two("mv", [P, G, 2]), two("rstd", [P, G, 1]), two("shift", [P, G, 1])
        stats, work, knots = sb("stats", [P, G, 6]), sb("work", [P, 2, G]), sb("knots", [P, KNOTS])
        silu = sb("silu", [P, G * D])
        near_dve, near_act = sb("near_dve", [P, G * D]), two("near_act", [P, G * D])
        cube = [sb(f"cube{i}", [P, G * D]) for i in range(KNOTS)]
        zero_row = sb("zero_row", [1, 512], mybir.dt.bfloat16)
        turned = ctx.enter_context(nc.psum_tensor("kan_turned", [P, 8 * D], F32))
        val = [ctx.enter_context(nc.psum_tensor(f"kan_val{i}", [P, 8, D], F32)) for i in (0, 1)]
        dots = ctx.enter_context(nc.psum_tensor("kan_dots", [P, 512], F32))
        s_num, s_step, s_x3, s_norm, s_h, s_turned, s_ht, s_tanh, s_silu, s_near, s_square, s_cube, s_dots, s_taken, s_mult, s_kept, s_made = (
            sem(n) for n in ("numbers_staged", "step", "x3_made", "norm", "h_made", "h_turned", "ht_made", "tanh_made", "silu_made",
                             "near_made", "squared", "cubed", "dots_made", "dots_taken", "multiplied", "values_kept", "constants_made"))
        s_hd = [m.lasting_sem(f"kan_hd_in{i}") for i in (0, 1)]
        s_yd = [sem(f"yd_in{i}") for i in (0, 1)]
        s_near_dve = sem("near_dve_made")
        block = ctx.enter_context(nc.Block())

        @block.gpsimd
        def _(pool):
            nc.gpsimd.memset(zero_row[:, :], 0.0).then_inc(s_made, 1)
            for n in range(KNOTS):
                nc.gpsimd.memset(knots[:, n:n + 1], knot[n]).then_inc(s_made, 1)

            def body(i, first):
                for slot in (0, 1):
                    g = i * 2 + slot
                    if not first:
                        hold(pool, m.passed, s_x3, g - 1)
                    stage_columns(pool, nc, m, numbers, m.dst_idx[o], i, slot, s_num, g + 1)
                    gather(pool, hd[slot], m.h2_table, numbers[slot], s_hd[slot])
            turns(pool, body)

        @block.sync
        def _(sp):
            def body(i, first):
                for slot in (0, 1):
                    g = i * 2 + slot
                    if not first:
                        sp.wait_ge(s_h, g - 1)
                    sp.dma_start(yd[slot][:, :, :], chunk(m.y_dst, i, slot)).then_inc(s_yd[slot], 16)
            turns(sp, body)

        @block.vector
        def _(dve):
            v = nc.vector
            steps = Steps(dve, s_step)

            def normalise(i, slot, first):
                g = i * 2 + slot
                dve.wait_ge(s_hd[slot], i * (16 * G) + 16 * G)
                dve.wait_ge(s_yd[slot], i * 16 + 16)
                v.tensor_tensor(yd[slot][:, :, :], yd[slot][:, :, :], hd[slot][:, :, :], ALU.add).then_inc(s_x3, 1)
                dve.wait_ge(s_x3, g + 1)
                steps.link(row_stats(v, m, steps, yd[slot], G, stats, mv[slot]))
                norm_rows(v, steps, mv[slot], work, rstd[slot][:, :, 0], shift[slot][:, :, 0]).then_inc(s_norm, 1)

            def features(i, slot, g, first):
                dve.wait_ge(s_ht, g + 1)

                def near(n):
                    v.tensor_scalar(near_dve[:, :], ht[slot][:, :], knot[n], knot[n], ALU.min, ALU.subtract).then_inc(s_near_dve, 1)

                near(0)
                dve.wait_ge(s_tanh, g + 1)
                v.scalar_tensor_tensor(silu[:, :], silu[:, :], 1.0, ht[slot][:, :], ALU.add, ALU.mult).then_inc(s_silu, 1)
                for n in range(KNOTS):
                    dve.wait_ge(s_square, g * KNOTS + (n + 1))
                    source = near_dve if n < DVE_KNOTS else near_act[n % 2]
                    v.tensor_tensor(cube[n][:, :], cube[n][:, :], source[:, :], ALU.mult).then_inc(s_cube, 1)
                    if n + 1 < DVE_KNOTS:
                        dve.wait_ge(s_cube, g * KNOTS + (n + 1))
                        near(n + 1)
                dve.wait_ge(s_dots, g + 1)
                v.tensor_copy(m.score3[:, group(i, slot), 0], dots[:, 0:G]).then_inc(s_taken, 1)

            def body(i, first):
                for slot in (0, 1):
                    normalise(i, slot, first)
                    if not first:
                        features(i - 1, slot, i * 2 + (slot - 2), False)
            turns(dve, body, steps, 2 * (2 * G + 13))
            for slot in (0, 1):
                features(PAIRS - 1, slot, NG - 2 + slot, False)

        @block.scalar
        def _(act):
            act.wait_ge(s_made, KNOTS + 1)

            def normalise(i, slot, first):
                g = i * 2 + slot
                act.wait_ge(s_norm, g + 1)
                if not first:
                    act.wait_ge(s_turned, g - 1)
                for k in range(G):
                    ins = nc.scalar.activation(h[slot][:, k, :], yd[slot][:, k, :], ACT.Relu,
                                               bias=shift[slot][:, k, :], scale=rstd[slot][:, k, :])
                ins.then_inc(s_h, 1)

            def features(i, slot, g, first):
                act.wait_ge(s_turned, g + 1)
                nc.scalar.activation(ht[slot][:, :], turned[:, 0:G * D], ACT.Copy).then_inc(s_ht, 1)
                act.wait_ge(s_ht, g + 1)
                if not first:
                    act.wait_ge(s_mult, g * parts - (parts - 1))
                nc.scalar.activation(silu[:, :], ht[slot][:, :], ACT.Tanh, scale=0.5).then_inc(s_tanh, 1)
                for n in range(KNOTS):
                    if n < DVE_KNOTS:
                        act.wait_ge(s_near_dve, g * DVE_KNOTS + (n + 1))
                        near = near_dve
                    else:
                        a = n - DVE_KNOTS
                        near = near_act[n % 2]
                        if a >= 2:
                            act.wait_ge(s_cube, g * KNOTS + (n - 1))
                        elif not first:
                            act.wait_ge(s_cube, g * KNOTS)
                        nc.scalar.activation(near[:, :], ht[slot][:, :], ACT.Relu, bias=knots[:, n:n + 1], scale=-1.0).then_inc(s_near, 1)
                        act.wait_ge(s_near, g * (KNOTS - DVE_KNOTS) + (a + 1))
                    if not first:
                        act.wait_ge(s_mult, g * parts - (parts - 2 - n))
                    nc.scalar.activation(cube[n][:, :], near[:, :], ACT.Square).then_inc(s_square, 1)

            def keep(i, slot, groups):
                act.wait_ge(s_mult, groups * parts)
                nc.scalar.activation(m.rows[:, group(i, slot), :], val[slot][:, 0:G, :], ACT.Copy).then_inc(s_kept, 1)

            def body(i, first):
                for slot in (0, 1):
                    normalise(i, slot, first)
                    if not (first and slot == 0):
                        features(i - (1 - slot), 1 - slot, i * 2 + (slot - 1), first and slot == 1)
                    if not first:
                        keep(i - 1, slot, i * 2 + (slot - 1))
            turns(act, body)
            features(PAIRS - 1, 1, NG - 1, False)
            keep(PAIRS - 1, 0, NG - 1)
            keep(PAIRS - 1, 1, NG)

        @block.tensor
        def _(pe):
            pe.wait_ge(s_made, 1)

            def turn(i, slot, first):
                g = i * 2 + slot
                pe.wait_ge(s_h, g + 1)
                if not (first and slot == 0):
                    pe.wait_ge(s_ht, g)
                for k in range(G):
                    ins = nc.tensor.transpose(turned[:, k * D:(k + 1) * D], h[slot][:, k, :], m.ident[:, :])
                ins.then_inc(s_turned, 1)

            def multiply(i, slot, g, first, second):
                if not first:
                    pe.wait_ge(s_taken, g)
                    if not second:
                        pe.wait_ge(s_kept, g - 1)
                pe.wait_ge(s_ht, g + 1)
                for k in range(G):
                    ins = nc.tensor.matmul(dots[:, k:k + 1], ht[slot][:, k * D:(k + 1) * D], m.to_dst[:, :], start=True, stop=True)
                ins.then_inc(s_dots, 1)
                for half in (0, 4):
                    nc.tensor.matmul(val[slot][:, half:half + 4, :], zero_row[:, 0:P], zero_row[:, :], start=True, stop=False)
                for n in range(parts):
                    if n:
                        pe.wait_ge(s_cube, g * KNOTS + n)
                    else:
                        pe.wait_ge(s_silu, g + 1)
                    part = cube[n - 1] if n else silu
                    for k in range(G):
                        ins = nc.tensor.matmul(val[slot][:, k, :], part[:, k * D:(k + 1) * D], m.w_kan[:, n, :], start=False, stop=False)
                    if n == parts - 1:
                        for half in (0, 4):
                            ins = nc.tensor.matmul(val[slot][:, half:half + 4, :], zero_row[:, 0:P], zero_row[:, :], start=False, stop=True)
                    ins.then_inc(s_mult, 1)

            turn(0, 0, True)
            turn(0, 1, False)
            multiply(0, 0, 0, True, False)
            turn(1, 0, False)
            multiply(0, 1, 1, False, True)
            turn(1, 1, False)
            multiply(1, 0, 2, False, False)
            with pe.Fori(2, PAIRS) as i:
                for slot in (0, 1):
                    turn(i, slot, False)
                    multiply(i - (1 - slot), 1 - slot, i * 2 + (slot - 1), False, False)
            multiply(PAIRS - 1, 1, NG - 1, False, False)


def score_edges3(nc, m):
    with ExitStack() as ctx:
        s_step = m.sem("leaky_step")
        block = ctx.enter_context(nc.Block())

        @block.vector
        def _(dve):
            steps = Steps(dve, s_step)
            steps.link(nc.vector.tensor_tensor(m.score3[:, :, :], m.score3[:, :, :], m.to_self[:, :, :], ALU.add))
            steps.link(nc.vector.scalar_tensor_tensor(m.score3[:, :, :], m.score3[:, :, :], 0.2, m.score3[:, :, :], ALU.mult, ALU.max))


def build(nc, x, records, src, dst, w, out):
    with ExitStack() as ctx:
        m = Memory(nc, ctx)
        sort_edges(nc, m, src, dst)
        m.end_phase()
        index_edges(nc, m, records)
        m.end_phase()
        load_weights(nc, m, w)
        m.end_phase()
        sum_source_rows(nc, m, x)
        m.end_phase()
        transform_sums0(nc, m, x)
        m.end_phase()
        batch_norm_rows(nc, m)
        m.end_phase()
        dense_pass(nc, m, x, out, records)
        m.end_phase()
        with nc.sbuf_tensor("scores", [P, T, H], F32) as scores, nc.sbuf_tensor("totals1", [P, T, H], F32) as totals:
            attend(nc, m, scores)
            m.end_phase()
            softmax(nc, m, BY_DST, scores, H, DK ** -0.5, "sm1_")
            m.end_phase()
            weigh(nc, m, BY_DST, scores, H, totals, "w1_", with_dinv=True)
            m.end_phase()
            finish(nc, m, BY_DST, totals, H, True, m.x1_dst, out, "f1_")
            m.end_phase()
        sum_neighbour_rows(nc, m, out)
        m.end_phase()
        transform_sums2(nc, m, out)
        m.end_phase()
        kan(nc, m)
        m.end_phase()
        score_edges3(nc, m)
        m.end_phase()
        softmax(nc, m, BY_SRC, m.score3, 1, 1.0, "sm3_")
        m.end_phase()
        weigh(nc, m, BY_SRC, m.score3, 1, m.total3, "w3_")
        m.end_phase()
        finish(nc, m, BY_SRC, m.total3, 1, False, m.x3_src, out, "f3_")
        m.end_phase()


def kernel(**inputs):
    import numpy as np
    import concourse.bacc as bacc
    from concourse.bass_utils import run_bass_kernel_spmd as run

    def array(name):
        return np.ascontiguousarray(inputs[name])

    records = np.zeros((E, 4), np.int32)
    records[:, SRC], records[:, DST], records[:, WEIGHT] = array("src"), array("dst"), array("edge_weight").view(np.int32)
    arrays = {
        "x": array("x"), "records": records, "src": array("src"), "dst": array("dst"),
        "w0": array("L0_gnn_W").T, "b0": array("L0_gnn_b"), "gamma": array("L0_gnn_gamma"), "beta": array("L0_gnn_beta"),
        "wk": array("L1_gnn_Wk").T, "bk": array("L1_gnn_bk"), "wq": array("L1_gnn_Wq").T, "bq": array("L1_gnn_bq"),
        "wv": array("L1_gnn_Wv"), "bv": array("L1_gnn_bv"), "rel": array("L1_gnn_rel_att").reshape(D),
        "rel_msg": array("L1_gnn_rel_msg"), "w2": array("L2_gnn_kernel"), "b2": array("L2_gnn_bias"),
        "w3t": array("L3_gnn_W").T, "a": array("L3_gnn_a"), "base": array("L3_gnn_base_weight").T,
        "spline": array("L3_gnn_spline_weight").transpose(2, 1, 0),
    }
    arrays = {"in_" + name: np.ascontiguousarray(a) for name, a in arrays.items()}
    nc = bacc.Bacc("TRN2", target_bir_lowering=False, num_devices=1)
    aps = {name[3:]: nc.dram_tensor(name, a.shape, mybir.dt.from_np(a.dtype), kind="ExternalInput").ap()
           for name, a in arrays.items()}
    out = nc.dram_tensor("out_x", (N, D), F32, kind="ExternalOutput").ap()
    x, records, src, dst = (aps.pop(name) for name in ("x", "records", "src", "dst"))
    build(nc, x, records, src, dst, aps, out)
    return run(nc, [arrays], core_ids=[0]).results[0]["out_x"]
```

```python
import concourse.bass as bass
from concourse import mybir
from contextlib import ExitStack

F32 = mybir.dt.float32
I32 = mybir.dt.int32
ALU = mybir.AluOpType
ACT = mybir.ActivationFunctionType
AX = mybir.AxisListType

N = 100000
E = 25000
D = 128
H = 8
DK = D // H
P = 128
T = -(-E // P)
G = 7
NG = T // G
PAIRS = NG // 2
DEEP = 4
FOURS = NG // DEEP
SORT = 32768
SF = SORT // P
ID_BITS = 15
HALF = N // 2
CODE = 15000
PAD_NODE = N + 1
PAD_CODE = PAD_NODE - HALF + CODE
OUT_OF_RANGE = 200000
BIG = 1.0e38
EPS = 1e-5
BY_DST, BY_SRC = 0, 1
SRC, DST, WEIGHT = 0, 1, 2
TABLE_ROWS = 11
BULK_TURNS = 2 * PAIRS
BULK_ROWS = -(-(N // P) // (2 * BULK_TURNS))
LAST_ROWS = N // P - (2 * BULK_TURNS - 1) * BULK_ROWS
BULK_MAIN = P * (N // P)
TABLE_STEPS = N // P // TABLE_ROWS
BACK_TURNS = BULK_TURNS - PAIRS - 1
BACK_STEPS = (T - 1) // BACK_TURNS
ZERO_ROWS = N // P // (2 * NG)
KNOTS = 6
DVE_KNOTS = 3
GRID_STEP = 0.4
BANK_TILES = 3
SPLINES = 8


class Steps:

    def __init__(self, eng, sem):
        self.eng, self.sem, self.base, self.k = eng, sem, 0, 0

    def inc(self, ins):
        ins.then_inc(self.sem, 1)
        self.k += 1

    def wait(self):
        self.eng.wait_ge(self.sem, self.base + self.k)

    def hold(self, passed):
        hold(self.eng, passed, self.sem, self.base + self.k)

    def link(self, ins):
        self.inc(ins)
        self.wait()


def hold(eng, passed, sem, value):
    eng.wait_ge(sem, value)
    if not isinstance(value, int):
        eng.sem_inc(passed, 1)


def turns(eng, body, steps=None, per=0, peeled=1, count=None):
    count = count or PAIRS
    for i in range(peeled):
        body(i, i == 0)
    before = steps.base + steps.k if steps else 0
    with eng.Fori(peeled, count) as i:
        if steps:
            steps.base, steps.k = i * per + (before - per * peeled), 0
        body(i, False)
        assert not steps or steps.k == per, (steps.k, per)
    if steps:
        steps.base, steps.k = before + per * (count - peeled), 0


def is_first(i):
    return isinstance(i, int) and i == 0


def group(i, slot):
    return bass.ds((i * 2 + slot) * G, G)


def group_of(g):
    return bass.ds(g * G, G)


def chunk(rows, i, slot):
    return rows[:, group(i, slot), :]


class Memory:

    def __init__(self, nc, ctx):
        def sb(name, shape, dt=F32):
            return ctx.enter_context(nc.sbuf_tensor(name, shape, dt))

        self.nc, self.ctx, self.sb = nc, ctx, sb
        self.words_dram = nc.dram_tensor("sorted_words", (2, SORT + P), I32).ap()
        self.h0_table = nc.dram_tensor("h0_table", (N, D), F32).ap()
        self.h2_table = nc.dram_tensor("h2_table", (N, D), F32).ap()
        self.dinv_table = nc.dram_tensor("dinv_table", (N, 1), F32).ap()
        def edge_rows(name):
            return nc.dram_tensor(name, (P, T, D), F32).ap()

        self.x_src, self.x_dst, self.x1_dst = edge_rows("x_src"), edge_rows("x_dst"), edge_rows("x1_dst")
        self.y_src, self.y_dst, self.x3_src = edge_rows("y_src"), edge_rows("y_dst"), edge_rows("x3_src")
        self.rows = sb("rows", [P, T, D])
        self.ident = sb("ident", [P, P])
        self.ones = sb("ones", [P, P])
        self.epsilon = sb("epsilon", [P, 1])
        self.in_head = sb("in_head", [D, H])
        self.mix = sb("mix", [D, D])
        self.edge_no = [sb(f"edge_no{o}", [P, T], I32) for o in (0, 1)]
        self.code = [sb(f"code{o}", [P, T + 2]) for o in (0, 1)]
        self.same = [sb(f"same{o}", [P, T + 1]) for o in (0, 1)]
        self.tail = [sb(f"tail{o}", [P, T, 1]) for o in (0, 1)]
        self.first = [sb(f"first{o}", [P, T, 1]) for o in (0, 1)]
        self.last = [sb(f"last{o}", [P, T, 1]) for o in (0, 1)]
        self.before = [sb(f"before{o}", [P, P]) for o in (0, 1)]
        self.after = [sb(f"after{o}", [P, P]) for o in (0, 1)]
        self.src_idx = [sb(f"src_idx{o}", [P, T], I32) for o in (0, 1)]
        self.dst_idx = [sb(f"dst_idx{o}", [P, T], I32) for o in (0, 1)]
        self.tail_idx = [sb(f"tail_idx{o}", [P, T], I32) for o in (0, 1)]
        self.weight = sb("weight", [P, T, 1])
        self.carry = sb("carry", [P, 1, D])
        def spread(name, cols=D):
            return sb(name, [P, 1, cols])

        self.b0, self.rb0, self.scale0, self.shift0 = spread("b0"), spread("rb0"), spread("scale0"), spread("shift0")
        self.b2, self.rb2 = spread("b2"), spread("rb2")
        self.bv = spread("bv_mixed")
        self.to_src = spread("to_src")
        self.gamma_beta = sb("gamma_beta", [1, 2 * D])
        self.totals = sb("totals", [1, 2 * D])
        self.w0, self.w2 = sb("w0", [D, D]), sb("w2", [D, D])
        self.to_dst = sb("to_dst", [D, 1])
        self.w_value = sb("w_value", [D, D])
        self.w_key, self.w_query = sb("w_key", [D, D + 2 * H]), sb("w_query", [D, D + H])
        self.bk_bq_rel = sb("bk_bq_rel", [P, 2, H])
        self.w_kan = sb("w_kan", [D, KNOTS + 1, D])
        self.score3 = sb("score3", [P, T, 1])
        self.total3 = sb("total3", [P, T, 1])
        self.to_self = sb("to_self", [P, T, 1])
        self.dinv_src = sb("dinv_src", [P, T, 1])
        self.dinv_dst = sb("dinv_dst", [P, T, 1])
        self.phase_sems = []
        self.passed = self.lasting_sem("passed")

    def sem(self, name):
        sem = self.nc.alloc_semaphore(name=name)
        self.phase_sems.append(sem)
        return sem

    def lasting_sem(self, name):
        return self.nc.alloc_semaphore(name=name)

    def end_phase(self):
        for sem in self.phase_sems:
            self.nc.sync.sem_clear(sem)
            self.nc.release_semaphore(sem)
        self.phase_sems = []
        self.nc.all_engine_barrier()


def zero_h2_table(sp, m, zeros, half, begun, sem):
    first = half * NG * ZERO_ROWS
    table = m.h2_table[0:BULK_MAIN, :].rearrange("(p r) d -> p (r d)", p=P)
    with sp.Fori(0, NG) as g:
        sp.wait_ge(begun, g + 1)
        sp.dma_start(table[:, bass.ds(g * (ZERO_ROWS * D) + first * D, ZERO_ROWS * D)], zeros[:, :]).then_inc(sem, 16)
    if half:
        rest = N // P - 2 * NG * ZERO_ROWS
        for at in range(N // P - rest, N // P, ZERO_ROWS):
            n = min(ZERO_ROWS, N // P - at)
            sp.dma_start(table[:, at * D:(at + n) * D], zeros[:, 0:n * D]).then_inc(sem, 16)
        sp.dma_start(m.h2_table[BULK_MAIN:N, :], zeros[0:N - BULK_MAIN, 0:D]).then_inc(sem, 16)
        sp.wait_ge(sem, 16 * (NG + -(-rest // ZERO_ROWS) + 1))
    else:
        sp.wait_ge(sem, 16 * NG)


def sort_edges(nc, m, src, dst):
    with ExitStack() as ctx:
        def sb(name, shape, dt=F32):
            return ctx.enter_context(nc.sbuf_tensor(name, shape, dt))

        key = sb("sort_key", [P, 2, SF], I32)
        key_f = sb("sort_key_f", [P, 2, SF])
        low = sb("sort_low", [P, 2, SF])
        code = sb("sort_code", [P, 2, SF], I32)
        slot = sb("sort_slot", [P, 2, SF], I32)
        gray = sb("sort_gray", [P, 2, SF], I32)
        flips = sb("sort_flips", [P, 2, SF], I32)
        zero_row = sb("sort_zero", [1, 2], I32)
        words = [sb(f"sort_words{i}", [P, 2 * SF]) for i in (0, 1)]
        turned = [ctx.enter_context(nc.psum_tensor(f"sort_turned{i}", [P, 2 * SF], F32)) for i in (0, 1)]
        s_key_pad, s_keys, s_ident, s_slot = (m.sem(n) for n in ("key_pad", "keys_in", "ident_made", "slot_made"))
        s_step, s_ready, s_turned = m.sem("sort_step"), m.sem("sort_ready"), m.sem("sort_turned_done")
        zeros = sb("table_zeros", [P, TABLE_ROWS * D])
        s_zero, s_tables, s_marks = m.sem("zeros_made"), m.sem("tables_zeroed"), m.sem("constants_made")
        s_out, s_zero_row = m.sem("words_out"), m.sem("zero_row_made")
        full = E // SF
        rest = E - full * SF
        s_sorted = m.sem("sorted")

        block = ctx.enter_context(nc.Block())

        @block.sync
        def _(sp):
            sp.wait_ge(s_key_pad, 1)
            for o, keys in ((BY_DST, dst), (BY_SRC, src)):
                sp.dma_start(key[0:full, o, :], keys[0:full * SF].rearrange("(p f) -> p f", f=SF)).then_inc(s_keys, 16)
                sp.dma_start(key[full:full + 1, o, 0:rest],
                             keys[full * SF:E].rearrange("(p f) -> p f", p=1)).then_inc(s_keys, 16)
            sp.wait_ge(s_zero, 1)
            whole = m.h0_table[0:BULK_MAIN, :].rearrange("(p r) d -> p (r d)", p=P)
            with sp.Fori(0, TABLE_STEPS) as i:
                sp.dma_start(whole[:, bass.ds(i * (TABLE_ROWS * D), TABLE_ROWS * D)], zeros[:, :]).then_inc(s_tables, 16)
            sp.dma_start(m.h0_table[BULK_MAIN:N, :], zeros[0:N - BULK_MAIN, 0:D]).then_inc(s_tables, 16)
            sp.dma_start(m.dinv_table[0:BULK_MAIN, :].rearrange("(p r) d -> p (r d)", p=P),
                         zeros[:, 0:N // P]).then_inc(s_tables, 16)
            sp.dma_start(m.dinv_table[BULK_MAIN:N, :], zeros[0:N - BULK_MAIN, 0:1]).then_inc(s_tables, 16)
            sp.wait_ge(s_tables, 16 * (TABLE_STEPS + 3))

        @block.scalar
        def _(act):
            act.wait_ge(s_zero_row, 1)
            for o in (BY_DST, BY_SRC):
                act.dma_start(m.words_dram[o:o + 1, 0:1], zero_row[0:1, o:o + 1]).then_inc(s_out, 16)
            act.wait_ge(s_sorted, 1)
            for o in (BY_DST, BY_SRC):
                act.dma_start(m.words_dram[o, 1:1 + SORT].rearrange("(p f) -> p f", f=SF),
                              words[0][:, o * SF:(o + 1) * SF].bitcast(I32)).then_inc(s_out, 16)
            act.wait_ge(s_out, 64)

        @block.gpsimd
        def _(pool):
            nc.gpsimd.memset(key[:, :, :], PAD_NODE).then_inc(s_key_pad, 1)
            nc.gpsimd.memset(m.ident[:, :], 0.0).then_inc(s_ident, 1)
            nc.gpsimd.iota(slot[:, :, :], pattern=[[0, 2], [1, SF]], base=0, channel_multiplier=SF).then_inc(s_slot, 1)
            nc.gpsimd.memset(zeros[:, :], 0.0).then_inc(s_zero, 1)
            nc.gpsimd.memset(zero_row[:, :], 0).then_inc(s_zero_row, 1)
            nc.gpsimd.memset(m.mix[:, :], 0.0).then_inc(s_marks, 1)
            nc.gpsimd.memset(m.ones[:, :], 1.0).then_inc(s_marks, 1)
            nc.gpsimd.memset(m.epsilon[:, :], EPS).then_inc(s_marks, 1)
            nc.gpsimd.memset(m.in_head[:, :], 1.0).then_inc(s_marks, 1)
            pool.wait_ge(s_ident, 1)
            nc.gpsimd.affine_select(out=m.ident[:, :], in_=m.ident[:, :], compare_op=ALU.not_equal, fill=1.0,
                                    base=0, pattern=[[-1, P]], channel_multiplier=1).then_inc(s_ident, 1)
            pool.wait_ge(s_marks, 4)
            nc.gpsimd.affine_select(out=m.in_head[:, :], in_=m.in_head[:, :], compare_op=ALU.is_ge, fill=0.0,
                                    base=0, pattern=[[-DK, H]], channel_multiplier=1).then_inc(s_marks, 1)
            pool.wait_ge(s_marks, 5)
            nc.gpsimd.affine_select(out=m.in_head[:, :], in_=m.in_head[:, :], compare_op=ALU.is_ge, fill=0.0,
                                    base=DK - 1, pattern=[[DK, H]], channel_multiplier=-1).then_inc(s_marks, 1)
            pool.wait_ge(s_marks, 6)

        @block.vector
        def _(dve):
            steps = Steps(dve, s_step)
            dve.wait_ge(s_slot, 1)
            dve.wait_ge(s_keys, 64)
            v = nc.vector
            steps.inc(v.tensor_scalar(gray[:, :, :], slot[:, :, :], 1, None, ALU.logical_shift_right))
            steps.link(v.tensor_copy(key_f[:, :, :], key[:, :, :]))
            steps.inc(v.tensor_tensor(flips[:, :, :], gray[:, :, :], slot[:, :, :], ALU.bitwise_xor))
            steps.link(v.tensor_scalar(low[:, :, :], key_f[:, :, :], float(HALF), float(2 ** 16 + HALF), ALU.is_lt, ALU.mult))
            steps.inc(v.tensor_copy(gray[:, :, :], flips[:, :, :]))
            steps.link(v.scalar_tensor_tensor(code[:, :, :], key_f[:, :, :], float(CODE - HALF), low[:, :, :], ALU.add, ALU.add))
            steps.inc(v.tensor_scalar(key[:, :, :], code[:, :, :], ID_BITS, None, ALU.logical_shift_left))
            steps.link(v.tensor_scalar(flips[:, :, :], slot[:, :, :], 30, -2 ** 31, ALU.logical_shift_left, ALU.bitwise_and))
            flat = [w[:, :].bitcast(I32) for w in words]
            slot2, key2 = (a[:, :, :].rearrange("p o f -> p (o f)") for a in (slot, key))
            flips2, gray2 = (a[:, :, :].rearrange("p o f -> p (o f)") for a in (flips, gray))
            steps.link(v.tensor_tensor(flat[0], key2, slot2, ALU.bitwise_or))
            turns = 0
            at = 0

            def exchange(a, b, distance):
                x, y = (w[:, :].rearrange("p (a two b) -> p a two b", two=2, b=distance) for w in (words[a], words[b]))
                steps.inc(v.tensor_tensor(y[:, :, 0, :], x[:, :, 0, :], x[:, :, 1, :], ALU.min))
                steps.link(v.tensor_tensor(y[:, :, 1, :], x[:, :, 0, :], x[:, :, 1, :], ALU.max))

            def turn(a, b):
                nonlocal turns
                v.nop().then_inc(s_ready, 1)
                turns += 1
                dve.wait_ge(s_turned, turns)
                steps.link(v.tensor_copy(words[b][:, :], turned[0][:, :]))

            for k in range(1, ID_BITS + 1):
                if k > 1:
                    steps.link(v.tensor_scalar(flips2, gray2, 32 - k, -2 ** 31, ALU.logical_shift_left, ALU.bitwise_and))
                steps.link(v.tensor_tensor(flat[1 - at], flat[at], flips2, ALU.bitwise_xor))
                at = 1 - at
                if k > 8:
                    turn(at, 1 - at)
                    at = 1 - at
                    for j in range(k - 1, 7, -1):
                        exchange(at, 1 - at, 2 ** (j - 8))
                        at = 1 - at
                    exchange(at, 1 - at, P)
                    at = 1 - at
                    turn(at, 1 - at)
                    at = 1 - at
                for j in range(min(k - 1, 6 if k > 8 else 7), -1, -1):
                    exchange(at, 1 - at, 2 ** j)
                    at = 1 - at
            if at:
                steps.link(v.tensor_copy(words[0][:, :], words[1][:, :]))
            v.nop().then_inc(s_sorted, 1)

        @block.tensor
        def _(pe):
            pe.wait_ge(s_ident, 2)
            at, turns = 0, 0
            for k in range(1, ID_BITS + 1):
                at = 1 - at
                if k > 8:
                    for exchanges in (k - 7, 0):
                        turns += 1
                        pe.wait_ge(s_ready, turns)
                        for b in range(4):
                            last = nc.tensor.transpose(turned[0][:, b * P:(b + 1) * P], words[at][:, b * P:(b + 1) * P], m.ident[:, :])
                        last.then_inc(s_turned, 1)
                        at = (at + 1 + exchanges) % 2
                at = (at + (7 if k > 8 else k)) % 2


def record_slots(m, ctx, name):
    stage = [ctx.enter_context(m.nc.sbuf_tensor(f"{name}numbers{i}", [P, G], I32)) for i in (0, 1)]
    got = [ctx.enter_context(m.nc.sbuf_tensor(f"{name}slot{i}", [P, G, 4], I32)) for i in (0, 1)]
    return stage, got, m.sem(name + "staged"), m.sem(name + "taken"), [m.lasting_sem(f"{name}in{i}") for i in (0, 1)]


def fetch_records(nc, m, pool, o, records, fetch):
    stage, got, s_stage, s_taken, s_in = fetch
    other, column = (m.src_idx[o], SRC) if o == BY_DST else (m.dst_idx[o], DST)
    copies = 2 if o == BY_DST else 1

    def take(i, slot):
        hold(pool, m.passed, s_in[slot], i * (16 * G) + 16 * G)
        nc.gpsimd.tensor_copy(other[:, group(i, slot)], got[slot][:, :, column]).then_inc(s_taken, 1)
        if o == BY_DST:
            nc.gpsimd.tensor_copy(m.weight[:, group(i, slot), 0].bitcast(I32), got[slot][:, :, WEIGHT]).then_inc(s_taken, 1)

    def body(i, first):
        for slot in (0, 1):
            g = i * 2 + slot
            if not first:
                hold(pool, m.passed, s_taken, (g - 1) * copies)
            stage_columns(pool, nc, m, stage, m.edge_no[o], i, slot, s_stage, g + 1)
            gather(pool, got[slot], records, stage[slot], s_in[slot])
            if not (first and slot == 0):
                take(i - (1 - slot), 1 - slot)
    turns(pool, body)
    take(PAIRS - 1, 1)
    pool.wait_ge(s_taken, NG * copies)


def index_edges(nc, m, records, ctx, block):
    def sb(name, shape, dt=F32):
        return ctx.enter_context(nc.sbuf_tensor(name, shape, dt))

    words = [sb(f"words{o}", [P, T + 2], I32) for o in (0, 1)]
    code_i = sb("code_i", [P, T + 2], I32)
    edge_f = sb("edge_f", [P, T])
    not_pad = sb("not_pad", [P, T])
    end_rows = sb("end_rows", [P, P])
    upper = sb("upper", [P, P])
    row_end = ctx.enter_context(nc.psum_tensor("row_end", [P, P], F32))
    before_t = ctx.enter_context(nc.psum_tensor("before_t", [P, P], F32))
    count_ps = ctx.enter_context(nc.psum_tensor("count_carry", [P, 512], F32))
    row_f, node_f = sb("row_f", [P, T]), sb("node_f", [P, T])
    ones_row, count, root = sb("ones_row", [P, T]), sb("count", [P, T]), sb("root", [P, T])
    s_words, s_step, s_ids, s_upper = m.sem("words_in"), m.sem("index_step"), m.sem("edge_ids"), m.sem("upper_made")
    s_row, s_rowt, s_bef, s_beft = m.sem("end_rows_ready"), m.sem("end_rows_turned"), m.sem("before_ready"), m.sem("before_turned")
    s_count, s_counted, s_root = m.sem("counts"), m.sem("counts_carried"), m.sem("count_roots")
    fetch = record_slots(m, ctx, "rec0_")


    @block.sync
    def _(sp):
        for o in (BY_DST, BY_SRC):
            w = m.words_dram[o, :]
            src = bass.AP(tensor=w.tensor, offset=w.offset, ap=[[T, P], [1, T + 2]])
            sp.dma_start(words[o][:, :], src).then_inc(s_words, 16)

    @block.gpsimd
    def _(pool):
        nc.gpsimd.memset(upper[:, :], 1.0).then_inc(s_upper, 1)
        pool.wait_ge(s_upper, 1)
        nc.gpsimd.affine_select(out=upper[:, :], in_=upper[:, :], compare_op=ALU.is_gt, fill=0.0,
                                base=0, pattern=[[1, P]], channel_multiplier=-1).then_inc(s_upper, 1)
        pool.wait_ge(s_ids, 1)
        fetch_records(nc, m, pool, BY_DST, records, fetch)

    @block.vector
    def _(dve):
        v = nc.vector
        steps = Steps(dve, s_step)
        dve.wait_ge(s_words, 32)
        for o in (BY_DST, BY_SRC):
            code = m.code[o]
            steps.inc(v.tensor_scalar(m.edge_no[o][:, :], words[o][:, 1:T + 1], 2 ** ID_BITS - 1, None, ALU.bitwise_and))
            steps.link(v.tensor_scalar(code_i[:, :], words[o][:, :], ID_BITS, None, ALU.logical_shift_right))
            steps.inc(v.tensor_scalar(edge_f[:, :], m.edge_no[o][:, :], float(E - 1), None, ALU.min))
            steps.link(v.tensor_copy(code[:, :], code_i[:, :]))
            v.tensor_copy(m.edge_no[o][:, :], edge_f[:, :]).then_inc(s_ids, 1)
            dve.wait_ge(s_ids, o + 1)
            steps.link(v.tensor_scalar(row_f[:, :], code[:, 1:T + 1], float(2 ** 16), float(-(2 ** 16 + HALF)), ALU.is_ge, ALU.mult))
            steps.link(v.scalar_tensor_tensor(node_f[:, :], code[:, 1:T + 1], float(HALF - CODE), row_f[:, :], ALU.add, ALU.add))
            own = m.dst_idx[o] if o == BY_DST else m.src_idx[o]
            steps.inc(v.tensor_scalar(own[:, :], node_f[:, :], float(N - 1), None, ALU.min))
            steps.inc(v.tensor_tensor(m.same[o][:, :], code[:, 0:T + 1], code[:, 1:T + 2], ALU.is_equal))
            steps.inc(v.tensor_tensor(m.tail[o][:, :, 0], code[:, 1:T + 1], code[:, 2:T + 2], ALU.not_equal))
            steps.inc(v.tensor_scalar(not_pad[:, :], code[:, 1:T + 1], float(PAD_CODE), None, ALU.not_equal))
            steps.inc(v.tensor_scalar(m.first[o][:, :, 0], code[:, 1:T + 1], code[:, 1:2], None, ALU.is_equal))
            steps.inc(v.tensor_scalar(m.last[o][:, :, 0], code[:, 1:T + 1], code[:, T:T + 1], None, ALU.is_equal))
            steps.inc(v.tensor_scalar(end_rows[:, :], m.ident[:, :], 0.0, code[:, 1:2], ALU.mult, ALU.add))
            steps.wait()
            v.tensor_tensor(m.tail[o][:, :, 0], m.tail[o][:, :, 0], not_pad[:, :], ALU.mult).then_inc(s_row, 1)
            dve.wait_ge(s_row, o + 1)
            steps.link(v.tensor_scalar(row_f[:, :], m.tail[o][:, :, 0], float(-OUT_OF_RANGE), float(OUT_OF_RANGE), ALU.mult, ALU.add))
            steps.link(v.tensor_tensor(m.tail_idx[o][:, :], row_f[:, :], node_f[:, :], ALU.add))
            dve.wait_ge(s_rowt, o + 1)
            if o == 0:
                dve.wait_ge(s_upper, 2)
            steps.link(v.tensor_scalar(m.before[o][:, :], row_end[:, :], code[:, T:T + 1], None, ALU.is_equal))
            v.tensor_tensor(m.before[o][:, :], m.before[o][:, :], upper[:, :], ALU.mult).then_inc(s_bef, 1)
            dve.wait_ge(s_beft, o + 1)
            steps.link(v.tensor_copy(m.after[o][:, :], before_t[:, :]))
        steps.link(v.memset(ones_row[:, :], 1.0))
        v.tensor_tensor_scan(count[:, :], m.same[BY_SRC][:, 0:T], ones_row[:, :], 0.0, ALU.mult, ALU.add).then_inc(s_count, 1)
        dve.wait_ge(s_counted, 1)
        v.scalar_tensor_tensor(count[:, :], m.first[BY_SRC][:, :, 0], count_ps[:, 0:1], count[:, :], ALU.mult,
                               ALU.add).then_inc(s_count, 1)
        dve.wait_ge(s_root, 1)
        steps.link(v.reciprocal(m.dinv_src[:, :, 0], root[:, :]))

    @block.scalar
    def _(act):
        act.wait_ge(s_count, 2)
        nc.scalar.activation(root[:, :], count[:, :], ACT.Sqrt).then_inc(s_root, 1)

    @block.tensor
    def _(pe):
        for o in (BY_DST, BY_SRC):
            pe.wait_ge(s_row, o + 1)
            nc.tensor.transpose(row_end[:, :], end_rows[:, :], m.ident[:, :]).then_inc(s_rowt, 1)
            pe.wait_ge(s_bef, o + 1)
            nc.tensor.transpose(before_t[:, :], m.before[o][:, :], m.ident[:, :]).then_inc(s_beft, 1)
        pe.wait_ge(s_count, 1)
        nc.tensor.matmul(count_ps[:, 0:1], m.before[BY_SRC][:, :], count[:, T - 1:T], start=True, stop=True).then_inc(s_counted, 1)


def load_weights(nc, m, w, ctx, block):
    def sb(name, shape, dt=F32):
        return ctx.enter_context(nc.sbuf_tensor(name, shape, dt))

    wv, mix = sb("wv", [D, D]), m.mix
    wk_rows, wq_rows = sb("wk_rows", [D, D]), sb("wq_rows", [D, D])
    bv, bq, bk, rel = (sb(n, [D, 1]) for n in ("bv", "bq", "bk", "rel"))
    bq_rel, bk_heads = sb("bq_rel", [D, 2, H]), sb("bk_heads", [D, H])
    w3t, a_src, a_dst = sb("w3t", [D, D]), sb("a_src", [D, 1]), sb("a_dst", [D, 1])
    a_wide, bv_wide, bk_wide = sb("a_wide", [D, 1, P]), sb("bv_wide", [D, P]), sb("bk_wide", [D, P])
    base = sb("base", [D, D])
    spline = sb("spline", [D, SPLINES, D])
    prod = ctx.enter_context(nc.psum_tensor("weight_products", [P, 4 * D], F32))
    small = ctx.enter_context(nc.psum_tensor("small_products", [P, 512], F32))
    s_in, s_step, s_wide, s_prod, s_mix = (
        m.sem(n) for n in ("weights_in", "weight_step", "a_wide_made", "products", "mix_in"))
    rows = [(m.b0, w["b0"]), (m.b2, w["b2"])]
    columns = [(bv, w["bv"]), (bq, w["bq"]), (bk, w["bk"]), (rel, w["rel"])]
    whole = [(m.w0, w["w0"]), (m.w_key[:, 0:D], w["wk"]), (m.w_query[:, 0:D], w["wq"]), (m.w2, w["w2"]), (wv, w["wv"]), (w3t, w["w3t"]),
             (wk_rows, w["wk_rows"]), (wq_rows, w["wq_rows"])]
    n_in = len(rows) + len(columns) + len(whole) + 6

    @block.sync
    def _(sp):
        for out, row in rows:
            sp.dma_start(out[:, 0, :], row.partition_broadcast(P)).then_inc(s_in, 16)
        for out, mat in whole:
            sp.dma_start(out[:, :], mat).then_inc(s_in, 16)
        for out, column in columns:
            sp.dma_start(out[:, :], column.rearrange("(d a) -> d a", a=1)).then_inc(s_in, 16)
        sp.dma_start(a_src[:, :], w["a"][0:D, :]).then_inc(s_in, 16)
        sp.dma_start(a_dst[:, :], w["a"][D:2 * D, :]).then_inc(s_in, 16)
        sp.dma_start(base[:, :], w["base"]).then_inc(s_in, 16)
        sp.dma_start(spline[:, :, :], w["spline"].rearrange("c i o -> i c o")).then_inc(s_in, 16)
        sp.dma_start(m.gamma_beta[0:1, 0:D], w["gamma"].rearrange("(a d) -> a d", a=1)).then_inc(s_in, 16)
        sp.dma_start(m.gamma_beta[0:1, D:2 * D], w["beta"].rearrange("(a d) -> a d", a=1)).then_inc(s_in, 16)
        for h in range(H):
            sp.dma_start(mix[h * DK:(h + 1) * DK, h * DK:(h + 1) * DK], w["rel_msg"][h, :, :]).then_inc(s_mix, 16)
        sp.wait_ge(s_mix, 16 * H)

    @block.tensor
    def _(pe):
        pe.wait_ge(s_in, 16 * n_in)
        pe.wait_ge(s_mix, 16 * H)
        pe.wait_ge(s_wide, 6)
        nc.tensor.matmul(prod[:, 0:D], wv[:, :], mix[:, :], start=True, stop=True)
        nc.tensor.matmul(prod[:, D:2 * D], bv_wide[:, :], mix[:, :], start=True, stop=True)
        nc.tensor.matmul(prod[:, 2 * D:3 * D], a_wide[:, 0, :], w3t[:, :], start=True, stop=True)
        nc.tensor.matmul(prod[:, 3 * D:3 * D + 1], w3t[:, :], a_dst[:, 0:1], start=True, stop=True)
        both = bq_rel[:, :, :].rearrange("d n h -> d (n h)")
        nc.tensor.matmul(small[:, 0:2 * H], wk_rows[:, :], both, start=True, stop=True)
        nc.tensor.matmul(small[:, 2 * H:4 * H], bk_wide[:, :], both, start=True, stop=True)
        nc.tensor.matmul(small[:, 4 * H:5 * H], wq_rows[:, :], bk_heads[:, :], start=True, stop=True).then_inc(s_prod, 1)

    @block.vector
    def _(dve):
        v = nc.vector
        steps = Steps(dve, s_step)
        dve.wait_ge(s_in, 16 * n_in)
        v.tensor_scalar(a_wide[:, 0, :], m.ones[:, :], a_src[:, 0:1], None, ALU.mult).then_inc(s_wide, 1)
        v.tensor_scalar(bv_wide[:, :], m.ones[:, :], bv[:, 0:1], None, ALU.mult).then_inc(s_wide, 1)
        v.tensor_scalar(bk_wide[:, :], m.ones[:, :], bk[:, 0:1], None, ALU.mult).then_inc(s_wide, 1)
        v.tensor_scalar(bq_rel[:, 0, :], m.in_head[:, :], bq[:, 0:1], None, ALU.mult).then_inc(s_wide, 1)
        v.tensor_scalar(bq_rel[:, 1, :], m.in_head[:, :], rel[:, 0:1], None, ALU.mult).then_inc(s_wide, 1)
        v.tensor_scalar(bk_heads[:, :], m.in_head[:, :], bk[:, 0:1], None, ALU.mult).then_inc(s_wide, 1)
        steps.inc(v.tensor_scalar(m.rb0[:, :, :], m.b0[:, :, :], 0.0, None, ALU.max))
        steps.inc(v.tensor_scalar(m.rb2[:, :, :], m.b2[:, :, :], 0.0, None, ALU.max))
        steps.inc(v.tensor_scalar(m.w_kan[:, 0, :], base[:, :], 0.5, None, ALU.mult))
        choose = (1, -4, 6, -4, 1)
        for n in range(KNOTS):
            knot = n + 6
            terms = [(j, choose[knot - j] / 6.0 / GRID_STEP ** 3 * (-1 if n < DVE_KNOTS else 1)) for j in range(max(0, knot - 4), min(SPLINES, knot + 1))]
            for at, (j, c) in enumerate(terms):
                if at == 0:
                    steps.link(v.tensor_scalar(m.w_kan[:, 1 + n, :], spline[:, j, :], c, None, ALU.mult))
                else:
                    steps.link(v.scalar_tensor_tensor(m.w_kan[:, 1 + n, :], spline[:, j, :], c, m.w_kan[:, 1 + n, :],
                                                      ALU.mult, ALU.add))
        dve.wait_ge(s_prod, 1)
        steps.inc(v.tensor_copy(m.w_value[:, :], prod[:, 0:D]))
        steps.inc(v.tensor_copy(m.bv[:, 0, :], prod[:, D:2 * D]))
        steps.inc(v.tensor_copy(m.w_key[:, D:], small[:, 0:2 * H]))
        steps.inc(v.tensor_copy(m.bk_bq_rel[:, :, :], small[:, 2 * H:4 * H].rearrange("p (n h) -> p n h", h=H)))
        steps.inc(v.tensor_copy(m.w_query[:, D:], small[:, 4 * H:5 * H]))
        steps.inc(v.tensor_copy(m.to_src[:, 0, :], prod[:, 2 * D:3 * D]))
        steps.inc(v.tensor_copy(m.to_dst[:, :], prod[:, 3 * D:3 * D + 1]))
        steps.wait()


def stage_columns(pool, nc, m, stage, idx, i, slot, s_stage, count):
    nc.gpsimd.tensor_copy(stage[slot][:, :], idx[:, group(i, slot)]).then_inc(s_stage, 1)
    hold(pool, m.passed, s_stage, count)


def stage_group(pool, nc, m, stage, idx, g, s_stage):
    nc.gpsimd.tensor_copy(stage[:, :], idx[:, group_of(g)]).then_inc(s_stage, 1)
    hold(pool, m.passed, s_stage, g + 1)


def gather(pool, out, table, stage, sem):
    for k in range(G):
        pool.indirect_dma_start(out[:, k, :], None, table,
                                bass.IndirectOffsetOnAxis(ap=stage[:, k:k + 1], axis=0)).then_inc(sem, 16)


def scatter(pool, table, rows, stage, sem):
    for k in range(G):
        pool.indirect_dma_start(table, bass.IndirectOffsetOnAxis(ap=stage[:, k:k + 1], axis=0), rows[:, k, :], None,
                                bounds_check=N - 1, oob_is_err=False).then_inc(sem, 16)


def row_stats(v, m, steps, rows, n, stats, mean_var):
    for k in range(n):
        steps.inc(v.bn_stats(stats[:, k, :], rows[:, k, :]))
    steps.hold(m.passed)
    for k in range(n - 1):
        steps.inc(v.bn_aggr(mean_var[:, k, :], stats[:, k, :]))
    return v.bn_aggr(mean_var[:, n - 1, :], stats[:, n - 1, :])


def norm_rows(v, steps, mean_var, work, rstd, shift):
    half, y = work[:, 0, :], rstd
    steps.inc(v.tensor_scalar(half, mean_var[:, :, 1], -0.5, -0.5 * EPS, ALU.mult, ALU.add))
    steps.link(v.tensor_scalar(y, mean_var[:, :, 1], EPS, None, ALU.add))
    steps.link(v.tensor_scalar(y.bitcast(I32), y.bitcast(I32), 1, None, ALU.logical_shift_right))
    steps.link(v.tensor_scalar(y.bitcast(I32), y.bitcast(I32), -1.0, float(0x5f3759df), ALU.mult, ALU.add))
    for _ in range(3):
        steps.link(v.tensor_tensor(work[:, 1, :], y, y, ALU.mult))
        steps.link(v.tensor_tensor(work[:, 1, :], work[:, 1, :], half, ALU.mult))
        steps.link(v.scalar_tensor_tensor(y, work[:, 1, :], 1.5, y, ALU.add, ALU.mult))
    return v.scalar_tensor_tensor(shift, mean_var[:, :, 0], -1.0, y, ALU.mult, ALU.mult)


def sum_source_rows(nc, m, x):
    with ExitStack() as ctx:
        def sb(name, shape, dt=F32):
            return ctx.enter_context(nc.sbuf_tensor(name, shape, dt))

        o = BY_DST
        slots = range(DEEP)
        stage = [sb(f"l0_stage{i}", [P, G], I32) for i in slots]
        got = [sb(f"l0_got{i}", [P, G, D]) for i in slots]
        h = [sb(f"l0_h{i}", [P, G, D]) for i in (0, 1)]
        same_g = [sb(f"l0_same{i}", [P, G]) for i in (0, 1)]
        stats, mv, rstd, shift = sb("l0_stats", [P, G, 6]), [sb(f"l0_mv{i}", [P, G, 2]) for i in (0, 1)], \
            [sb(f"l0_rstd{i}", [P, G, 1]) for i in (0, 1)], [sb(f"l0_shift{i}", [P, G, 1]) for i in (0, 1)]
        work = sb("l0_work", [P, 2, G])
        s_stage, s_step, s_norm, s_h, s_sum, s_kept = (
            m.sem("l0_" + n) for n in ("staged", "step", "norm", "h", "summed", "kept"))
        s_got = [m.lasting_sem(f"l0_rows_in{i}") for i in slots]
        s_stored = [m.sem(f"l0_rows_stored{i}") for i in slots]
        block = ctx.enter_context(nc.Block())

        @block.gpsimd
        def _(pool):
            def body(i, first):
                for slot in slots:
                    g = i * DEEP + slot
                    if not first:
                        hold(pool, m.passed, s_h, g - 3)
                        hold(pool, m.passed, s_stored[slot], i * 16)
                    stage_group(pool, nc, m, stage[slot], m.src_idx[o], g, s_stage)
                    gather(pool, got[slot], x, stage[slot], s_got[slot])
            turns(pool, body, count=FOURS)

        @block.sync
        def _(sp):
            with sp.Fori(0, FOURS) as i:
                for slot in slots:
                    sp.wait_ge(s_got[slot], i * (16 * G) + 16 * G)
                    sp.dma_start(m.x_src[:, group_of(i * DEEP + slot), :], got[slot][:, :, :]).then_inc(s_stored[slot], 16)
            for slot in slots:
                sp.wait_ge(s_stored[slot], 16 * FOURS)

        @block.scalar
        def _(act):
            def body(i, first):
                for slot in slots:
                    g = i * DEEP + slot
                    act.wait_ge(s_norm, g + 1)
                    if not (first and slot == 0):
                        act.wait_ge(s_sum, g)
                    if not (first and slot < 2):
                        act.wait_ge(s_kept, g - 1)
                    for k in range(G):
                        ins = nc.scalar.activation(h[slot % 2][:, k, :], got[slot][:, k, :], ACT.Relu,
                                                   bias=shift[slot % 2][:, k, :], scale=rstd[slot % 2][:, k, :])
                    ins.then_inc(s_h, 1)
                    if not (first and slot == 0):
                        keep(g - 1, (slot - 1) % DEEP)

            def keep(g, slot):
                act.wait_ge(s_sum, g + 1)
                nc.scalar.copy(m.rows[:, group_of(g), :], h[slot % 2][:, :, :]).then_inc(s_kept, 1)
            turns(act, body, count=FOURS)
            keep(NG - 1, DEEP - 1)

        @block.vector
        def _(dve):
            v = nc.vector
            steps = Steps(dve, s_step)

            def normalise(i, slot):
                g = i * DEEP + slot
                dve.wait_ge(s_got[slot], i * (16 * G) + 16 * G)
                steps.link(row_stats(v, m, steps, got[slot], G, stats, mv[slot % 2]))
                steps.inc(v.tensor_copy(same_g[slot % 2][:, :], m.same[o][:, group_of(i * DEEP + slot)]))
                norm_rows(v, steps, mv[slot % 2], work, rstd[slot % 2][:, :, 0], shift[slot % 2][:, :, 0]).then_inc(s_norm, 1)

            def sums(g, slot):
                dve.wait_ge(s_h, g + 1)
                for k in range(G):
                    if k == 0 and is_first(g):
                        continue
                    before = h[slot % 2][:, k - 1, :] if k else h[1 - slot % 2][:, G - 1, :]
                    ins = v.scalar_tensor_tensor(h[slot % 2][:, k, :], before, same_g[slot % 2][:, k:k + 1], h[slot % 2][:, k, :],
                                                 ALU.mult, ALU.add)
                    if k < G - 1:
                        steps.link(ins)
                    else:
                        ins.then_inc(s_sum, 1)
                        dve.wait_ge(s_sum, g + 1)

            def body(i, first):
                for slot in slots:
                    normalise(i, slot)
                    if not (first and slot == 0):
                        sums(i * DEEP + (slot - 1), (slot - 1) % DEEP)
            turns(dve, body, steps, DEEP * (3 * G + 13), count=FOURS)
            sums(NG - 1, DEEP - 1)


def value_slots(m, ctx, name):
    stage = [ctx.enter_context(m.nc.sbuf_tensor(f"{name}numbers{i}", [P, G], I32)) for i in (0, 1)]
    value = [ctx.enter_context(m.nc.sbuf_tensor(f"{name}value{i}", [P, G], F32)) for i in (0, 1)]
    return stage, value, m.sem(name + "staged"), m.sem(name + "copied"), [m.lasting_sem(f"{name}moved{i}") for i in (0, 1)]


def put_dinv(nc, m, pool, i, slot, first, slots):
    stage, value, s_stage, s_value, s_moved = slots
    g = i * 2 + slot
    if not first:
        hold(pool, m.passed, s_moved[slot], i * (16 * G))
    nc.gpsimd.tensor_copy(value[slot][:, :], m.dinv_src[:, group(i, slot), 0]).then_inc(s_value, 1)
    hold(pool, m.passed, s_value, g + 1)
    stage_columns(pool, nc, m, stage, m.tail_idx[BY_SRC], i, slot, s_stage, g + 1)
    for k in range(G):
        pool.indirect_dma_start(m.dinv_table, bass.IndirectOffsetOnAxis(ap=stage[slot][:, k:k + 1], axis=0),
                                value[slot][:, k:k + 1], None, bounds_check=N - 1, oob_is_err=False).then_inc(s_moved[slot], 16)


def get_dinv(nc, m, pool, slots):
    stage, value, s_stage, s_copied, s_moved = slots

    def body(i, first):
        for slot in (0, 1):
            g = i * 2 + slot
            if not first:
                hold(pool, m.passed, s_copied, g - 1)
            stage_columns(pool, nc, m, stage, m.dst_idx[BY_SRC], i, slot, s_stage, g + 1)
            for k in range(G):
                pool.indirect_dma_start(value[slot][:, k:k + 1], None, m.dinv_table,
                                        bass.IndirectOffsetOnAxis(ap=stage[slot][:, k:k + 1], axis=0)).then_inc(s_moved[slot], 16)
            if not (first and slot == 0):
                take(i - (1 - slot), 1 - slot)

    def take(i, slot):
        hold(pool, m.passed, s_moved[slot], i * (16 * G) + 16 * G)
        nc.gpsimd.tensor_copy(m.dinv_dst[:, group(i, slot), 0], value[slot][:, :]).then_inc(s_copied, 1)
    turns(pool, body)
    take(PAIRS - 1, 1)
    pool.wait_ge(s_copied, NG)


def transform_sums0(nc, m, x):
    with ExitStack() as ctx:
        def sb(nm, shape, dt=F32):
            return ctx.enter_context(nc.sbuf_tensor("t0_" + nm, shape, dt))

        def two(nm, shape, dt=F32):
            return [sb(f"{nm}{i}", shape, dt) for i in (0, 1)]

        def psum(nm, cols):
            return ctx.enter_context(nc.psum_tensor("t0_" + nm, [P, cols], F32))

        def sem(nm):
            return m.sem("t0_" + nm)

        o = BY_DST
        numbers = two("numbers", [P, G], I32)
        u, d, sq, uts = two("u", [P, G, D]), two("d", [P, G, D]), two("sq", [P, G, D]), two("uts", [P, G * D])
        fix, tmp, zero_row = sb("fix", [P, G, D]), sb("tmp", [P, G, D]), sb("zero_row", [1, 2 * D])
        ut, z, carry_ps, sums_ps = [psum(f"ut{i}", 8 * D) for i in (0, 1)], psum("z", 8 * D), psum("carry", 512), psum("sums", 512)
        s_numbers, s_step, s_carry, s_u, s_turned, s_uts, s_z, s_d, s_kept, s_square, s_sums, s_zero_row = (
            sem(n) for n in ("numbers_staged", "step", "carry_made", "u_made", "u_turned", "uts_made",
                             "z_made", "d_made", "d_kept", "squared", "summed", "zero_row_made"))
        s_scat = [m.lasting_sem(f"t0_scattered{i}") for i in (0, 1)]
        zeros = sb("zeros", [P, ZERO_ROWS * D])
        s_zero, s_zeroed = sem("zeros_made"), sem("table_zeroed")
        block = ctx.enter_context(nc.Block())

        @block.sync
        def _(sp):
            sp.wait_ge(s_zero, 1)
            zero_h2_table(sp, m, zeros, 0, s_u, s_zeroed)

        @block.gpsimd
        def _(pool):
            nc.gpsimd.memset(zeros[:, :], 0.0).then_inc(s_zero, 1)

            def body(i, first):
                for slot in (0, 1):
                    g = i * 2 + slot
                    if not first:
                        hold(pool, m.passed, s_scat[slot], i * (16 * G))
                    stage_columns(pool, nc, m, numbers, m.tail_idx[o], i, slot, s_numbers, g + 1)
                    hold(pool, m.passed, s_d, g + 1)
                    scatter(pool, m.h0_table, d[slot], numbers[slot], s_scat[slot])
            turns(pool, body)
            for slot in (0, 1):
                pool.wait_ge(s_scat[slot], 16 * G * PAIRS)

        @block.tensor
        def _(pe):
            nc.tensor.matmul(carry_ps[:, 0:D], m.before[o][:, :], m.rows[:, T - 1, :], start=True, stop=True).then_inc(s_carry, 1)
            pe.wait_ge(s_zero_row, 1)
            nc.tensor.matmul(sums_ps[0:1, 0:2 * D], m.ones[0:1, 0:1], zero_row[0:1, :], start=True, stop=False)

            def body(i, first):
                for slot in (0, 1):
                    g = i * 2 + slot
                    pe.wait_ge(s_u, g + 1)
                    for k in range(G):
                        ins = nc.tensor.transpose(ut[slot][:, k * D:(k + 1) * D], u[slot][:, k, :], m.ident[:, :])
                    ins.then_inc(s_turned, 1)
                    pe.wait_ge(s_uts, g + 1)
                    if not (first and slot == 0):
                        pe.wait_ge(s_d, g)
                    for k in range(G):
                        ins = nc.tensor.matmul(z[:, k * D:(k + 1) * D], uts[slot][:, k * D:(k + 1) * D], m.w0[:, :],
                                               start=True, stop=True)
                    ins.then_inc(s_z, 1)
                    if not (first and slot == 0):
                        sum_up(1 - slot, g)

            def sum_up(slot, count):
                pe.wait_ge(s_square, count)
                for k in range(G):
                    nc.tensor.matmul(sums_ps[0:1, 0:D], m.ones[:, 0:1], d[slot][:, k, :], start=False, stop=False)
                    ins = nc.tensor.matmul(sums_ps[0:1, D:2 * D], m.ones[:, 0:1], sq[slot][:, k, :], start=False, stop=False)
                ins.then_inc(s_sums, 1)
            turns(pe, body)
            sum_up(1, NG)
            nc.tensor.matmul(sums_ps[0:1, 0:2 * D], m.ones[0:1, 0:1], zero_row[0:1, :], start=False, stop=True).then_inc(s_sums, 1)

        @block.scalar
        def _(act):
            def body(i, first):
                for slot in (0, 1):
                    g = i * 2 + slot
                    act.wait_ge(s_turned, g + 1)
                    nc.scalar.activation(uts[slot][:, :], ut[slot][:, 0:G * D], ACT.Copy).then_inc(s_uts, 1)
                    if not (first and slot == 0):
                        keep(i - (1 - slot), 1 - slot, g)

            def keep(i, slot, count):
                act.wait_ge(s_d, count)
                if not is_first(i):
                    act.wait_ge(s_sums, count - 2)
                nc.scalar.activation(sq[slot][:, :, :], d[slot][:, :, :], ACT.Square).then_inc(s_square, 1)
                nc.scalar.activation(m.rows[:, group(i, slot), :], d[slot][:, :, :], ACT.Copy).then_inc(s_kept, 1)
            turns(act, body, peeled=2)
            keep(PAIRS - 1, 1, NG)

        @block.vector
        def _(dve):
            v = nc.vector
            steps = Steps(dve, s_step)
            v.memset(zero_row[:, :], 0.0).then_inc(s_zero_row, 1)
            dve.wait_ge(s_carry, 1)
            steps.link(v.tensor_copy(m.carry[:, 0, :], carry_ps[:, 0:D]))

            def sums(i, slot, count):
                steps.link(v.tensor_tensor(fix[:, :, :], m.carry[:, :, :].to_broadcast([P, G, D]),
                                           m.first[o][:, group(i, slot), :].to_broadcast([P, G, D]), ALU.mult))
                v.tensor_tensor(u[slot][:, :, :], fix[:, :, :], m.rows[:, group(i, slot), :], ALU.add).then_inc(s_u, 1)
                dve.wait_ge(s_u, count)

            def rows(i, slot, count):
                dve.wait_ge(s_z, count)
                z3 = z[:, 0:G * D].rearrange("p (g d) -> p g d", d=D)
                steps.link(v.tensor_tensor(tmp[:, :, :], z3, m.b0[:, :, :].to_broadcast([P, G, D]), ALU.add))
                steps.link(v.scalar_tensor_tensor(tmp[:, :, :], tmp[:, :, :], 0.0, m.rb0[:, :, :].to_broadcast([P, G, D]),
                                                  ALU.max, ALU.subtract))
                if not is_first(i):
                    dve.wait_ge(s_scat[slot], i * (16 * G))
                    dve.wait_ge(s_sums, count - 2)
                    dve.wait_ge(s_kept, count - 2)
                v.tensor_tensor(d[slot][:, :, :], tmp[:, :, :], m.tail[o][:, group(i, slot), :].to_broadcast([P, G, D]),
                                ALU.mult).then_inc(s_d, 1)
                dve.wait_ge(s_d, count)

            def body(i, first):
                for slot in (0, 1):
                    sums(i, slot, i * 2 + (slot + 1))
                    if not (first and slot == 0):
                        rows(i - (1 - slot), 1 - slot, i * 2 + slot)
            turns(dve, body, steps, 2 * 3, peeled=2)
            rows(PAIRS - 1, 1, NG)
            dve.wait_ge(s_sums, NG + 1)
            steps.link(v.tensor_scalar(m.totals[0:1, 0:2 * D], sums_ps[0:1, 0:2 * D], 1.0 / N, None, ALU.mult))


def batch_norm_rows(nc, m):
    with ExitStack() as ctx:
        work = [ctx.enter_context(nc.sbuf_tensor(f"bn_work{i}", [1, D], F32)) for i in range(4)]
        both = ctx.enter_context(nc.sbuf_tensor("bn_both", [1, 2 * D], F32))
        wide = ctx.enter_context(nc.psum_tensor("bn_wide", [P, 2 * D], F32))
        s_step, s_var, s_std, s_both, s_wide = (m.sem("bn_" + n) for n in ("step", "var", "std", "both", "wide"))
        mean, square = m.totals[0:1, 0:D], m.totals[0:1, D:2 * D]
        block = ctx.enter_context(nc.Block())

        @block.vector
        def _(dve):
            v = nc.vector
            steps = Steps(dve, s_step)
            steps.link(v.tensor_tensor(work[0][:, :], mean, mean, ALU.mult))
            steps.link(v.tensor_tensor(work[1][:, :], square, work[0][:, :], ALU.subtract))
            v.tensor_scalar(work[1][:, :], work[1][:, :], 0.0, None, ALU.max).then_inc(s_var, 1)
            dve.wait_ge(s_std, 1)
            steps.link(v.reciprocal(work[3][:, :], work[2][:, :]))
            steps.link(v.tensor_tensor(both[:, 0:D], work[3][:, :], m.gamma_beta[0:1, 0:D], ALU.mult))
            steps.link(v.tensor_tensor(work[0][:, :], both[:, 0:D], mean, ALU.mult))
            v.tensor_tensor(both[:, D:2 * D], m.gamma_beta[0:1, D:2 * D], work[0][:, :], ALU.subtract).then_inc(s_both, 1)
            dve.wait_ge(s_wide, 1)
            steps.inc(v.tensor_copy(m.scale0[:, 0, :], wide[:, 0:D]))
            steps.inc(v.tensor_copy(m.shift0[:, 0, :], wide[:, D:2 * D]))
            steps.wait()

        @block.scalar
        def _(act):
            act.wait_ge(s_var, 1)
            nc.scalar.activation(work[2][:, :], work[1][:, :], ACT.Sqrt, bias=m.epsilon[0:1, 0:1]).then_inc(s_std, 1)

        @block.tensor
        def _(pe):
            pe.wait_ge(s_both, 1)
            nc.tensor.matmul(wide[:, :], m.ones[0:1, 0:P], both[0:1, :], start=True, stop=True).then_inc(s_wide, 1)


def dense_pass(nc, m, x, out, records):
    with ExitStack() as ctx:
        def sb(nm, shape, dt=F32):
            return ctx.enter_context(nc.sbuf_tensor("dense_" + nm, shape, dt))

        def sem(nm):
            return m.sem("dense_" + nm)

        xin, xout = [sb(f"in{i}", [P, BULK_ROWS, D]) for i in (0, 1)], [sb(f"out{i}", [P, BULK_ROWS, D]) for i in (0, 1)]
        rest_in, rest_out = sb("rest_in", [N - BULK_MAIN, D]), sb("rest_out", [N - BULK_MAIN, D])
        base = sb("base", [P, 1, D])
        tmp = sb("tmp", [P, G, D])
        carry_ps = ctx.enter_context(nc.psum_tensor("dense_carry", [P, 512], F32))
        s_in, s_out = [sem(f"rows_in{i}") for i in (0, 1)], [sem(f"rows_out{i}") for i in (0, 1)]
        s_sum, s_step, s_rest, s_rest_in, s_rest_out, s_spread, s_carry = (
            sem(n) for n in ("summed", "step", "rest_summed", "rest_in", "rest_out", "spread", "carry"))
        fetch = record_slots(m, ctx, "rec1_")
        numbers, xd = [sb(f"numbers{i}", [P, G], I32) for i in (0, 1)], [sb(f"xd{i}", [P, G, D]) for i in (0, 1)]
        s_numbers, s_xd = sem("numbers_staged"), [m.lasting_sem(f"dense_xd_in{i}") for i in (0, 1)]
        s_stored = [sem(f"xd_stored{i}") for i in (0, 1)]
        x3, out3 = (t[0:BULK_MAIN, :].rearrange("(p r) d -> p r d", p=P) for t in (x, out))
        block = ctx.enter_context(nc.Block())
        last = (2 * BULK_TURNS - 1) * BULK_ROWS

        @block.sync
        def _(sp):
            sp.dma_start(rest_in[:, :], x[BULK_MAIN:N, :]).then_inc(s_rest_in, 16)
            sp.dma_start(xin[0][:, :, :], x3[:, 0:BULK_ROWS, :]).then_inc(s_in[0], 16)
            sp.dma_start(xin[1][:, :, :], x3[:, BULK_ROWS:2 * BULK_ROWS, :]).then_inc(s_in[1], 16)
            def load(i, slot):
                sp.wait_ge(s_sum, i * 2 + (slot - 1))
                sp.dma_start(xin[slot][:, :, :], x3[:, bass.ds((i * 2 + slot) * BULK_ROWS, BULK_ROWS), :]).then_inc(s_in[slot], 16)

            with sp.Fori(1, BULK_TURNS - 1) as i:
                for slot in (0, 1):
                    load(i, slot)
            load(BULK_TURNS - 1, 0)
            sp.wait_ge(s_sum, 2 * BULK_TURNS - 2)
            sp.dma_start(xin[1][:, 0:LAST_ROWS, :], x3[:, last:, :]).then_inc(s_in[1], 16)

        @block.scalar
        def _(act):
            def store(i, slot):
                act.wait_ge(s_sum, i * 2 + (slot + 1))
                act.dma_start(out3[:, bass.ds((i * 2 + slot) * BULK_ROWS, BULK_ROWS), :], xout[slot][:, :, :]).then_inc(s_out[slot], 16)

            with act.Fori(0, PAIRS) as i:
                for slot in (0, 1):
                    store(i, slot)
                    act.wait_ge(s_xd[slot], i * (16 * G) + 16 * G)
                    act.dma_start(chunk(m.x_dst, i, slot), xd[slot][:, :, :]).then_inc(s_stored[slot], 16)
            with act.Fori(PAIRS, BULK_TURNS - 1) as i:
                for slot in (0, 1):
                    store(i, slot)
            store(BULK_TURNS - 1, 0)
            for slot in (0, 1):
                act.wait_ge(s_stored[slot], 16 * PAIRS)
            act.wait_ge(s_sum, 2 * BULK_TURNS)
            act.dma_start(out3[:, last:, :], xout[1][:, 0:LAST_ROWS, :]).then_inc(s_out[1], 16)
            act.wait_ge(s_rest, 1)
            act.dma_start(out[BULK_MAIN:N, :], rest_out[:, :]).then_inc(s_rest_out, 16)
            for slot in (0, 1):
                act.wait_ge(s_out[slot], 16 * BULK_TURNS)
            act.wait_ge(s_rest_out, 16)

        @block.tensor
        def _(pe):
            pe.wait_ge(s_spread, 1)
            nc.tensor.matmul(carry_ps[:, 0:D], m.after[BY_DST][:, :], m.rows[:, 0, :], start=True, stop=True).then_inc(s_carry, 1)

        @block.gpsimd
        def _(pool):
            def body(i, first):
                for slot in (0, 1):
                    if not first:
                        hold(pool, m.passed, s_stored[slot], i * 16)
                    stage_columns(pool, nc, m, numbers, m.dst_idx[BY_DST], i, slot, s_numbers, i * 2 + slot + 1)
                    gather(pool, xd[slot], x, numbers[slot], s_xd[slot])
            turns(pool, body)
            fetch_records(nc, m, pool, BY_SRC, records, fetch)

        @block.vector
        def _(dve):
            v = nc.vector
            steps = Steps(dve, s_step)
            steps.link(v.tensor_tensor(base[:, :, :], m.shift0[:, :, :], m.rb2[:, :, :], ALU.add))

            def add(slot, n=BULK_ROWS):
                v.tensor_tensor(xout[slot][:, 0:n, :], xin[slot][:, 0:n, :], base[:, :, :].to_broadcast([P, n, D]),
                                ALU.add).then_inc(s_sum, 1)

            def add_next(i, slot, n=BULK_ROWS):
                dve.wait_ge(s_in[slot], i * 16 + 16)
                dve.wait_ge(s_out[slot], i * 16)
                add(slot, n)

            dve.wait_ge(s_rest_in, 16)
            v.tensor_tensor(rest_out[:, :], rest_in[:, :], base[0:N - BULK_MAIN, 0, :], ALU.add).then_inc(s_rest, 1)
            for slot in (0, 1):
                dve.wait_ge(s_in[slot], 16)
                add(slot)
            for i in range(1, 1 + BACK_TURNS):
                for slot in (0, 1):
                    add_next(i, slot)
                for t in range(T - 1 - (i - 1) * BACK_STEPS, T - 1 - i * BACK_STEPS, -1):
                    steps.link(v.scalar_tensor_tensor(m.rows[:, t - 1, :], m.rows[:, t, :], m.same[BY_DST][:, t:t + 1],
                                                      m.rows[:, t - 1, :], ALU.mult, ALU.add))
            v.nop().then_inc(s_spread, 1)
            dve.wait_ge(s_carry, 1)
            steps.link(v.tensor_copy(m.carry[:, 0, :], carry_ps[:, 0:D]))
            def fix(here):
                steps.link(v.tensor_tensor(tmp[:, :, :], m.carry[:, :, :].to_broadcast([P, G, D]),
                                           m.last[BY_DST][:, here, :].to_broadcast([P, G, D]), ALU.mult))
                steps.link(v.tensor_tensor(tmp[:, :, :], tmp[:, :, :], m.rows[:, here, :], ALU.add))
                steps.link(v.tensor_tensor(tmp[:, :, :], tmp[:, :, :], m.scale0[:, :, :].to_broadcast([P, G, D]), ALU.mult))
                steps.inc(v.tensor_tensor(m.rows[:, here, :], tmp[:, :, :], m.shift0[:, :, :].to_broadcast([P, G, D]), ALU.add))
                steps.hold(m.passed)

            with dve.Fori(1 + BACK_TURNS, BULK_TURNS - 1) as i:
                steps.base, steps.k = i * 8 + (1 + T - 8 * (1 + BACK_TURNS)), 0
                for slot in (0, 1):
                    add_next(i, slot)
                    fix(bass.ds((i * 2 + (slot - 2 * (1 + BACK_TURNS))) * G, G))
            steps.base, steps.k = 1 + T + 8 * (PAIRS - 1), 0
            for slot, n in ((0, BULK_ROWS), (1, LAST_ROWS)):
                add_next(BULK_TURNS - 1, slot, n)
                fix(slice((NG - 2 + slot) * G, (NG - 1 + slot) * G))


def attend(nc, m, scores):
    with ExitStack() as ctx:
        def sb(nm, shape, dt=F32):
            return ctx.enter_context(nc.sbuf_tensor("at_" + nm, shape, dt))

        def two(nm, shape, dt=F32):
            return [sb(f"{nm}{i}", shape, dt) for i in (0, 1)]

        def sem(nm):
            return m.sem("at_" + nm)

        o = BY_DST
        numbers = two("numbers", [P, G], I32)
        hg, xs, xd = two("hg", [P, G, D]), two("xs", [P, G, D]), two("xd", [P, G, D])
        h = sb("h", [P, 2 * G, D])
        ht = two("ht", [P, 2, G * D])
        qk, few, dots = sb("qk", [P, G, D]), sb("few", [P, G, H]), sb("dots", [P, G, H])
        stats, mv, rstd, shift = (sb(n, [P, 2 * G, w]) for n, w in (("stats", 6), ("mv", 2), ("rstd", 1), ("shift", 1)))
        work = sb("work", [P, 2, 2 * G])
        turned = ctx.enter_context(nc.psum_tensor("at_turned", [P, 3, 512], F32))
        key = ctx.enter_context(nc.psum_tensor("at_key", [P, 3, 512], F32))
        value = ctx.enter_context(nc.psum_tensor("at_value", [P, 8, D], F32))
        turned_rows = turned[:, :, :].rearrange("p b c -> p (b c)")
        q_kept = sb("q_kept", [P, G, D + H])
        full = BANK_TILES * (G // BANK_TILES)

        def tile(banks, k, width):
            return banks[:, k // BANK_TILES, k % BANK_TILES * width:(k % BANK_TILES + 1) * width]

        def key_parts(rows, a, b):
            banks = key[:, 0:2, 0:BANK_TILES * (D + 2 * H)].rearrange("p b (t c) -> p b t c", c=D + 2 * H)
            return ((banks[:, :, :, a:b], rows[:, 0:full, :].rearrange("p (b t) c -> p b t c", t=BANK_TILES)),
                    (key[:, 2:3, a:b], rows[:, full:G, :]))

        s_num, s_step, s_x1, s_norm, s_h, s_turned, s_ht, s_queries, s_keys, s_q, s_used, s_scored, s_val = (
            sem(n) for n in ("numbers_staged", "step", "x1_made", "norm", "h_made", "h_turned", "ht_made",
                             "queries_made", "keys_made", "queries_kept", "keys_used", "scored", "values_kept"))
        s_hg = [m.lasting_sem(f"at_hg_in{i}") for i in (0, 1)]
        dinv = value_slots(m, ctx, "dinv0_")
        s_xs, s_xd, s_x1d = ([sem(f"{n}{i}") for i in (0, 1)] for n in ("xs_in", "xd_in", "x1d_stored"))
        block = ctx.enter_context(nc.Block())

        @block.gpsimd
        def _(pool):
            def body(i, first):
                for slot in (0, 1):
                    g = i * 2 + slot
                    if not first:
                        hold(pool, m.passed, s_h, g * 2 - 3)
                    stage_columns(pool, nc, m, numbers, m.src_idx[o], i, slot, s_num, g + 1)
                    gather(pool, hg[slot], m.h0_table, numbers[slot], s_hg[slot])
                    put_dinv(nc, m, pool, i, slot, first, dinv)
            turns(pool, body)
            for slot in (0, 1):
                pool.wait_ge(dinv[-1][slot], 16 * G * PAIRS)

        @block.sync
        def _(sp):
            def body(i, first):
                for slot in (0, 1):
                    g = i * 2 + slot
                    if not first:
                        hold(sp, m.passed, s_h, g * 2 - 2)
                        hold(sp, m.passed, s_x1d[slot], i * 16)
                    sp.dma_start(xs[slot][:, :, :], chunk(m.x_src, i, slot)).then_inc(s_xs[slot], 16)
                    sp.dma_start(xd[slot][:, :, :], chunk(m.x_dst, i, slot)).then_inc(s_xd[slot], 16)
                    if not (first and slot == 0):
                        store(i - (1 - slot), 1 - slot, g)

            def store(i, slot, count):
                sp.wait_ge(s_x1, count)
                sp.dma_start(chunk(m.x1_dst, i, slot), xd[slot][:, :, :]).then_inc(s_x1d[slot], 16)
            turns(sp, body)
            store(PAIRS - 1, 1, NG)
            for slot in (0, 1):
                sp.wait_ge(s_x1d[slot], 16 * PAIRS)

        @block.vector
        def _(dve):
            v = nc.vector
            steps = Steps(dve, s_step)
            scale, shift0 = (r[:, :, :].to_broadcast([P, G, D]) for r in (m.scale0, m.shift0))

            def normalise(i, slot, first):
                g = i * 2 + slot
                dve.wait_ge(s_hg[slot], i * (16 * G) + 16 * G)
                steps.inc(v.tensor_tensor(hg[slot][:, :, :], hg[slot][:, :, :], scale, ALU.mult))
                dve.wait_ge(s_xs[slot], i * 16 + 16)
                dve.wait_ge(s_xd[slot], i * 16 + 16)
                v.tensor_tensor(xd[slot][:, :, :], m.rows[:, group(i, slot), :], xd[slot][:, :, :], ALU.add).then_inc(s_x1, 1)
                steps.wait()
                steps.link(v.tensor_tensor(hg[slot][:, :, :], hg[slot][:, :, :], xs[slot][:, :, :], ALU.add))
                steps.link(v.tensor_tensor(hg[slot][:, :, :], hg[slot][:, :, :], shift0, ALU.add))
                dve.wait_ge(s_x1, g + 1)
                for k in range(G):
                    steps.inc(v.bn_stats(stats[:, k, :], hg[slot][:, k, :]))
                    steps.inc(v.bn_stats(stats[:, G + k, :], xd[slot][:, k, :]))
                steps.hold(m.passed)
                for k in range(2 * G):
                    ins = v.bn_aggr(mv[:, k, :], stats[:, k, :])
                    steps.inc(ins)
                steps.wait()
                if not (first and slot == 0):
                    dve.wait_ge(s_h, g * 2)
                norm_rows(v, steps, mv, work, rstd[:, :, 0], shift[:, :, 0]).then_inc(s_norm, 1)

            def score(i, slot):
                g = i * 2 + slot
                (rel_full, few_full), (rel_last, few_last) = key_parts(few, D + H, D + 2 * H)
                (bq_full, dots_full), (bq_last, dots_last) = key_parts(dots, D, D + H)
                (key_full, q_full), (key_last, q_last) = key_parts(q_kept[:, :, 0:D], 0, D)
                (_, qk_full), (_, qk_last) = key_parts(qk, 0, D)
                dve.wait_ge(s_q, g + 1)
                dve.wait_ge(s_keys, g + 1)
                steps.inc(v.tensor_tensor(qk_full, q_full, key_full, ALU.mult))
                steps.inc(v.tensor_tensor(qk_last, q_last, key_last, ALU.mult))
                steps.inc(v.tensor_copy(few_full, rel_full))
                steps.link(v.tensor_copy(few_last, rel_last))
                steps.inc(v.tensor_tensor(few[:, :, :], few[:, :, :], m.weight[:, group(i, slot), :].to_broadcast([P, G, H]), ALU.mult))
                steps.link(v.tensor_reduce(dots[:, :, :], qk[:, :, :].rearrange("p g (h c) -> p g h c", c=DK), AX.X, ALU.add))
                steps.inc(v.tensor_tensor(few[:, :, :], few[:, :, :], scores[:, group(i, slot), :], ALU.add))
                steps.inc(v.tensor_tensor(dots_full, dots_full, bq_full, ALU.add))
                v.tensor_tensor(dots_last, dots_last, bq_last, ALU.add).then_inc(s_used, 1)
                dve.wait_ge(s_used, g + 1)
                steps.wait()
                steps.link(v.tensor_tensor(dots[:, :, :], dots[:, :, :], q_kept[:, :, D:], ALU.add))
                v.tensor_tensor(scores[:, group(i, slot), :], dots[:, :, :], few[:, :, :], ALU.add).then_inc(s_scored, 1)
                dve.wait_ge(s_scored, g + 1)

            heads = [P, T, H]
            steps.link(v.tensor_tensor(scores[:, :, :], m.weight[:, :, :].to_broadcast(heads),
                                       m.bk_bq_rel[:, 1:2, :].to_broadcast(heads), ALU.mult))
            steps.link(v.tensor_tensor(scores[:, :, :], scores[:, :, :], m.bk_bq_rel[:, 0:1, :].to_broadcast(heads), ALU.add))

            def body(i, first):
                for slot in (0, 1):
                    normalise(i, slot, first)
                    if not first:
                        score(i - 1, slot)
            turns(dve, body, steps, 2 * (3 + 2 * G + 2 * G + 13 + 9))
            score(PAIRS - 1, 0)
            score(PAIRS - 1, 1)

        @block.scalar
        def _(act):
            def body(i, first):
                for slot in (0, 1):
                    g = i * 2 + slot
                    act.wait_ge(s_norm, g + 1)
                    if not (first and slot == 0):
                        act.wait_ge(s_turned, g * 2)
                    for side, rows in ((0, hg[slot]), (1, xd[slot])):
                        for k in range(G):
                            ins = nc.scalar.activation(h[:, side * G + k, :], rows[:, k, :], ACT.Relu,
                                                       bias=shift[:, side * G + k, :], scale=rstd[:, side * G + k, :])
                        ins.then_inc(s_h, 1)
                    for side in (0, 1):
                        act.wait_ge(s_turned, g * 2 + (side + 1))
                        nc.scalar.activation(ht[slot][:, side, :], turned_rows[:, 0:G * D], ACT.Copy).then_inc(s_ht, 1)
                    if not (first and slot == 0):
                        keep(i - (1 - slot), 1 - slot, g, first)

            def keep(i, slot, count, first):
                act.wait_ge(s_queries, count)
                if not first:
                    act.wait_ge(s_scored, count - 1)
                width = BANK_TILES * (D + H)
                nc.scalar.activation(q_kept[:, 0:full, :].rearrange("p (b t) c -> p b (t c)", t=BANK_TILES),
                                     turned[:, 0:2, 0:width], ACT.Copy)
                nc.scalar.activation(q_kept[:, full:G, :], turned[:, 2:3, 0:D + H], ACT.Copy).then_inc(s_q, 1)
                act.wait_ge(s_keys, count)
                nc.scalar.activation(m.rows[:, group(i, slot), :], value[:, 0:G, :], ACT.Copy).then_inc(s_val, 1)
            turns(act, body)
            keep(PAIRS - 1, 1, NG, False)

        @block.tensor
        def _(pe):
            def body(i, first):
                for slot in (0, 1):
                    g = i * 2 + slot
                    for side in (0, 1):
                        pe.wait_ge(s_h, g * 2 + (side + 1))
                        if side or (first and slot):
                            pe.wait_ge(s_ht, g * 2 + side)
                        elif not first:
                            pe.wait_ge(s_q, g - 1)
                        for k in range(G):
                            ins = nc.tensor.transpose(turned_rows[:, k * D:(k + 1) * D], h[:, side * G + k, :], m.ident[:, :])
                        ins.then_inc(s_turned, 1)
                    if not (first and slot == 0):
                        multiply(1 - slot, g, first, g * 2 + 2)

            def multiply(slot, count, first, turned_sides):
                pe.wait_ge(s_ht, turned_sides)
                for k in range(G):
                    ins = nc.tensor.matmul(tile(turned, k, D + H), ht[slot][:, 1, k * D:(k + 1) * D], m.w_query[:, :], start=True, stop=True)
                ins.then_inc(s_queries, 1)
                if not first:
                    pe.wait_ge(s_used, count - 1)
                    pe.wait_ge(s_val, count - 1)
                for k in range(G):
                    of_src = ht[slot][:, 0, k * D:(k + 1) * D]
                    nc.tensor.matmul(value[:, k, :], of_src, m.w_value[:, :], start=True, stop=True)
                    ins = nc.tensor.matmul(tile(key, k, D + 2 * H), of_src, m.w_key[:, :], start=True, stop=True)
                ins.then_inc(s_keys, 1)
            turns(pe, body)
            pe.wait_ge(s_q, NG - 1)
            multiply(1, NG, False, NG * 2)


def softmax(nc, m, ctx, block, o, score, heads, scale, name):
    def sb(nm, shape, dt=F32):
        return ctx.enter_context(nc.sbuf_tensor(name + nm, shape, dt))

    top, top_back = sb("top", [P, T, heads]), sb("top_back", [P, T, heads])
    cut, cut_back = sb("cut", [P, T]), sb("cut_back", [P, T])
    cut_first, cut_last = sb("cut_first", [P, T]), sb("cut_last", [P, T])
    cut_chunks = [sb(f"cut_chunks{i}", [P, 1, P]) for i in (0, 1)]
    ends = sb("ends", [P, heads, P])
    all_ends = [ctx.enter_context(nc.psum_tensor(f"{name}all_ends{i}", [P, max(heads, 4), P], F32)) for i in (0, 1)]
    masked = sb("masked", [P, heads, P])
    reach = [sb(f"reach{i}", [P, heads]) for i in (0, 1)]
    s_step, s_ends, s_all, s_shifted, s_exp = (m.sem(name + n) for n in ("step", "ends", "all_ends", "shifted", "exp"))

    @block.vector
    def _(dve):
        v = nc.vector
        steps = Steps(dve, s_step)
        for out, mark in ((cut[:, :], m.same[o][:, 0:T]), (cut_back[:, :], m.same[o][:, 1:T + 1]), (cut_first[:, :], m.first[o][:, :, 0]),
                          (cut_last[:, :], m.last[o][:, :, 0]), (cut_chunks[0][:, 0, :], m.after[o][:, :]),
                          (cut_chunks[1][:, 0, :], m.before[o][:, :])):
            steps.inc(v.tensor_scalar(out, mark, -1.0, BIG, ALU.add, ALU.mult))
        steps.wait()
        for h in range(heads):
            steps.inc(v.tensor_tensor_scan(top[:, :, h], cut[:, :], score[:, :, h], -BIG, ALU.add, ALU.max))
        steps.wait()
        for h in range(heads):
            steps.inc(v.tensor_tensor_scan(top_back[:, ::-1, h], cut_back[:, ::-1], top[:, ::-1, h], -BIG, ALU.add, ALU.max))
        steps.wait()
        for side, t in ((0, T - 1), (1, 0)):
            v.tensor_copy(ends[:, :, :], top_back[:, t, :].unsqueeze(2).to_broadcast([P, heads, P])).then_inc(s_ends, 1)
            dve.wait_ge(s_all, side + 1)
            steps.link(v.tensor_tensor(masked[:, :, :], all_ends[side][:, 0:heads, :],
                                       cut_chunks[side][:, :, :].to_broadcast([P, heads, P]), ALU.add))
            steps.link(v.tensor_reduce(reach[side][:, :], masked[:, :, :], AX.X, ALU.max))
        for side, marks in ((0, cut_first), (1, cut_last)):
            for h in range(heads):
                steps.inc(v.scalar_tensor_tensor(top_back[:, :, h], marks[:, :], reach[side][:, h:h + 1], top_back[:, :, h],
                                                 ALU.add, ALU.max))
            steps.wait()
        v.tensor_tensor(score[:, :, :], score[:, :, :], top_back[:, :, :], ALU.subtract).then_inc(s_shifted, 1)

    @block.tensor
    def _(pe):
        for side in (0, 1):
            pe.wait_ge(s_ends, side + 1)
            for h in range(heads):
                ins = nc.tensor.transpose(all_ends[side][:, h, :], ends[:, h, :], m.ident[:, :])
            ins.then_inc(s_all, 1)

    @block.scalar
    def _(act):
        act.wait_ge(s_shifted, 1)
        nc.scalar.activation(score[:, :, :], score[:, :, :], ACT.Exp, scale=scale).then_inc(s_exp, 1)
    return s_exp


def weigh(nc, m, ctx, block, o, score, s_score, heads, total, name, with_dinv=False):
    def sb(nm, shape, dt=F32):
        return ctx.enter_context(nc.sbuf_tensor(name + nm, shape, dt))

    width = D // heads
    part = [sb(f"part{i}", [P, G, D]) for i in (0, 1)]
    carry_ps = ctx.enter_context(nc.psum_tensor(name + "carry", [P, 512], F32))
    total_ps = ctx.enter_context(nc.psum_tensor(name + "total", [P, 512], F32))
    s_step, s_sum, s_kept, s_carry = (m.sem(name + n) for n in ("step", "summed", "kept", "carry"))
    same_g = [sb(f"same{i}", [P, G]) for i in (0, 1)]
    if with_dinv:
        slots = value_slots(m, ctx, "dinv1_")
        zeros = sb("zeros", [P, ZERO_ROWS * D])
        s_zero, s_zeroed = m.sem("h2_zeros_made"), m.sem("h2_table_zeroed")

    @block.sync
    def _(sp):
        if with_dinv:
            sp.wait_ge(s_zero, 1)
            zero_h2_table(sp, m, zeros, 1, s_sum, s_zeroed)

    @block.gpsimd
    def _(pool):
        if with_dinv:
            nc.gpsimd.memset(zeros[:, :], 0.0).then_inc(s_zero, 1)
            get_dinv(nc, m, pool, slots)

    @block.vector
    def _(dve):
        v = nc.vector
        steps = Steps(dve, s_step)
        dve.wait_ge(s_score, 1)
        for h in range(heads):
            steps.inc(v.tensor_tensor_scan(total[:, :, h], m.same[o][:, 0:T], score[:, :, h], 0.0, ALU.mult, ALU.add))
        steps.wait()

        def body(i, first):
            for slot in (0, 1):
                g = i * 2 + slot
                if not first:
                    dve.wait_ge(s_kept, g - 1)
                steps.inc(v.tensor_copy(same_g[slot][:, :], m.same[o][:, group(i, slot)]))
                weighed = (part[slot][:, :, :], m.rows[:, group(i, slot), :], score[:, group(i, slot), :])
                if heads > 1:
                    out, row = (a.rearrange("p g (h c) -> p (g h) c", c=width) for a in weighed[0:2])
                    s = weighed[2].rearrange("p g h -> p (g h)").unsqueeze(2).to_broadcast([P, G * heads, width])
                else:
                    out, row, s = weighed[0], weighed[1], weighed[2].to_broadcast([P, G, D])
                steps.link(v.tensor_tensor(out, row, s, ALU.mult))
                for k in range(G):
                    if first and slot == 0 and k == 0:
                        continue
                    before = part[slot][:, k - 1, :] if k else part[1 - slot][:, G - 1, :]
                    ins = v.scalar_tensor_tensor(part[slot][:, k, :], before, same_g[slot][:, k:k + 1], part[slot][:, k, :],
                                                 ALU.mult, ALU.add)
                    if k < G - 1:
                        steps.link(ins)
                    else:
                        ins.then_inc(s_sum, 1)
                        dve.wait_ge(s_sum, g + 1)
        turns(dve, body, steps, 2 * (G + 1))
        dve.wait_ge(s_carry, 1)
        steps.inc(v.tensor_copy(m.carry[:, 0, :], carry_ps[:, 0:D]))
        for h in range(heads):
            steps.inc(v.scalar_tensor_tensor(total[:, :, h], m.first[o][:, :, 0], total_ps[:, h:h + 1], total[:, :, h],
                                             ALU.mult, ALU.add))
        steps.wait()
        steps.link(v.tensor_scalar(total[:, :, :], total[:, :, :], 1e-30, None, ALU.max))
        steps.link(v.reciprocal(total[:, :, :], total[:, :, :]))

    @block.scalar
    def _(act):
        def body(i, first):
            for slot in (0, 1):
                g = i * 2 + slot
                act.wait_ge(s_sum, g + 1)
                nc.scalar.activation(m.rows[:, group(i, slot), :], part[slot][:, :, :], ACT.Copy).then_inc(s_kept, 1)
        turns(act, body)

    @block.tensor
    def _(pe):
        pe.wait_ge(s_kept, NG)
        nc.tensor.matmul(carry_ps[:, 0:D], m.before[o][:, :], m.rows[:, T - 1, :], start=True, stop=True)
        nc.tensor.matmul(total_ps[:, 0:heads], m.before[o][:, :], total[:, T - 1, :], start=True, stop=True).then_inc(s_carry, 1)


def finish(nc, m, o, total, heads, rectify, base_rows, table, name):
    with ExitStack() as ctx:
        def sb(nm, shape, dt=F32):
            return ctx.enter_context(nc.sbuf_tensor(name + nm, shape, dt))

        numbers = [sb(f"numbers{i}", [P, G], I32) for i in (0, 1)]
        base = [sb(f"base{i}", [P, G, D]) for i in (0, 1)]
        row = [sb(f"row{i}", [P, G, D]) for i in (0, 1)]
        tmp = sb("tmp", [P, G, D])
        s_num, s_step, s_row = (m.sem(name + n) for n in ("numbers_staged", "step", "rows_made"))
        s_base = [m.sem(f"{name}base_in{i}") for i in (0, 1)]
        s_scat = [m.lasting_sem(f"{name}scattered{i}") for i in (0, 1)]
        block = ctx.enter_context(nc.Block())

        @block.sync
        def _(sp):
            def body(i, first):
                for slot in (0, 1):
                    g = i * 2 + slot
                    if not first:
                        sp.wait_ge(s_row, g - 1)
                    sp.dma_start(base[slot][:, :, :], chunk(base_rows, i, slot)).then_inc(s_base[slot], 16)
            turns(sp, body)

        @block.gpsimd
        def _(pool):
            def body(i, first):
                for slot in (0, 1):
                    g = i * 2 + slot
                    if not first:
                        hold(pool, m.passed, s_scat[slot], i * (16 * G))
                    stage_columns(pool, nc, m, numbers, m.tail_idx[o], i, slot, s_num, g + 1)
                    hold(pool, m.passed, s_row, g + 1)
                    scatter(pool, table, row[slot], numbers[slot], s_scat[slot])
            turns(pool, body)
            for slot in (0, 1):
                pool.wait_ge(s_scat[slot], 16 * G * PAIRS)

        @block.vector
        def _(dve):
            v = nc.vector
            steps = Steps(dve, s_step)
            width = D // heads

            def body(i, first):
                for slot in (0, 1):
                    g = i * 2 + slot
                    steps.link(v.tensor_tensor(tmp[:, :, :], m.carry[:, :, :].to_broadcast([P, G, D]),
                                               m.first[o][:, group(i, slot), :].to_broadcast([P, G, D]), ALU.mult))
                    steps.link(v.tensor_tensor(tmp[:, :, :], tmp[:, :, :], m.rows[:, group(i, slot), :], ALU.add))
                    if heads > 1:
                        split = tmp[:, :, :].rearrange("p g (h c) -> p (g h) c", c=width)
                        per_head = total[:, group(i, slot), :].rearrange("p g h -> p (g h)").unsqueeze(2).to_broadcast([P, G * heads, width])
                    else:
                        split, per_head = tmp[:, :, :], total[:, group(i, slot), :].to_broadcast([P, G, D])
                    steps.link(v.tensor_tensor(split, split, per_head, ALU.mult))
                    if rectify:
                        steps.link(v.tensor_tensor(tmp[:, :, :], tmp[:, :, :], m.bv[:, :, :].to_broadcast([P, G, D]), ALU.add))
                    dve.wait_ge(s_base[slot], i * 16 + 16)
                    if not first:
                        dve.wait_ge(s_scat[slot], i * (16 * G))
                    if rectify:
                        steps.link(v.scalar_tensor_tensor(tmp[:, :, :], tmp[:, :, :], 0.0, base[slot][:, :, :], ALU.max, ALU.add))
                        ins = v.tensor_tensor(row[slot][:, :, :], tmp[:, :, :], m.rb2[:, :, :].to_broadcast([P, G, D]), ALU.add)
                    else:
                        ins = v.tensor_tensor(row[slot][:, :, :], tmp[:, :, :], base[slot][:, :, :], ALU.add)
                    ins.then_inc(s_row, 1)
                    dve.wait_ge(s_row, g + 1)
            turns(dve, body, steps, 2 * (5 if rectify else 3))


def sum_neighbour_rows(nc, m, out):
    with ExitStack() as ctx:
        def sb(nm, shape, dt=F32):
            return ctx.enter_context(nc.sbuf_tensor("l2_" + nm, shape, dt))

        def two(nm, shape, dt=F32):
            return [sb(f"{nm}{i}", shape, dt) for i in (0, 1)]

        def sem(nm):
            return m.sem("l2_" + nm)

        o = BY_SRC
        slots = range(DEEP)
        dst_numbers, yd = ([sb(f"{n}{i}", shape, dt) for i in slots] for n, shape, dt in (("dst_numbers", [P, G], I32), ("yd", [P, G, D], F32)))
        x2, h = two("x2", [P, G, D]), two("h", [P, G, D])
        same_g, mv, rstd, shift = two("same", [P, G]), two("mv", [P, G, 2]), two("rstd", [P, G, 1]), two("shift", [P, G, 1])
        stats, work = sb("stats", [P, G, 6]), sb("work", [P, 2, G])
        s_dst, s_step, s_x2, s_norm, s_h, s_sum, s_kept = (
            sem(n) for n in ("dst_staged", "step", "x2_made", "norm", "h_made", "summed", "kept"))
        s_yd = [m.lasting_sem(f"l2_yd_in{i}") for i in slots]
        s_stored = [sem(f"yd_stored{i}") for i in slots]
        block = ctx.enter_context(nc.Block())

        @block.gpsimd
        def _(pool):
            def body(i, first):
                for slot in slots:
                    g = i * DEEP + slot
                    if not first:
                        hold(pool, m.passed, s_x2, g - 3)
                        hold(pool, m.passed, s_stored[slot], i * 16)
                    stage_group(pool, nc, m, dst_numbers[slot], m.dst_idx[o], g, s_dst)
                    gather(pool, yd[slot], out, dst_numbers[slot], s_yd[slot])
            turns(pool, body, count=FOURS)

        @block.sync
        def _(sp):
            with sp.Fori(0, FOURS) as i:
                for slot in slots:
                    sp.wait_ge(s_yd[slot], i * (16 * G) + 16 * G)
                    sp.dma_start(m.y_dst[:, group_of(i * DEEP + slot), :], yd[slot][:, :, :]).then_inc(s_stored[slot], 16)
            for slot in slots:
                sp.wait_ge(s_stored[slot], 16 * FOURS)

        @block.scalar
        def _(act):
            def body(i, first):
                for slot in slots:
                    g = i * DEEP + slot
                    act.wait_ge(s_norm, g + 1)
                    if not (first and slot == 0):
                        act.wait_ge(s_sum, g)
                    if not (first and slot < 2):
                        act.wait_ge(s_kept, g - 1)
                    for k in range(G):
                        ins = nc.scalar.activation(h[slot % 2][:, k, :], x2[slot % 2][:, k, :], ACT.Relu,
                                                   bias=shift[slot % 2][:, k, :], scale=rstd[slot % 2][:, k, :])
                    ins.then_inc(s_h, 1)
                    if not (first and slot == 0):
                        keep(g - 1, (slot - 1) % DEEP)

            def keep(g, slot):
                act.wait_ge(s_sum, g + 1)
                nc.scalar.activation(m.rows[:, group_of(g), :], h[slot % 2][:, :, :], ACT.Copy).then_inc(s_kept, 1)
            turns(act, body, count=FOURS)
            keep(NG - 1, DEEP - 1)

        @block.vector
        def _(dve):
            v = nc.vector
            steps = Steps(dve, s_step)

            def normalise(i, slot):
                g = i * DEEP + slot
                dve.wait_ge(s_yd[slot], i * (16 * G) + 16 * G)
                v.tensor_tensor(x2[slot % 2][:, :, :], yd[slot][:, :, :], m.rb2[:, :, :].to_broadcast([P, G, D]),
                                ALU.subtract).then_inc(s_x2, 1)
                dve.wait_ge(s_x2, g + 1)
                steps.link(row_stats(v, m, steps, x2[slot % 2], G, stats, mv[slot % 2]))
                steps.inc(v.tensor_copy(same_g[slot % 2][:, :], m.same[o][:, group_of(i * DEEP + slot)]))
                steps.link(norm_rows(v, steps, mv[slot % 2], work, rstd[slot % 2][:, :, 0], shift[slot % 2][:, :, 0]))
                steps.inc(v.tensor_tensor(rstd[slot % 2][:, :, :], rstd[slot % 2][:, :, :], m.dinv_dst[:, group_of(i * DEEP + slot), :], ALU.mult))
                v.tensor_tensor(shift[slot % 2][:, :, :], shift[slot % 2][:, :, :], m.dinv_dst[:, group_of(i * DEEP + slot), :],
                                ALU.mult).then_inc(s_norm, 1)
                steps.wait()

            def sums(g, slot):
                dve.wait_ge(s_h, g + 1)
                for k in range(G):
                    if k == 0 and is_first(g):
                        continue
                    before = h[slot % 2][:, k - 1, :] if k else h[1 - slot % 2][:, G - 1, :]
                    ins = v.scalar_tensor_tensor(h[slot % 2][:, k, :], before, same_g[slot % 2][:, k:k + 1], h[slot % 2][:, k, :],
                                                 ALU.mult, ALU.add)
                    if k < G - 1:
                        steps.link(ins)
                    else:
                        ins.then_inc(s_sum, 1)
                        dve.wait_ge(s_sum, g + 1)

            def body(i, first):
                for slot in slots:
                    normalise(i, slot)
                    if not (first and slot == 0):
                        sums(i * DEEP + (slot - 1), (slot - 1) % DEEP)
            turns(dve, body, steps, DEEP * (3 * G + 15), count=FOURS)
            sums(NG - 1, DEEP - 1)


def transform_sums2(nc, m, out):
    with ExitStack() as ctx:
        def sb(nm, shape, dt=F32):
            return ctx.enter_context(nc.sbuf_tensor("t2_" + nm, shape, dt))

        def two(nm, shape, dt=F32):
            return [sb(f"{nm}{i}", shape, dt) for i in (0, 1)]

        def psum(nm, cols):
            return ctx.enter_context(nc.psum_tensor("t2_" + nm, [P, cols], F32))

        def sem(nm):
            return m.sem("t2_" + nm)

        o = BY_SRC
        numbers, src_numbers = two("numbers", [P, G], I32), two("src_numbers", [P, G], I32)
        u, d, uts, ys, h = two("u", [P, G, D]), two("d", [P, G, D]), two("uts", [P, G * D]), two("ys", [P, G, D]), two("h", [P, G, D])
        mv, rstd, shift = two("mv", [P, G, 2]), two("rstd", [P, G, 1]), two("shift", [P, G, 1])
        tmp, fix, dot, stats, work = sb("tmp", [P, G, D]), sb("fix", [P, G, D]), sb("dot", [P, G, D]), sb("stats", [P, G, 6]), sb("work", [P, 2, G])
        ut, z, carry_ps, end_ps = [psum(f"ut{i}", 8 * D) for i in (0, 1)], psum("z", 8 * D), psum("carry", 512), psum("end", 512)
        s_num, s_step, s_carry, s_u, s_turned, s_uts, s_z, s_d, s_x3, s_norm, s_h, s_spread, s_end, s_src = (
            sem(n) for n in ("numbers_staged", "step", "carry_made", "u_made", "u_turned", "uts_made", "z_made", "d_made",
                             "x3_made", "norm", "h_made", "scores_spread", "scores_carried", "src_staged"))
        s_scat = [m.lasting_sem(f"t2_scattered{i}") for i in (0, 1)]
        s_ys = [m.lasting_sem(f"t2_ys_in{i}") for i in (0, 1)]
        s_stored = [sem(f"x3_stored{i}") for i in (0, 1)]
        block = ctx.enter_context(nc.Block())

        @block.gpsimd
        def _(pool):
            def body(i, first):
                for slot in (0, 1):
                    g = i * 2 + slot
                    if not first:
                        hold(pool, m.passed, s_stored[slot], i * 16)
                        hold(pool, m.passed, s_h, g - 1)
                    stage_columns(pool, nc, m, src_numbers, m.src_idx[o], i, slot, s_src, g + 1)
                    gather(pool, ys[slot], out, src_numbers[slot], s_ys[slot])
                    if not (first and slot == 0):
                        put(i - (1 - slot), 1 - slot, g)

            def put(i, slot, count):
                if not is_first(i):
                    hold(pool, m.passed, s_scat[slot], i * (16 * G))
                stage_columns(pool, nc, m, numbers, m.tail_idx[o], i, slot, s_num, count)
                hold(pool, m.passed, s_d, count)
                scatter(pool, m.h2_table, d[slot], numbers[slot], s_scat[slot])
            turns(pool, body, peeled=2)
            put(PAIRS - 1, 1, NG)
            for slot in (0, 1):
                pool.wait_ge(s_scat[slot], 16 * G * PAIRS)

        @block.sync
        def _(sp):
            with sp.Fori(0, PAIRS) as i:
                for slot in (0, 1):
                    hold(sp, m.passed, s_x3, i * 2 + (slot + 1))
                    sp.dma_start(chunk(m.x3_src, i, slot), ys[slot][:, :, :]).then_inc(s_stored[slot], 16)
            for slot in (0, 1):
                sp.wait_ge(s_stored[slot], 16 * PAIRS)

        @block.tensor
        def _(pe):
            nc.tensor.matmul(carry_ps[:, 0:D], m.before[o][:, :], m.rows[:, T - 1, :], start=True, stop=True).then_inc(s_carry, 1)

            def body(i, first):
                for slot in (0, 1):
                    g = i * 2 + slot
                    pe.wait_ge(s_u, g + 1)
                    for k in range(G):
                        ins = nc.tensor.transpose(ut[slot][:, k * D:(k + 1) * D], u[slot][:, k, :], m.ident[:, :])
                    ins.then_inc(s_turned, 1)
                    pe.wait_ge(s_uts, g + 1)
                    if not (first and slot == 0):
                        pe.wait_ge(s_d, g)
                    for k in range(G):
                        ins = nc.tensor.matmul(z[:, k * D:(k + 1) * D], uts[slot][:, k * D:(k + 1) * D], m.w2[:, :],
                                               start=True, stop=True)
                    ins.then_inc(s_z, 1)
            turns(pe, body)
            pe.wait_ge(s_spread, 1)
            nc.tensor.matmul(end_ps[:, 0:1], m.after[o][:, :], m.to_self[:, 0, :], start=True, stop=True).then_inc(s_end, 1)

        @block.scalar
        def _(act):
            def body(i, first):
                for slot in (0, 1):
                    g = i * 2 + slot
                    act.wait_ge(s_turned, g + 1)
                    nc.scalar.activation(uts[slot][:, :], ut[slot][:, 0:G * D], ACT.Copy).then_inc(s_uts, 1)
                    if not (first and slot == 0):
                        normalise(1 - slot, g)

            def normalise(slot, count):
                act.wait_ge(s_norm, count)
                for k in range(G):
                    ins = nc.scalar.activation(h[slot][:, k, :], ys[slot][:, k, :], ACT.Relu,
                                               bias=shift[slot][:, k, :], scale=rstd[slot][:, k, :])
                ins.then_inc(s_h, 1)
            turns(act, body)
            normalise(1, NG)

        @block.vector
        def _(dve):
            v = nc.vector
            steps = Steps(dve, s_step)
            dve.wait_ge(s_carry, 1)
            steps.link(v.tensor_copy(m.carry[:, 0, :], carry_ps[:, 0:D]))

            def sums(i, slot):
                steps.link(v.tensor_tensor(fix[:, :, :], m.carry[:, :, :].to_broadcast([P, G, D]),
                                           m.first[o][:, group(i, slot), :].to_broadcast([P, G, D]), ALU.mult))
                v.tensor_tensor(u[slot][:, :, :], fix[:, :, :], m.rows[:, group(i, slot), :], ALU.add).then_inc(s_u, 1)
                dve.wait_ge(s_u, i * 2 + (slot + 1))

            def rows(i, slot, count):
                dve.wait_ge(s_z, count)
                z3 = z[:, 0:G * D].rearrange("p (g d) -> p g d", d=D)
                steps.link(v.tensor_tensor(tmp[:, :, :], z3, m.dinv_src[:, group(i, slot), :].to_broadcast([P, G, D]), ALU.mult))
                steps.link(v.tensor_tensor(tmp[:, :, :], tmp[:, :, :], m.b2[:, :, :].to_broadcast([P, G, D]), ALU.add))
                if not is_first(i):
                    dve.wait_ge(s_scat[slot], i * (16 * G))
                v.scalar_tensor_tensor(d[slot][:, :, :], tmp[:, :, :], 0.0, m.rb2[:, :, :].to_broadcast([P, G, D]),
                                       ALU.max, ALU.subtract).then_inc(s_d, 1)
                dve.wait_ge(s_d, count)
                dve.wait_ge(s_ys[slot], i * (16 * G) + 16 * G)
                v.tensor_tensor(ys[slot][:, :, :], ys[slot][:, :, :], d[slot][:, :, :], ALU.add).then_inc(s_x3, 1)
                dve.wait_ge(s_x3, count)
                steps.link(row_stats(v, m, steps, ys[slot], G, stats, mv[slot]))
                norm_rows(v, steps, mv[slot], work, rstd[slot][:, :, 0], shift[slot][:, :, 0]).then_inc(s_norm, 1)

            def part_of_score(i, slot, count):
                dve.wait_ge(s_h, count)
                steps.link(v.tensor_tensor(dot[:, :, :], h[slot][:, :, :], m.to_src[:, :, :].to_broadcast([P, G, D]), ALU.mult))
                steps.link(v.tensor_reduce(m.to_self[:, group(i, slot), 0], dot[:, :, :], AX.X, ALU.add))

            def body(i, first):
                for slot in (0, 1):
                    g = i * 2 + slot
                    sums(i, slot)
                    if not first:
                        part_of_score(i - 1, slot, g - 1)
                    if not (first and slot == 0):
                        rows(i - (1 - slot), 1 - slot, g)
            turns(dve, body, steps, 2 * (1 + 2 + 2 + 2 * G + 13), peeled=2)
            part_of_score(PAIRS - 1, 0, NG - 1)
            rows(PAIRS - 1, 1, NG)
            part_of_score(PAIRS - 1, 1, NG)
            steps.link(v.tensor_tensor(m.to_self[:, :, 0], m.to_self[:, :, 0], m.tail[o][:, :, 0], ALU.mult))
            steps.link(v.tensor_tensor_scan(m.score3[:, ::-1, 0], m.same[o][:, T:0:-1], m.to_self[:, ::-1, 0], 0.0, ALU.mult, ALU.add))
            v.tensor_copy(m.to_self[:, :, 0], m.score3[:, :, 0]).then_inc(s_spread, 1)
            dve.wait_ge(s_end, 1)
            steps.link(v.scalar_tensor_tensor(m.to_self[:, :, 0], m.last[o][:, :, 0], end_ps[:, 0:1], m.score3[:, :, 0],
                                              ALU.mult, ALU.add))


def kan(nc, m):
    with ExitStack() as ctx:
        def sb(nm, shape, dt=F32):
            return ctx.enter_context(nc.sbuf_tensor("kan_" + nm, shape, dt))

        def two(nm, shape, dt=F32):
            return [sb(f"{nm}{i}", shape, dt) for i in (0, 1)]

        def sem(nm):
            return m.sem("kan_" + nm)

        o = BY_SRC
        parts = KNOTS + 1
        knot = [(n + 0.5) * GRID_STEP for n in range(KNOTS)]
        numbers = two("numbers", [P, G], I32)
        hd, yd, h, ht = two("hd", [P, G, D]), two("yd", [P, G, D]), two("h", [P, G, D]), two("ht", [P, G * D])
        mv, rstd, shift = two("mv", [P, G, 2]), two("rstd", [P, G, 1]), two("shift", [P, G, 1])
        stats, work, knots = sb("stats", [P, G, 6]), sb("work", [P, 2, G]), sb("knots", [P, KNOTS])
        silu = sb("silu", [P, G * D])
        near_dve, near_act = [sb(f"near_dve{n}", [P, G * D]) for n in range(DVE_KNOTS)], two("near_act", [P, G * D])
        cube = [sb(f"cube{i}", [P, G * D]) for i in range(KNOTS)]
        zero_row = sb("zero_row", [1, 512], mybir.dt.bfloat16)
        turned = ctx.enter_context(nc.psum_tensor("kan_turned", [P, 8 * D], F32))
        val = [ctx.enter_context(nc.psum_tensor(f"kan_val{i}", [P, 8, D], F32)) for i in (0, 1)]
        dots = ctx.enter_context(nc.psum_tensor("kan_dots", [P, 512], F32))
        s_num, s_step, s_x3, s_norm, s_h, s_turned, s_ht, s_tanh, s_silu, s_near, s_square, s_cube, s_dots, s_taken, s_mult, s_kept, s_made = (
            sem(n) for n in ("numbers_staged", "step", "x3_made", "norm", "h_made", "h_turned", "ht_made", "tanh_made", "silu_made",
                             "near_made", "squared", "cubed", "dots_made", "dots_taken", "multiplied", "values_kept", "constants_made"))
        s_hd = [m.lasting_sem(f"kan_hd_in{i}") for i in (0, 1)]
        s_yd = [sem(f"yd_in{i}") for i in (0, 1)]
        s_near_dve = sem("near_dve_made")
        block = ctx.enter_context(nc.Block())

        @block.gpsimd
        def _(pool):
            nc.gpsimd.memset(zero_row[:, :], 0.0).then_inc(s_made, 1)
            for n in range(KNOTS):
                nc.gpsimd.memset(knots[:, n:n + 1], knot[n]).then_inc(s_made, 1)

            def body(i, first):
                for slot in (0, 1):
                    g = i * 2 + slot
                    if not first:
                        hold(pool, m.passed, s_x3, g - 1)
                    stage_columns(pool, nc, m, numbers, m.dst_idx[o], i, slot, s_num, g + 1)
                    gather(pool, hd[slot], m.h2_table, numbers[slot], s_hd[slot])
            turns(pool, body)

        @block.sync
        def _(sp):
            def body(i, first):
                for slot in (0, 1):
                    g = i * 2 + slot
                    if not first:
                        sp.wait_ge(s_h, g - 1)
                    sp.dma_start(yd[slot][:, :, :], chunk(m.y_dst, i, slot)).then_inc(s_yd[slot], 16)
            turns(sp, body)

        @block.vector
        def _(dve):
            v = nc.vector
            steps = Steps(dve, s_step)

            def normalise(i, slot, first):
                g = i * 2 + slot
                dve.wait_ge(s_hd[slot], i * (16 * G) + 16 * G)
                dve.wait_ge(s_yd[slot], i * 16 + 16)
                v.tensor_tensor(yd[slot][:, :, :], yd[slot][:, :, :], hd[slot][:, :, :], ALU.add).then_inc(s_x3, 1)
                dve.wait_ge(s_x3, g + 1)
                steps.link(row_stats(v, m, steps, yd[slot], G, stats, mv[slot]))
                norm_rows(v, steps, mv[slot], work, rstd[slot][:, :, 0], shift[slot][:, :, 0]).then_inc(s_norm, 1)

            def features(i, slot, g, first):
                dve.wait_ge(s_ht, g + 1)

                def near(n):
                    v.tensor_scalar(near_dve[n][:, :], ht[slot][:, :], knot[n], knot[n], ALU.min, ALU.subtract).then_inc(s_near_dve, 1)

                for n in range(DVE_KNOTS):
                    near(n)
                dve.wait_ge(s_tanh, g + 1)
                v.scalar_tensor_tensor(silu[:, :], silu[:, :], 1.0, ht[slot][:, :], ALU.add, ALU.mult).then_inc(s_silu, 1)
                for n in range(KNOTS):
                    dve.wait_ge(s_square, g * KNOTS + (n + 1))
                    source = near_dve[n] if n < DVE_KNOTS else near_act[n % 2]
                    v.tensor_tensor(cube[n][:, :], cube[n][:, :], source[:, :], ALU.mult).then_inc(s_cube, 1)
                dve.wait_ge(s_dots, g + 1)
                v.tensor_copy(m.score3[:, group(i, slot), 0], dots[:, 0:G]).then_inc(s_taken, 1)

            def body(i, first):
                for slot in (0, 1):
                    normalise(i, slot, first)
                    if not first:
                        features(i - 1, slot, i * 2 + (slot - 2), False)
            turns(dve, body, steps, 2 * (2 * G + 13))
            for slot in (0, 1):
                features(PAIRS - 1, slot, NG - 2 + slot, False)

        @block.scalar
        def _(act):
            act.wait_ge(s_made, KNOTS + 1)

            def normalise(i, slot, first):
                g = i * 2 + slot
                act.wait_ge(s_norm, g + 1)
                if not first:
                    act.wait_ge(s_turned, g - 1)
                for k in range(G):
                    ins = nc.scalar.activation(h[slot][:, k, :], yd[slot][:, k, :], ACT.Relu,
                                               bias=shift[slot][:, k, :], scale=rstd[slot][:, k, :])
                ins.then_inc(s_h, 1)

            def features(i, slot, g, first):
                act.wait_ge(s_turned, g + 1)
                nc.scalar.activation(ht[slot][:, :], turned[:, 0:G * D], ACT.Copy).then_inc(s_ht, 1)
                act.wait_ge(s_ht, g + 1)
                if not first:
                    act.wait_ge(s_mult, g * parts - (parts - 1))
                nc.scalar.activation(silu[:, :], ht[slot][:, :], ACT.Tanh, scale=0.5).then_inc(s_tanh, 1)

                def near(n):
                    a = n - DVE_KNOTS
                    if a >= 2:
                        act.wait_ge(s_cube, g * KNOTS + (n - 1))
                    elif not first:
                        act.wait_ge(s_cube, g * KNOTS)
                    nc.scalar.activation(near_act[n % 2][:, :], ht[slot][:, :], ACT.Relu, bias=knots[:, n:n + 1], scale=-1.0).then_inc(s_near, 1)

                def square(n):
                    if n < DVE_KNOTS:
                        act.wait_ge(s_near_dve, g * DVE_KNOTS + (n + 1))
                        source = near_dve[n]
                    else:
                        act.wait_ge(s_near, g * (KNOTS - DVE_KNOTS) + (n - DVE_KNOTS + 1))
                        source = near_act[n % 2]
                    if not first:
                        act.wait_ge(s_mult, g * parts - (parts - 2 - n))
                    nc.scalar.activation(cube[n][:, :], source[:, :], ACT.Square).then_inc(s_square, 1)

                for n in range(KNOTS):
                    if DVE_KNOTS <= n + 1 < KNOTS and n + 1 - DVE_KNOTS < 2:
                        near(n + 1)
                    elif n - DVE_KNOTS >= 2:
                        near(n)
                    square(n)

            def keep(i, slot, groups):
                act.wait_ge(s_mult, groups * parts)
                nc.scalar.activation(m.rows[:, group(i, slot), :], val[slot][:, 0:G, :], ACT.Copy).then_inc(s_kept, 1)

            def body(i, first):
                for slot in (0, 1):
                    normalise(i, slot, first)
                    if not (first and slot == 0):
                        features(i - (1 - slot), 1 - slot, i * 2 + (slot - 1), first and slot == 1)
                    if not first:
                        keep(i - 1, slot, i * 2 + (slot - 1))
            turns(act, body)
            features(PAIRS - 1, 1, NG - 1, False)
            keep(PAIRS - 1, 0, NG - 1)
            keep(PAIRS - 1, 1, NG)

        @block.tensor
        def _(pe):
            pe.wait_ge(s_made, 1)

            def turn(i, slot, first):
                g = i * 2 + slot
                pe.wait_ge(s_h, g + 1)
                if not (first and slot == 0):
                    pe.wait_ge(s_ht, g)
                for k in range(G):
                    ins = nc.tensor.transpose(turned[:, k * D:(k + 1) * D], h[slot][:, k, :], m.ident[:, :])
                ins.then_inc(s_turned, 1)

            def multiply(i, slot, g, first, second):
                if not first:
                    pe.wait_ge(s_taken, g)
                    if not second:
                        pe.wait_ge(s_kept, g - 1)
                pe.wait_ge(s_ht, g + 1)
                for k in range(G):
                    ins = nc.tensor.matmul(dots[:, k:k + 1], ht[slot][:, k * D:(k + 1) * D], m.to_dst[:, :], start=True, stop=True)
                ins.then_inc(s_dots, 1)
                for half in (0, 4):
                    nc.tensor.matmul(val[slot][:, half:half + 4, :], zero_row[:, 0:P], zero_row[:, :], start=True, stop=False)
                for n in range(parts):
                    if n:
                        pe.wait_ge(s_cube, g * KNOTS + n)
                    else:
                        pe.wait_ge(s_silu, g + 1)
                    part = cube[n - 1] if n else silu
                    for k in range(G):
                        ins = nc.tensor.matmul(val[slot][:, k, :], part[:, k * D:(k + 1) * D], m.w_kan[:, n, :], start=False, stop=False)
                    if n == parts - 1:
                        for half in (0, 4):
                            ins = nc.tensor.matmul(val[slot][:, half:half + 4, :], zero_row[:, 0:P], zero_row[:, :], start=False, stop=True)
                    ins.then_inc(s_mult, 1)

            turn(0, 0, True)
            turn(0, 1, False)
            multiply(0, 0, 0, True, False)
            turn(1, 0, False)
            multiply(0, 1, 1, False, True)
            turn(1, 1, False)
            multiply(1, 0, 2, False, False)
            with pe.Fori(2, PAIRS) as i:
                for slot in (0, 1):
                    turn(i, slot, False)
                    multiply(i - (1 - slot), 1 - slot, i * 2 + (slot - 1), False, False)
            multiply(PAIRS - 1, 1, NG - 1, False, False)


def score_edges3(nc, m, block):
    s_step = m.sem("leaky_step")

    @block.vector
    def _(dve):
        steps = Steps(dve, s_step)
        steps.link(nc.vector.tensor_tensor(m.score3[:, :, :], m.score3[:, :, :], m.to_self[:, :, :], ALU.add))
        steps.link(nc.vector.scalar_tensor_tensor(m.score3[:, :, :], m.score3[:, :, :], 0.2, m.score3[:, :, :], ALU.mult, ALU.max))


def build(nc, x, records, src, dst, w, out):
    with ExitStack() as ctx:
        m = Memory(nc, ctx)
        sort_edges(nc, m, src, dst)
        m.end_phase()
        with ExitStack() as phase, nc.Block() as block:
            index_edges(nc, m, records, phase, block)
            load_weights(nc, m, w, phase, block)
        m.end_phase()
        sum_source_rows(nc, m, x)
        m.end_phase()
        transform_sums0(nc, m, x)
        m.end_phase()
        batch_norm_rows(nc, m)
        m.end_phase()
        dense_pass(nc, m, x, out, records)
        m.end_phase()
        with nc.sbuf_tensor("scores", [P, T, H], F32) as scores, nc.sbuf_tensor("totals1", [P, T, H], F32) as totals:
            attend(nc, m, scores)
            m.end_phase()
            with ExitStack() as phase, nc.Block() as block:
                s_exp = softmax(nc, m, phase, block, BY_DST, scores, H, DK ** -0.5, "sm1_")
                weigh(nc, m, phase, block, BY_DST, scores, s_exp, H, totals, "w1_", with_dinv=True)
            m.end_phase()
            finish(nc, m, BY_DST, totals, H, True, m.x1_dst, out, "f1_")
            m.end_phase()
        sum_neighbour_rows(nc, m, out)
        m.end_phase()
        transform_sums2(nc, m, out)
        m.end_phase()
        kan(nc, m)
        m.end_phase()
        with ExitStack() as phase, nc.Block() as block:
            score_edges3(nc, m, block)
            s_exp = softmax(nc, m, phase, block, BY_SRC, m.score3, 1, 1.0, "sm3_")
            weigh(nc, m, phase, block, BY_SRC, m.score3, s_exp, 1, m.total3, "w3_")
        m.end_phase()
        finish(nc, m, BY_SRC, m.total3, 1, False, m.x3_src, out, "f3_")
        m.end_phase()


def kernel(**inputs):
    import numpy as np
    import concourse.bacc as bacc
    from concourse.bass_utils import run_bass_kernel_spmd as run

    def array(name):
        return np.ascontiguousarray(inputs[name])

    records = np.zeros((E, 4), np.int32)
    records[:, SRC], records[:, DST], records[:, WEIGHT] = array("src"), array("dst"), array("edge_weight").view(np.int32)
    arrays = {
        "x": array("x"), "records": records, "src": array("src"), "dst": array("dst"),
        "w0": array("L0_gnn_W").T, "b0": array("L0_gnn_b"), "gamma": array("L0_gnn_gamma"), "beta": array("L0_gnn_beta"),
        "wk": array("L1_gnn_Wk").T, "bk": array("L1_gnn_bk"), "wq": array("L1_gnn_Wq").T, "bq": array("L1_gnn_bq"),
        "wv": array("L1_gnn_Wv"), "bv": array("L1_gnn_bv"), "rel": array("L1_gnn_rel_att").reshape(D),
        "rel_msg": array("L1_gnn_rel_msg"),
        "wk_rows": array("L1_gnn_Wk"), "wq_rows": array("L1_gnn_Wq"), "w2": array("L2_gnn_kernel"), "b2": array("L2_gnn_bias"),
        "w3t": array("L3_gnn_W").T, "a": array("L3_gnn_a"), "base": array("L3_gnn_base_weight").T,
        "spline": array("L3_gnn_spline_weight").transpose(2, 1, 0),
    }
    arrays = {"in_" + name: np.ascontiguousarray(a) for name, a in arrays.items()}
    nc = bacc.Bacc("TRN2", target_bir_lowering=False, num_devices=1)
    aps = {name[3:]: nc.dram_tensor(name, a.shape, mybir.dt.from_np(a.dtype), kind="ExternalInput").ap()
           for name, a in arrays.items()}
    out = nc.dram_tensor("out_x", (N, D), F32, kind="ExternalOutput").ap()
    x, records, src, dst = (aps.pop(name) for name in ("x", "records", "src", "dst"))
    build(nc, x, records, src, dst, aps, out)
    return run(nc, [arrays], core_ids=[0]).results[0]["out_x"]
```
